# Optimizing a Trainium2 kernel written in Bass

```python
import numpy as np
import jax
import jax.numpy as jnp

def _softmax(x, axis=-1):
    return jax.nn.softmax(x, axis=axis)

def _gelu(x):
    return jax.nn.gelu(x, approximate=True)

def _silu(x):
    return jax.nn.silu(x)

def _sigmoid(x):
    return jax.nn.sigmoid(x)

def _layernorm(x, axis=-1, eps=1e-05):
    m = jnp.mean(x, axis=axis, keepdims=True)
    v = jnp.var(x, axis=axis, keepdims=True)
    return (x - m) / jnp.sqrt(v + eps)

def _scatter_add(tgt, idx, src, axis=0):
    return tgt.at[idx].add(src)

def _segment_sum(src, seg, n):
    return jax.ops.segment_sum(src, seg, n)
kernel_name = 'mk_gnn_ffn_d1_gnn_r32_b03417'

def setup_inputs(seed: int=0):
    np.random.seed(seed)
    _w = jnp.asarray

    def _rec_inputs():
        import jax
        import jax.numpy as jnp
        _gk = jax.random.key(seed)
        x = -0.000364 + 1 * jax.random.normal(jax.random.fold_in(_gk, 1), (625, 768), jnp.float32)
        src = jax.random.randint(jax.random.fold_in(_gk, 2), (20000,), 0, 625, jnp.int32)
        dst = jnp.minimum((625 * jax.random.uniform(jax.random.fold_in(_gk, 3), (20000,)) ** 2.0).astype(jnp.int32), 19999)
        _o = jnp.argsort(dst, stable=True)
        src = src[_o]
        dst = dst[_o]
        return (x, src, dst)
    x, src, dst = _rec_inputs()

    def _L0_gnn_setup():
        import jax, jax.numpy as jnp
        import numpy as np
        N, E, DIM, HEADS = (625, 10000, 768, 8)
        HD = DIM // HEADS
        EPS = 1e-05

        def layer_norm(x, w, b):
            mu = jnp.mean(x, axis=-1, keepdims=True)
            var = jnp.var(x, axis=-1, keepdims=True)
            return (x - mu) * jax.lax.rsqrt(var + EPS) * w + b

        def gatv2(x, src, dst, Ws, bs, Wd, bd, attn):
            H, D = attn.shape
            fs = (x @ Ws + bs).reshape(-1, H, D)
            fd = (x @ Wd + bd).reshape(-1, H, D)
            e = jax.nn.leaky_relu(fs[src] + fd[dst], 0.2)
            logits = jnp.einsum('ehd,hd->eh', e, attn)
            m = jax.ops.segment_max(logits, dst, num_segments=N)
            ex = jnp.exp(logits - m[dst])
            denom = jax.ops.segment_sum(ex, dst, num_segments=N)
            alpha = ex / denom[dst]
            out = jax.ops.segment_sum(alpha[:, :, None] * fs[src], dst, num_segments=N)
            return jax.nn.elu(out)
        key = jax.random.key(seed)
        ks = jax.random.split(key, 10)
        s = 1.0 / np.sqrt(DIM)
        return {'x': jax.random.normal(ks[0], (N, DIM), jnp.float32), 'src': jax.random.randint(ks[1], (E,), 0, N, jnp.int32), 'dst': jax.random.randint(ks[2], (E,), 0, N, jnp.int32), 'W1s': jax.random.normal(ks[3], (DIM, DIM), jnp.float32) * s, 'b1s': jnp.zeros((DIM,), jnp.float32), 'W1d': jax.random.normal(ks[4], (DIM, DIM), jnp.float32) * s, 'b1d': jnp.zeros((DIM,), jnp.float32), 'attn1': jax.random.normal(ks[5], (HEADS, HD), jnp.float32) * s, 'ln1_w': jnp.ones((DIM,), jnp.float32), 'ln1_b': jnp.zeros((DIM,), jnp.float32), 'Wos': jax.random.normal(ks[6], (DIM, DIM), jnp.float32) * s, 'bos': jnp.zeros((DIM,), jnp.float32), 'Wod': jax.random.normal(ks[7], (DIM, DIM), jnp.float32) * s, 'bod': jnp.zeros((DIM,), jnp.float32), 'attno': jax.random.normal(ks[8], (1, DIM), jnp.float32) * s, 'lno_w': jnp.ones((DIM,), jnp.float32), 'lno_b': jnp.zeros((DIM,), jnp.float32)}
    _L0_gnn_all = _L0_gnn_setup()
    _L0_gnn_in = {k: v for k, v in _L0_gnn_all.items() if k in ('W1s', 'b1s', 'W1d', 'b1d', 'attn1', 'ln1_w', 'ln1_b', 'Wos', 'bos', 'Wod', 'bod', 'attno', 'lno_w', 'lno_b')}
    del _L0_gnn_all

    def _L0_ffn_setup():
        import jax, jax.numpy as jnp
        import numpy as np
        SEQ, BATCH, EMBED = (1024, 2, 768)
        E = 16
        FFN_H = 1536
        K_SHARED = 1
        K_ROUTE = 3
        LN_EPS = 1e-05
        NEG_INF = -1000000000.0
        key = jax.random.key(seed)
        ks = jax.random.split(key, 4)
        x = jax.random.normal(ks[0], (SEQ, BATCH, EMBED), dtype=jnp.float32)
        gate_w = jax.random.normal(ks[1], (EMBED, E), dtype=jnp.float32) * 0.02
        gate_b = jnp.zeros((E,), jnp.float32)
        fc1_w = jax.random.normal(ks[2], (E, EMBED, FFN_H), dtype=jnp.float32) * 0.02
        fc1_b = jnp.zeros((E, FFN_H), jnp.float32)
        ln_w = jnp.ones((E, FFN_H), jnp.float32)
        ln_b = jnp.zeros((E, FFN_H), jnp.float32)
        fc2_w = jax.random.normal(ks[3], (E, FFN_H, EMBED), dtype=jnp.float32) * 0.02
        fc2_b = jnp.zeros((E, EMBED), jnp.float32)
        return {'x': x, 'gate_w': gate_w, 'gate_b': gate_b, 'fc1_w': fc1_w, 'fc1_b': fc1_b, 'ln_w': ln_w, 'ln_b': ln_b, 'fc2_w': fc2_w, 'fc2_b': fc2_b}
    _L0_ffn_all = _L0_ffn_setup()
    _L0_ffn_in = {k: v for k, v in _L0_ffn_all.items() if k in ('gate_w', 'gate_b', 'fc1_w', 'fc1_b', 'ln_w', 'ln_b', 'fc2_w', 'fc2_b')}
    del _L0_ffn_all
    return {'x': x, 'src': src, 'dst': dst, 'L0_gnn_W1s': _L0_gnn_in['W1s'], 'L0_gnn_b1s': _L0_gnn_in['b1s'], 'L0_gnn_W1d': _L0_gnn_in['W1d'], 'L0_gnn_b1d': _L0_gnn_in['b1d'], 'L0_gnn_attn1': _L0_gnn_in['attn1'], 'L0_gnn_ln1_w': _L0_gnn_in['ln1_w'], 'L0_gnn_ln1_b': _L0_gnn_in['ln1_b'], 'L0_gnn_Wos': _L0_gnn_in['Wos'], 'L0_gnn_bos': _L0_gnn_in['bos'], 'L0_gnn_Wod': _L0_gnn_in['Wod'], 'L0_gnn_bod': _L0_gnn_in['bod'], 'L0_gnn_attno': _L0_gnn_in['attno'], 'L0_gnn_lno_w': _L0_gnn_in['lno_w'], 'L0_gnn_lno_b': _L0_gnn_in['lno_b'], 'L0_ffn_gate_w': _L0_ffn_in['gate_w'], 'L0_ffn_gate_b': _L0_ffn_in['gate_b'], 'L0_ffn_fc1_w': _L0_ffn_in['fc1_w'], 'L0_ffn_fc1_b': _L0_ffn_in['fc1_b'], 'L0_ffn_ln_w': _L0_ffn_in['ln_w'], 'L0_ffn_ln_b': _L0_ffn_in['ln_b'], 'L0_ffn_fc2_w': _L0_ffn_in['fc2_w'], 'L0_ffn_fc2_b': _L0_ffn_in['fc2_b']}

def reference(x, src, dst, L0_gnn_W1s, L0_gnn_b1s, L0_gnn_W1d, L0_gnn_b1d, L0_gnn_attn1, L0_gnn_ln1_w, L0_gnn_ln1_b, L0_gnn_Wos, L0_gnn_bos, L0_gnn_Wod, L0_gnn_bod, L0_gnn_attno, L0_gnn_lno_w, L0_gnn_lno_b, L0_ffn_gate_w, L0_ffn_gate_b, L0_ffn_fc1_w, L0_ffn_fc1_b, L0_ffn_ln_w, L0_ffn_ln_b, L0_ffn_fc2_w, L0_ffn_fc2_b):
    import jax
    import jax.numpy as jnp

    def _L0_gnn_ref(x, src, dst, W1s, b1s, W1d, b1d, attn1, ln1_w, ln1_b, Wos, bos, Wod, bod, attno, lno_w, lno_b):
        import jax, jax.numpy as jnp
        import numpy as np
        N, E, DIM, HEADS = (625, 10000, 768, 8)
        HD = DIM // HEADS
        EPS = 1e-05

        def layer_norm(x, w, b):
            mu = jnp.mean(x, axis=-1, keepdims=True)
            var = jnp.var(x, axis=-1, keepdims=True)
            return (x - mu) * jax.lax.rsqrt(var + EPS) * w + b

        def gatv2(x, src, dst, Ws, bs, Wd, bd, attn):
            H, D = attn.shape
            fs = (x @ Ws + bs).reshape(-1, H, D)
            fd = (x @ Wd + bd).reshape(-1, H, D)
            e = jax.nn.leaky_relu(fs[src] + fd[dst], 0.2)
            logits = jnp.einsum('ehd,hd->eh', e, attn)
            m = jax.ops.segment_max(logits, dst, num_segments=N)
            ex = jnp.exp(logits - m[dst])
            denom = jax.ops.segment_sum(ex, dst, num_segments=N)
            alpha = ex / denom[dst]
            out = jax.ops.segment_sum(alpha[:, :, None] * fs[src], dst, num_segments=N)
            return jax.nn.elu(out)
        h = gatv2(x, src, dst, W1s, b1s, W1d, b1d, attn1).reshape(N, DIM)
        h = layer_norm(h + x, ln1_w, ln1_b)
        out = gatv2(h, src, dst, Wos, bos, Wod, bod, attno).reshape(N, DIM)
        return layer_norm(out, lno_w, lno_b)

    def _L0_ffn_ref(x, gate_w, gate_b, fc1_w, fc1_b, ln_w, ln_b, fc2_w, fc2_b):
        import jax, jax.numpy as jnp
        import numpy as np
        SEQ, BATCH, EMBED = (1024, 2, 768)
        E = 16
        FFN_H = 1536
        K_SHARED = 1
        K_ROUTE = 3
        LN_EPS = 1e-05
        NEG_INF = -1000000000.0
        S, B, D = x.shape
        T = S * B
        xf = x.reshape(T, D)
        scores = xf @ gate_w + gate_b
        scores = scores.at[:, :K_SHARED].set(NEG_INF)
        probs = jax.nn.softmax(scores, axis=-1)
        topv, topi = jax.lax.top_k(probs, K_ROUTE)
        combine = jnp.zeros((T, E), xf.dtype)
        combine = combine.at[jnp.arange(T)[:, None], topi].add(topv)
        combine = combine.at[:, :K_SHARED].add(1.0)
        h = jnp.einsum('td,edh->eth', xf, fc1_w) + fc1_b[:, None, :]
        h = jax.nn.gelu(h, approximate=False)
        mu = h.mean(-1, keepdims=True)
        var = h.var(-1, keepdims=True)
        h = (h - mu) * jax.lax.rsqrt(var + LN_EPS) * ln_w[:, None, :] + ln_b[:, None, :]
        y = jnp.einsum('eth,ehd->etd', h, fc2_w) + fc2_b[:, None, :]
        out = jnp.einsum('te,etd->td', combine, y)
        return out.reshape(S, B, D)
    x = x + _L0_gnn_ref(_layernorm(x, axis=-1), src, dst, L0_gnn_W1s, L0_gnn_b1s, L0_gnn_W1d, L0_gnn_b1d, L0_gnn_attn1, L0_gnn_ln1_w, L0_gnn_ln1_b, L0_gnn_Wos, L0_gnn_bos, L0_gnn_Wod, L0_gnn_bod, L0_gnn_attno, L0_gnn_lno_w, L0_gnn_lno_b)
    x = x + _L0_ffn_ref(_layernorm(x, axis=-1)[None], L0_ffn_gate_w, L0_ffn_gate_b, L0_ffn_fc1_w, L0_ffn_fc1_b, L0_ffn_ln_w, L0_ffn_ln_b, L0_ffn_fc2_w, L0_ffn_fc2_b)[0]
    return x

_drawn_inputs = setup_inputs


def setup_inputs(seed=0):
    import zlib

    import numpy as np

    out = dict(_drawn_inputs(seed))
    spreads = {'L0_gnn_b1s': (0.0, 0.1),
     'L0_gnn_b1d': (0.0, 0.8),
     'L0_gnn_ln1_w': (1.0, 0.2),
     'L0_gnn_ln1_b': (0.0, 0.1),
     'L0_gnn_bos': (0.0, 0.1),
     'L0_gnn_bod': (0.0, 0.392),
     'L0_gnn_lno_w': (1.0, 0.2),
     'L0_gnn_lno_b': (0.0, 0.1),
     'L0_ffn_gate_b': (0.0, 0.1),
     'L0_ffn_fc1_b': (0.0, 0.1),
     'L0_ffn_ln_w': (1.0, 0.2),
     'L0_ffn_ln_b': (0.0, 0.1),
     'L0_ffn_fc2_b': (0.0, 0.1)}
    factors = {'L0_gnn_W1d': 3.143}
    for name, (base, spread) in spreads.items():
        noise = np.random.default_rng([zlib.crc32(name.encode()), seed]).standard_normal(out[name].shape)
        drawn = base * np.exp(spread * noise) if base else spread * noise
        out[name] = jnp.asarray(drawn.astype(out[name].dtype))
    for name, factor in factors.items():
        out[name] = (out[name] * factor).astype(out[name].dtype)
    return out
```

```python
import concourse.bass as bass
from concourse import mybir
from contextlib import ExitStack, contextmanager

F32 = mybir.dt.float32
F16 = mybir.dt.float16
I32 = mybir.dt.int32
ALU = mybir.AluOpType
ACT = mybir.ActivationFunctionType
AX = mybir.AxisListType

N, D, E_GNN = 625, 768, 20000
P, T = 125, 5
ET = E_GNN // P
KD = D // 128
HALF = D // 2
SLOPE, EPS = 0.2, 1e-5
ABSENT = -1e30
TRASH = N * N
G = 8
LAG_B, LAG_S = 2, 5

X, FF = 16, 1536
TOP = 3
KF = FF // 128
S = 128
SHARED = (N + S - 1) // S
MAXT = SHARED + (N * TOP + X * (S - 1)) // S
MINT = SHARED + (N * TOP + S - 1) // S
NTAB = MAXT + 1


@contextmanager
def stage(nc):
    used = []

    def sem(name):
        used.append(nc.alloc_semaphore(name))
        return used[-1]

    with ExitStack() as memory:
        yield memory, sem
        nc.clear_and_free_semaphores(used)
        nc.all_engine_barrier()


class Chain:

    def __init__(self, engine, sem):
        self.engine, self.sem, self.n = engine, sem, 0

    def __call__(self, ins):
        self.n += 1
        ins.then_inc(self.sem, 1)
        self.engine.wait_ge(self.sem, self.n)


def gnn_moe(nc, a, out):
    top = ExitStack()
    with top:
        def sb(name, shape, dt=F32, ctx=top):
            return ctx.enter_context(nc.sbuf_tensor(name, shape, dt))

        def dram(name, shape, dt=F32):
            return nc.dram_tensor(name, shape, dt, kind="Internal").ap()

        bank = [top.enter_context(nc.psum_tensor(f"bank{i}", [128, 512], F32)) for i in range(8)]
        x_rows = sb("x_rows", [P, T, D])
        ident = sb("ident", [128, 128])
        eps = sb("eps", [128, 1])
        before = sb("before", [P, P])
        ones = sb("ones", [P, P])
        slot_out = dram("slot_out", (NTAB * S, D))
        gnn = ExitStack()
        with gnn:
            graph_layers(nc, a, gnn, sb, dram, bank, x_rows, ident, eps, before, ones, slot_out)
        moe = ExitStack()
        with moe:
            mixture(nc, a, out, moe, sb, dram, bank, x_rows, ident, eps, before, ones, slot_out)


def row_stats(nc, chain, src, width, stats, mv):
    parts = width // (384 if width == D else 512)
    step = width // parts
    for c in range(parts):
        last = nc.vector.bn_stats(stats[:, c, :], src[:, c * step:(c + 1) * step])
        if c < parts - 1:
            last.then_inc(chain.sem, 1)
            chain.n += 1
    chain(last)
    chain(nc.vector.bn_aggr(mv, stats[:, 0:parts, :].rearrange("p c s -> p (c s)")))


def graph_layers(nc, a, gnn, sb, dram, bank, x_rows, ident, eps, before, ones, slot_out):
    def gb(name, shape, dt=F32):
        return sb(name, shape, dt, gnn)

    xn = gb("xn", [P, T, D])
    fs = gb("fs", [P, T, D])
    counts = gb("counts", [P, T, N])
    edge_idx = gb("edge_idx", [P, ET, 3], I32)
    end_f = gb("end_f", [P, 2, ET])
    src_iota = gb("src_iota", [P, N], F16)
    weights = gb("weights", [128, 2, KD, D])
    vecs = gb("vecs", [P, 5, D])
    attn_s = gb("attn_s", [P, 2, D])
    mv = gb("mv", [P, T, 2])
    stats = gb("stats", [P, 2, 6])
    std = gb("std", [P, T])
    rstd = gb("rstd", [P, T])

    def inputs(k):
        p = ("W1s", "W1d", "b1s", "b1d", "attn1", "ln1_w", "ln1_b") if k == 0 else \
            ("Wos", "Wod", "bos", "bod", "attno", "lno_w", "lno_b")
        return [a["L0_gnn_" + n] for n in p]

    heads = (8, 1)
    logit_tab = [dram(f"logit_tab{k}", (N * N + P, heads[k])) for k in range(2)]
    fs_tab = [dram(f"fs_tab{k}", (N, D + heads[k])) for k in range(2)]
    fd_tab = [dram(f"fd_tab{k}", (N, D + heads[k])) for k in range(2)]

    with stage(nc) as (prep, sem):
        absent = sb("absent", [128, N * 8], F32, prep)
        later = sb("later", [P, P], F32, prep)
        trash = sb("trash", [P, 1], F32, prep)
        ends = sb("ends", [P, 2, ET], I32, prep)
        key = sb("key", [P, ET], F32, prep)
        key_col = sb("key_col", [P, 2, 4], F32, prep)
        repeats = sb("repeats", [P, ET], F32, prep)
        tmp = sb("tmp", [P, ET], F32, prep)
        junk = sb("junk", [P, 4, P], F32, prep)
        x_in, ends_in, const_ok, absent_ok = (sem(s) for s in ("x_in", "ends_in", "const_ok", "absent_ok"))
        tab_set, prep_chain, prep_act = sem("tab_set"), sem("prep_chain"), sem("prep_act")
        var_ok, cols_ok, keys_turned, keys_read, pool_chain = (
            sem(s) for s in ("var_ok", "cols_ok", "keys_turned", "keys_read", "pool_chain"))
        with nc.Block() as block:
            @block.sync
            def _(sp):
                sp.dma_start(x_rows[:], a["x"].rearrange("(t p) d -> p t d", p=P)).then_inc(x_in, 16)
                sp.wait_ge(absent_ok, 1)
                tab0 = logit_tab[0][0:N * N, :].rearrange("(t p s) h -> t p (s h)", t=T, p=P)
                for t in range(T):
                    sp.dma_start(tab0[t], absent[0:P, :]).then_inc(tab_set, 16)
                sp.dma_start(logit_tab[1][0:N * N, :].rearrange("(p s) h -> p (s h)", p=P),
                             absent[0:P, 0:N * T]).then_inc(tab_set, 16)
                row = MINT * S
                blocks = 0
                while row < NTAB * S:
                    per = min(6, (NTAB * S - row) // 128)
                    sp.dma_start(slot_out[row:row + 128 * per, :].rearrange("(p r) d -> p (r d)", p=128),
                                 absent[:, 0:per * D]).then_inc(tab_set, 16)
                    row += 128 * per
                    blocks += 1
                sp.wait_ge(tab_set, 16 * (T + 1 + blocks))

            @block.gpsimd
            def _(pool):
                nc.gpsimd.memset(absent[:], ABSENT).then_inc(absent_ok, 1)
                link = Chain(pool, pool_chain)
                link(nc.gpsimd.memset(ident[:], 0.0))
                link(nc.gpsimd.affine_select(out=ident[:], in_=ident[:], compare_op=ALU.not_equal, fill=1.0,
                                             base=0, pattern=[[-1, 128]], channel_multiplier=1))
                link(nc.gpsimd.memset(ones[:], 1.0))
                link(nc.gpsimd.memset(eps[:], EPS))
                link(nc.gpsimd.affine_select(out=later[:], in_=ones[:], compare_op=ALU.is_gt, fill=0.0,
                                             base=0, pattern=[[-1, P]], channel_multiplier=1))
                link(nc.gpsimd.affine_select(out=before[:], in_=ones[:], compare_op=ALU.is_gt, fill=0.0,
                                             base=0, pattern=[[1, P]], channel_multiplier=-1))
                link(nc.gpsimd.iota(trash[:], pattern=[[0, 1]], base=TRASH, channel_multiplier=1,
                                    allow_small_or_imprecise_dtypes=True))
                nc.gpsimd.iota(src_iota[:], pattern=[[1, N]], base=0, channel_multiplier=0,
                               allow_small_or_imprecise_dtypes=True).then_inc(const_ok, 1)

            @block.scalar
            def _(act):
                act.dma_start(ends[:, 0, :], a["src"].rearrange("(p t) -> p t", p=P)).then_inc(ends_in, 16)
                act.dma_start(ends[:, 1, :], a["dst"].rearrange("(p t) -> p t", p=P)).then_inc(ends_in, 16)
                act.wait_ge(const_ok, 1)
                act.wait_ge(var_ok, 1)
                nc.scalar.activation(std[:], mv[:, :, 1], ACT.Sqrt, bias=eps[0:P, :]).then_inc(prep_act, 1)

            @block.vector
            def _(dve):
                link = Chain(dve, prep_chain)
                dve.wait_ge(ends_in, 32)
                link(nc.vector.tensor_copy(end_f[:], ends[:]))
                link(nc.vector.tensor_copy(edge_idx[:, :, 0:2], ends[:].rearrange("p c t -> p t c")))
                link(nc.vector.scalar_tensor_tensor(out=key[:], in0=end_f[:, 1, :], scalar=float(N),
                                                    in1=end_f[:, 0, :], op0=ALU.mult, op1=ALU.add))
                dve.wait_ge(x_in, 16)
                for t in range(T):
                    row_stats(nc, link, x_rows[:, t, :], D, stats, mv[:, t, :])
                nc.vector.tensor_copy(repeats[:], key[:]).then_inc(var_ok, 1)
                dve.wait_ge(var_ok, 1)
                dve.wait_ge(prep_act, 1)
                link(nc.vector.reciprocal(rstd[:], std[:]))
                for t in range(T):
                    link(nc.vector.tensor_scalar(xn[:, t, :], x_rows[:, t, :], mv[:, t, 0:1], rstd[:, t:t + 1],
                                                 ALU.subtract, ALU.mult))
                with dve.Fori(0, ET // 8) as g:
                    for b in range(2):
                        dve.wait_ge(keys_turned, 2 * g + b)
                        nc.vector.tensor_copy(key_col[:, b, :], key[:, bass.ds(g * 8 + 4 * b, 4)]).then_inc(cols_ok, 1)
                    for b in range(2):
                        dve.wait_ge(keys_turned, 2 * g + b + 1)
                        for u in range(4):
                            last = nc.vector.scalar_tensor_tensor(
                                out=junk[:, u, :], in0=bank[b][0:P, u * P:(u + 1) * P],
                                scalar=key_col[:, b, u:u + 1], in1=later[:], op0=ALU.is_equal, op1=ALU.mult,
                                accum_out=repeats[:, bass.ds(g * 8 + 4 * b + u, 1)])
                            last.then_inc(keys_read, 1)
                            dve.wait_ge(keys_read, g * 8 + 4 * b + u + 1)
                link(nc.vector.tensor_scalar(repeats[:], repeats[:], 1.0, None, ALU.min))
                link(nc.vector.tensor_scalar(tmp[:], key[:], -1.0, trash[:, 0:1], ALU.mult, ALU.add))
                link(nc.vector.tensor_tensor(tmp[:], tmp[:], repeats[:], ALU.mult))
                link(nc.vector.tensor_tensor(tmp[:], tmp[:], key[:], ALU.add))
                link(nc.vector.tensor_copy(edge_idx[:, :, 2], tmp[:]))

            @block.tensor
            def _(pe):
                pe.wait_ge(const_ok, 1)
                with pe.Fori(0, ET // 8) as g:
                    for b in range(2):
                        pe.wait_ge(cols_ok, 2 * g + b + 1)
                        pe.wait_ge(keys_read, g * 8)
                        for u in range(4):
                            last = nc.tensor.transpose(bank[b][0:P, u * P:(u + 1) * P],
                                                       key_col[:, b, u:u + 1].to_broadcast([P, P]),
                                                       ident[0:P, 0:P])
                        last.then_inc(keys_turned, 1)

    for k in range(2):
        H = heads[k]
        HD = D // H
        Ws, Wd, bs, bd, attn, ln_w, ln_b = inputs(k)

        with stage(nc) as (project, sem):
            xT = sb(f"xT{k}", [128, KD, N], F32, project)
            table_rows = sb(f"table_rows{k}", [P, 4, D + H], F32, project)
            prod = sb(f"prod{k}", [P, D], F32, project)
            w_in = [sem(f"w_in{k}{c}") for c in range(2)]
            vec_in, turned, xT_ok = sem(f"vec_in{k}"), sem(f"turned{k}"), sem(f"xT_ok{k}")
            proj_ok, proj_read = sem(f"proj_ok{k}"), sem(f"proj_read{k}")
            tab_row_ok, tab_out, pchain = sem(f"tab_row_ok{k}"), [sem(f"tab_out{k}{u}") for u in range(4)], sem(f"pchain{k}")
            with nc.Block() as block:
                @block.sync
                def _(sp):
                    for c, w in enumerate((Ws, Wd)):
                        sp.dma_start(weights[:, c], w.rearrange("(k p) n -> p k n", p=128)).then_inc(w_in[c], 16)
                    for n in range(2 * T):
                        t, c = divmod(n, 2)
                        sp.wait_ge(tab_row_ok, n + 1)
                        tab = (fs_tab, fd_tab)[c][k]
                        sp.dma_start(tab[t * P:(t + 1) * P, :], table_rows[:, n % 4, :]).then_inc(tab_out[n % 4], 16)
                    for u in range(4):
                        sp.wait_ge(tab_out[u], 16 * len(range(u, 2 * T, 4)))

                @block.scalar
                def _(act):
                    for c, v in enumerate((bs, bd, attn, ln_w, ln_b)):
                        flat = v if len(v.shape) == 1 else v.rearrange("h d -> (h d)")
                        act.dma_start(vecs[:, c, :], flat.partition_broadcast(P)).then_inc(vec_in, 16)
                    for n in range(2 * T):
                        act.wait_ge(turned, n + 1)
                        t, h = divmod(n, 2)
                        nc.scalar.copy(xT[:, 3 * h:3 * h + 3, t * P:(t + 1) * P],
                                       bank[4 + n % 4][:, 0:3 * P].rearrange("p (k n) -> p k n", k=3)).then_inc(xT_ok, 1)

                @block.tensor
                def _(pe):
                    for n in range(2 * T):
                        t, h = divmod(n, 2)
                        if n >= 4:
                            pe.wait_ge(xT_ok, n - 3)
                        for u in range(3):
                            c = 3 * h + u
                            last = nc.tensor.transpose(bank[4 + n % 4][:, u * P:(u + 1) * P],
                                                       xn[:, t, c * 128:(c + 1) * 128], ident[0:P, 0:P])
                        last.then_inc(turned, 1)
                    for n in range(2 * T):
                        t, c = divmod(n, 2)
                        pe.wait_ge(xT_ok, 2 * t + 2)
                        pe.wait_ge(w_in[c], 16)
                        if n >= 2:
                            pe.wait_ge(proj_read, n - 1)
                        for h in range(2):
                            for kk in range(KD):
                                last = nc.tensor.matmul(bank[2 * (n % 2) + h][0:P, 0:HALF],
                                                        xT[:, kk, t * P:(t + 1) * P],
                                                        weights[:, c, kk, h * HALF:(h + 1) * HALF],
                                                        start=(kk == 0), stop=(kk == KD - 1))
                        last.then_inc(proj_ok, 1)

                @block.vector
                def _(dve):
                    link = Chain(dve, pchain)
                    dve.wait_ge(vec_in, 16 * 5)
                    link(nc.vector.tensor_scalar(attn_s[:, 0, :], vecs[:, 2, :], SLOPE, None, ALU.mult))
                    link(nc.vector.tensor_scalar(attn_s[:, 1, :], vecs[:, 2, :], 1.0 - SLOPE, None, ALU.mult))
                    for n in range(2 * T):
                        t, c = divmod(n, 2)
                        dve.wait_ge(proj_ok, n + 1)
                        if n >= 4:
                            dve.wait_ge(tab_out[n % 4], 16 * (n // 4))
                        for h in range(2):
                            last = nc.vector.tensor_tensor(table_rows[:, n % 4, h * HALF:(h + 1) * HALF],
                                                           bank[2 * (n % 2) + h][0:P, 0:HALF],
                                                           vecs[:, c, h * HALF:(h + 1) * HALF], ALU.add)
                            if h == 0:
                                link(last)
                        last.then_inc(proj_read, 1)
                        dve.wait_ge(proj_read, n + 1)
                        row = table_rows[:, n % 4, 0:D]
                        if c == 0:
                            link(nc.vector.tensor_copy(fs[:, t, :], row))
                        link(nc.vector.tensor_tensor(prod[:], row, attn_s[:, 0, :], ALU.mult))
                        nc.vector.tensor_reduce(table_rows[:, n % 4, D:D + H],
                                                prod[:].rearrange("p (h d) -> p h d", h=H),
                                                AX.X, ALU.add).then_inc(tab_row_ok, 1)
                        dve.wait_ge(tab_row_ok, n + 1)

        with stage(nc) as (edges, sem):
            z = sb(f"z{k}", [P, G, D + H], F32, edges)
            logit = sb(f"logit{k}", [P, G, H], F32, edges)
            idx = sb(f"idx{k}", [P, G, 3], I32, edges)
            relu = sb(f"relu{k}", [P, 2, D], F32, edges)
            part = sb(f"part{k}", [P, 2, H], F32, edges)
            idx_ok, go, logit_ok, scattered = (sem(f"{s}{k}") for s in ("idx_ok", "go", "logit_ok", "scattered"))
            src_in = [sem(f"src_in{k}{u}") for u in range(G)]
            sum_in = [sem(f"sum_in{k}{u}") for u in range(G)]
            relu_ok, part_ok = sem(f"relu_ok{k}"), sem(f"part_ok{k}")
            if k == 0:
                hot = sb("hot", [P, 2, 2, N], F16, edges)
                hot_ok, counted = sem("hot_ok"), sem("counted")
                REST = N - 512
            with nc.Block() as block:
                @block.gpsimd
                def _(pool):
                    def copy_idx(u, n):
                        nc.gpsimd.tensor_copy(idx[:, u, :], edge_idx[:, bass.ds(n, 1), :]
                                              .rearrange("p o c -> p (o c)")).then_inc(idx_ok, 1)

                    def gather_source(u, n, g, again):
                        copy_idx(u, n)
                        pool.wait_ge(idx_ok, n + 1)
                        if again:
                            pool.wait_ge(logit_ok, n + 1 - G)
                        nc.gpsimd.sem_inc(go, 1)
                        nc.gpsimd.indirect_dma_start(
                            z[:, u, :], None, fs_tab[k],
                            bass.IndirectOffsetOnAxis(ap=idx[:, u, 0:1], axis=0)).then_inc(src_in[u], 16)

                    def add_destination(u, g):
                        pool.wait_ge(src_in[u], g * 16 + 16)
                        nc.gpsimd.sem_inc(go, 1)
                        nc.gpsimd.indirect_dma_start(
                            z[:, u, :], None, fd_tab[k],
                            bass.IndirectOffsetOnAxis(ap=idx[:, u, 1:2], axis=0),
                            compute_op=ALU.add).then_inc(sum_in[u], 16)

                    def scatter(u, n):
                        pool.wait_ge(logit_ok, n + 1)
                        pool.wait_ge(scattered, n * 16)
                        nc.gpsimd.sem_inc(go, 1)
                        nc.gpsimd.indirect_dma_start(
                            logit_tab[k], bass.IndirectOffsetOnAxis(ap=idx[:, u, 2:3], axis=0),
                            logit[:, u, :], None).then_inc(scattered, 16)

                    for u in range(G):
                        gather_source(u, u, 0, False)
                        if u >= LAG_B:
                            add_destination(u - LAG_B, 0)
                        if u >= LAG_S:
                            scatter(u - LAG_S, u - LAG_S)
                    with pool.Fori(1, ET // G) as g:
                        for u in range(G):
                            gather_source(u, g * G + u, g, True)
                            if u >= LAG_B:
                                add_destination(u - LAG_B, g)
                            else:
                                add_destination(u - LAG_B + G, g - 1)
                            scatter((u - LAG_S) % G, g * G + u - LAG_S)
                    for u in range(LAG_B):
                        add_destination(G - LAG_B + u, ET // G - 1)
                    for u in range(LAG_S):
                        scatter(G - LAG_S + u, ET - LAG_S + u)
                    pool.wait_ge(scattered, 16 * ET)

                @block.vector
                def _(dve):
                    def reduce_tile(u, n, g, again):
                        b = u % 2
                        if k == 0:
                            if again or u >= 2:
                                dve.wait_ge(counted, n - 1)
                            for c in range(2):
                                nc.vector.tensor_scalar(hot[:, b, c, :], src_iota[:], end_f[:, c, bass.ds(n, 1)],
                                                        None, ALU.is_equal).then_inc(hot_ok, 1)
                        dve.wait_ge(sum_in[u], g * 16 + 16)
                        if again:
                            dve.wait_ge(scattered, (n + 1 - G) * 16)
                        if H == 1:
                            nc.vector.scalar_tensor_tensor(out=relu[:, b, :], in0=z[:, u, 0:D], scalar=0.0,
                                                           in1=attn_s[:, 1, :], op0=ALU.max, op1=ALU.mult,
                                                           accum_out=part[:, b, :]).then_inc(part_ok, 1)
                        else:
                            nc.vector.scalar_tensor_tensor(out=relu[:, b, :], in0=z[:, u, 0:D], scalar=0.0,
                                                           in1=attn_s[:, 1, :], op0=ALU.max,
                                                           op1=ALU.mult).then_inc(relu_ok, 1)
                            dve.wait_ge(relu_ok, n + 1)
                            nc.vector.tensor_reduce(part[:, b, :], relu[:, b, :].rearrange("p (h d) -> p h d", h=H),
                                                    AX.X, ALU.add).then_inc(part_ok, 1)
                        dve.wait_ge(part_ok, n + 1)
                        nc.vector.tensor_tensor(logit[:, u, :], part[:, b, :], z[:, u, D:D + H],
                                                ALU.add).then_inc(logit_ok, 1)

                    for u in range(G):
                        reduce_tile(u, u, 0, False)
                    with dve.Fori(1, ET // G) as g:
                        for u in range(G):
                            reduce_tile(u, g * G + u, g, True)
                    if k == 0:
                        dve.wait_ge(counted, ET)
                        for t in range(T):
                            nc.vector.tensor_copy(counts[:, t, 0:512], bank[t][0:P, :])
                            nc.vector.tensor_copy(counts[:, t, 512:N],
                                                  bank[5 + t // 4][0:P, (t % 4) * REST:(t % 4 + 1) * REST])

                if k == 0:
                    @block.tensor
                    def _(pe):
                        def count_tile(u, n, first, final):
                            pe.wait_ge(hot_ok, 2 * n + 2)
                            for t in range(T):
                                dst_hot = hot[:, u % 2, 1, t * P:(t + 1) * P]
                                nc.tensor.matmul(bank[t][0:P, :], dst_hot, hot[:, u % 2, 0, 0:512],
                                                 start=first, stop=final, skip_group_check=True)
                                last = nc.tensor.matmul(
                                    bank[5 + t // 4][0:P, (t % 4) * REST:(t % 4 + 1) * REST], dst_hot,
                                    hot[:, u % 2, 0, 512:N], start=first and t % 4 == 0, stop=final,
                                    skip_group_check=True)
                            last.then_inc(counted, 1)

                        for u in range(G):
                            count_tile(u, u, u == 0, False)
                        with pe.Fori(1, ET // G) as g:
                            for u in range(G):
                                count_tile(u, g * G + u, False, False)

        with stage(nc) as (attend, sem):
            pair = sb(f"pair{k}", [P, 2, N, H], F32, attend)
            prob = sb(f"prob{k}", [P, H, N], F32, attend)
            probT = sb(f"probT{k}", [P, 2, T, P], F32, attend)
            negmax = sb(f"negmax{k}", [P, H], F32, attend)
            den = sb(f"den{k}", [P, H], F32, attend)
            rden = sb(f"rden{k}", [P, H], F32, attend)
            o = sb(f"o{k}", [P, D], F32, attend)
            o_neg = sb(f"o_neg{k}", [P, D], F32, attend)
            res = sb(f"res{k}", [P, T, D], F32, attend) if k == 1 else None
            pair_in = [sem(f"pair_in{k}{u}") for u in range(2)]
            max_ok, exp_ok, prob_ok, turned, probT_ok, summed, achain, neg_ok, elu_ok, std_ok, mul_ok, var_ok = (
                sem(f"{s}{k}") for s in ("max_ok", "exp_ok", "prob_ok", "p_turned", "probT_ok", "summed", "achain",
                                         "neg_ok", "elu_ok", "std_ok", "mul_ok", "a_var_ok"))
            cols = [(h * HD, HD) for h in range(H)] if H > 1 else [(0, HALF), (HALF, HALF)]
            with nc.Block() as block:
                @block.sync
                def _(sp):
                    tab = logit_tab[k][0:N * N, :].rearrange("(t p s) h -> t p (s h)", t=T, p=P)
                    for t in range(T):
                        if t >= 2:
                            sp.wait_ge(exp_ok, (t - 1) * H)
                        sp.dma_start(pair[:, t % 2].rearrange("p s h -> p (s h)"), tab[t]).then_inc(pair_in[t % 2], 16)

                @block.tensor
                def _(pe):
                    for t in range(T):
                        for h in range(H):
                            n = t * H + h
                            b = 2 + 2 * (n % 2)
                            pe.wait_ge(prob_ok, n + 1)
                            if n >= 2:
                                pe.wait_ge(probT_ok, 2 * (n - 1))
                            for c in range(T):
                                to = bank[b][0:P, c * P:(c + 1) * P] if c < 4 else bank[b + 1][0:P, 0:P]
                                last = nc.tensor.transpose(to, prob[:, h, c * P:(c + 1) * P], ident[0:P, 0:P])
                            last.then_inc(turned, 1)
                            pe.wait_ge(probT_ok, 2 * (n + 1))
                            if t >= 1 and h == 0:
                                pe.wait_ge(mul_ok, 2 * t)
                            for lo, w in ([cols[h]] if H > 1 else cols):
                                for c in range(T):
                                    last = nc.tensor.matmul(bank[lo // HALF][0:P, lo % HALF:lo % HALF + w],
                                                            probT[:, n % 2, c, :], fs[:, c, lo:lo + w],
                                                            start=(c == 0), stop=(c == T - 1))
                            last.then_inc(summed, 1)

                @block.scalar
                def _(act):
                    for t in range(T):
                        for h in range(H):
                            n = t * H + h
                            if h == 0:
                                act.wait_ge(max_ok, t + 1)
                            if t >= 1:
                                act.wait_ge(turned, n - H + 1)
                            nc.scalar.activation(prob[:, h, :], pair[:, t % 2, :, h], ACT.Exp,
                                                 bias=negmax[:, h:h + 1]).then_inc(exp_ok, 1)
                        for h in range(H):
                            n = t * H + h
                            act.wait_ge(turned, n + 1)
                            if n >= 2:
                                act.wait_ge(summed, n - 1)
                            b = 2 + 2 * (n % 2)
                            nc.scalar.copy(probT[:, n % 2, 0:4, :].rearrange("p c q -> p (c q)"),
                                           bank[b][0:P, 0:4 * P]).then_inc(probT_ok, 1)
                            nc.scalar.copy(probT[:, n % 2, 4, :], bank[b + 1][0:P, 0:P]).then_inc(probT_ok, 1)
                        act.wait_ge(neg_ok, t + 1)
                        nc.scalar.activation(o_neg[:], o_neg[:], ACT.Exp).then_inc(elu_ok, 1)
                    act.wait_ge(var_ok, 1)
                    nc.scalar.activation(std[:], mv[:, :, 1], ACT.Sqrt, bias=eps[0:P, :]).then_inc(std_ok, 1)

                @block.vector
                def _(dve):
                    link = Chain(dve, achain)
                    for t in range(T):
                        dve.wait_ge(pair_in[t % 2], 16 * (t // 2 + 1))
                        if t >= 1:
                            dve.wait_ge(exp_ok, t * H)
                        nc.vector.tensor_reduce(negmax[:], pair[:, t % 2].rearrange("p s h -> p h s"),
                                                AX.X, ALU.max, negate=True).then_inc(max_ok, 1)
                        for h in range(H):
                            n = t * H + h
                            dve.wait_ge(exp_ok, n + 1)
                            nc.vector.tensor_tensor_reduce(prob[:, h, :], prob[:, h, :], counts[:, t, :], 1.0, 0.0,
                                                           ALU.mult, ALU.add, den[:, h:h + 1]).then_inc(prob_ok, 1)
                        dve.wait_ge(prob_ok, (t + 1) * H)
                        link(nc.vector.tensor_scalar(den[:], den[:], 1e-30, None, ALU.max))
                        link(nc.vector.reciprocal(rden[:], den[:]))
                        dve.wait_ge(summed, (t + 1) * H)
                        for c in range(2):
                            hh = max(H // 2, 1)
                            scale = rden[:, (c * hh) % H:(c * hh) % H + hh]
                            nc.vector.tensor_tensor(
                                o[:, c * HALF:(c + 1) * HALF].rearrange("p (h d) -> p h d", h=hh),
                                bank[c][0:P, 0:HALF].rearrange("p (h d) -> p h d", h=hh),
                                scale.unsqueeze(2).to_broadcast([P, hh, HALF // hh]), ALU.mult).then_inc(mul_ok, 1)
                        dve.wait_ge(mul_ok, 2 * t + 2)
                        nc.vector.tensor_scalar(o_neg[:], o[:], 0.0, None, ALU.min).then_inc(neg_ok, 1)
                        dve.wait_ge(elu_ok, t + 1)
                        link(nc.vector.scalar_tensor_tensor(out=o[:], in0=o[:], scalar=0.0, in1=o_neg[:],
                                                            op0=ALU.max, op1=ALU.add))
                        dest = xn[:, t, :] if k == 0 else res[:, t, :]
                        if k == 0:
                            link(nc.vector.scalar_tensor_tensor(out=dest, in0=o[:], scalar=-1.0, in1=dest,
                                                                op0=ALU.add, op1=ALU.add))
                        else:
                            link(nc.vector.tensor_scalar(dest, o[:], -1.0, None, ALU.add))
                        row_stats(nc, link, dest, D, stats, mv[:, t, :])
                    nc.vector.tensor_copy(stats[:, 0, :], stats[:, 1, :]).then_inc(var_ok, 1)
                    dve.wait_ge(var_ok, 1)
                    dve.wait_ge(std_ok, 1)
                    link(nc.vector.reciprocal(rstd[:], std[:]))
                    for t in range(T):
                        dest = xn[:, t, :] if k == 0 else res[:, t, :]
                        link(nc.vector.scalar_tensor_tensor(out=dest, in0=dest, scalar=mv[:, t, 0:1],
                                                            in1=vecs[:, 3, :], op0=ALU.subtract, op1=ALU.mult))
                        link(nc.vector.scalar_tensor_tensor(out=dest, in0=dest, scalar=rstd[:, t:t + 1],
                                                            in1=vecs[:, 4, :], op0=ALU.mult, op1=ALU.add))
                        if k == 1:
                            link(nc.vector.tensor_tensor(x_rows[:, t, :], x_rows[:, t, :], dest, ALU.add))


def mixture(nc, a, out, moe, sb, dram, bank, x_rows, ident, eps, before, ones, slot_out):
    def mb(name, shape, dt=F32):
        return sb(name, shape, dt, moe)

    gate_w, gate_b, fc1_w, fc1_b, ln_w, ln_b, fc2_w, fc2_b = (
        a["L0_ffn_" + n] for n in ("gate_w", "gate_b", "fc1_w", "fc1_b", "ln_w", "ln_b", "fc2_w", "fc2_b"))
    token_rows = dram("token_rows", (N, D))
    slot_token = dram("slot_token", (NTAB * S, 1), I32)

    topv = mb("topv", [P, TOP, T])
    slot_i = mb("slot_i", [P, TOP * T], I32)
    tile_expert = mb("tile_expert", [1, NTAB], I32)
    last_tile = mb("last_tile", [1, 1], I32)

    with stage(nc) as (route, sem):
        def rb(name, shape, dt=F32):
            return sb(name, shape, dt, route)

        xf = rb("xf", [P, T, D])
        xfT = rb("xfT", [128, KD, N])
        gw = rb("gw", [128, KD, X])
        gbias = rb("gbias", [P, X])
        mv, stats = rb("r_mv", [P, T, 2]), rb("r_stats", [P, 2, 6])
        std, rstd = rb("r_std", [P, T]), rb("r_rstd", [P, T])
        pr = rb("pr", [P, T, X])
        m = rb("m", [P, T])
        eq = rb("eq", [P, T, X])
        chosen = rb("chosen", [P, TOP, T, X])
        sel = rb("sel", [P, T, X])
        pos = rb("pos", [P, T, X])
        total = rb("total", [P, X])
        tiles = rb("tiles", [P, X])
        more = rb("more", [P, X])
        ends = rb("tile_ends", [P, X])
        one_x = rb("one_x", [P, X])
        iota_x = rb("iota_x", [P, X])
        iota_j = rb("iota_j", [1, NTAB])
        at_or_past = rb("at_or_past", [1, NTAB, X])
        expert_f = rb("expert_f", [1, NTAB])
        slot_f = rb("slot_f", [P, TOP, T])
        token_id = rb("token_id", [P, T], I32)
        first_f = rb("first_f", [NTAB, S])
        row_is_shared = rb("row_is_shared", [NTAB, S])
        first_i = rb("first_i", [NTAB, S], I32)
        g_in, r_chain, r_var, r_std, xf_ok, x_out = (sem(s) for s in ("g_in", "r_chain", "r_var", "r_std_ok", "xf_ok", "x_out"))
        r_turned, xfT_ok, score_ok, sel_ok, pos_ok, exp_in, exp_out, r_const, r_pool = (
            sem(s) for s in ("r_turned", "xfT_ok", "score_ok", "sel_ok", "pos_ok", "exp_in", "exp_out", "r_const", "r_pool"))
        first_ok, first_out, slots_ok, slot_out_ok = (sem(s) for s in ("first_ok", "first_out", "slots_ok", "slot_out_ok"))
        with nc.Block() as block:
            @block.sync
            def _(sp):
                sp.dma_start(gw[:], gate_w.rearrange("(k p) e -> p k e", p=128)).then_inc(g_in, 16)
                sp.dma_start(gbias[:], gate_b.partition_broadcast(P)).then_inc(g_in, 16)
                sp.wait_ge(first_ok, 1)
                sp.dma_start(slot_token.rearrange("(j s) o -> j (s o)", s=S), first_i[:]).then_inc(first_out, 16)
                sp.wait_ge(xf_ok, T)
                sp.dma_start(token_rows.rearrange("(t p) d -> p t d", p=P), xf[:]).then_inc(x_out, 16)
                sp.wait_ge(x_out, 16)

            @block.gpsimd
            def _(pool):
                link = Chain(pool, r_pool)
                link(nc.gpsimd.iota(iota_x[:], pattern=[[1, X]], base=0, channel_multiplier=0,
                                    allow_small_or_imprecise_dtypes=True))
                link(nc.gpsimd.iota(iota_j[:], pattern=[[1, NTAB]], base=0, channel_multiplier=0,
                                    allow_small_or_imprecise_dtypes=True))
                link(nc.gpsimd.iota(token_id[:], pattern=[[P, T]], base=0, channel_multiplier=1))
                link(nc.gpsimd.iota(first_f[:], pattern=[[1, S]], base=0, channel_multiplier=S,
                                    allow_small_or_imprecise_dtypes=True))
                link(nc.gpsimd.memset(one_x[:], 1.0))
                nc.gpsimd.memset(row_is_shared[:], 1.0).then_inc(r_const, 1)
                pool.wait_ge(first_out, 16)
                pool.wait_ge(slots_ok, 1)
                for n in range(TOP * T):
                    if n:
                        pool.wait_ge(slot_out_ok, 16 * n)
                    nc.gpsimd.indirect_dma_start(
                        slot_token, bass.IndirectOffsetOnAxis(ap=slot_i[:, n:n + 1], axis=0),
                        token_id[:, n % T:n % T + 1], None).then_inc(slot_out_ok, 16)
                pool.wait_ge(slot_out_ok, 16 * TOP * T)

            @block.scalar
            def _(act):
                act.wait_ge(r_var, 1)
                nc.scalar.activation(std[:], mv[:, :, 1], ACT.Sqrt, bias=eps[0:P, :]).then_inc(r_std, 1)
                for n in range(2 * T):
                    t, h = divmod(n, 2)
                    act.wait_ge(r_turned, n + 1)
                    nc.scalar.copy(xfT[:, 3 * h:3 * h + 3, t * P:(t + 1) * P],
                                   bank[n % 4][:, 0:3 * P].rearrange("p (k n) -> p k n", k=3)).then_inc(xfT_ok, 1)
                act.wait_ge(exp_in, 1)
                nc.scalar.activation(pr[:], pr[:], ACT.Exp).then_inc(exp_out, 1)

            @block.tensor
            def _(pe):
                for n in range(2 * T):
                    t, h = divmod(n, 2)
                    pe.wait_ge(xf_ok, t + 1)
                    if n >= 4:
                        pe.wait_ge(xfT_ok, n - 3)
                    for u in range(3):
                        c = 3 * h + u
                        last = nc.tensor.transpose(bank[n % 4][:, u * P:(u + 1) * P],
                                                   xf[:, t, c * 128:(c + 1) * 128], ident[0:P, 0:P])
                    last.then_inc(r_turned, 1)
                pe.wait_ge(g_in, 32)
                for t in range(T):
                    pe.wait_ge(xfT_ok, 2 * t + 2)
                    for c in range(KD):
                        last = nc.tensor.matmul(bank[4][0:P, t * X:(t + 1) * X], xfT[:, c, t * P:(t + 1) * P],
                                                gw[:, c, :], start=(c == 0), stop=(c == KD - 1))
                last.then_inc(score_ok, 1)
                pe.wait_ge(sel_ok, 1)
                for t in range(T):
                    for c in range(t + 1):
                        last = nc.tensor.matmul(bank[5][0:P, t * X:(t + 1) * X], before[:] if c == t else ones[:],
                                                sel[:, c, :], start=(c == 0), stop=(c == t))
                for c in range(T):
                    last = nc.tensor.matmul(bank[6][0:P, 0:X], ones[:], sel[:, c, :], start=(c == 0), stop=(c == T - 1))
                last.then_inc(pos_ok, 1)

            @block.vector
            def _(dve):
                link = Chain(dve, r_chain)
                for t in range(T):
                    row_stats(nc, link, x_rows[:, t, :], D, stats, mv[:, t, :])
                nc.vector.tensor_copy(stats[:, 0, :], stats[:, 1, :]).then_inc(r_var, 1)
                dve.wait_ge(r_var, 1)
                dve.wait_ge(r_std, 1)
                link(nc.vector.reciprocal(rstd[:], std[:]))
                for t in range(T):
                    nc.vector.tensor_scalar(xf[:, t, :], x_rows[:, t, :], mv[:, t, 0:1], rstd[:, t:t + 1],
                                            ALU.subtract, ALU.mult).then_inc(xf_ok, 1)
                dve.wait_ge(r_const, 1)
                link(nc.vector.tensor_scalar(row_is_shared[:], first_f[:], float(SHARED * S), None, ALU.is_lt))
                link(nc.vector.tensor_scalar(first_f[:], first_f[:], float(N - 1), None, ALU.min))
                link(nc.vector.tensor_tensor(first_f[:], first_f[:], row_is_shared[:], ALU.mult))
                nc.vector.tensor_copy(first_i[:], first_f[:]).then_inc(first_ok, 1)
                dve.wait_ge(g_in, 32)
                dve.wait_ge(score_ok, 1)
                link(nc.vector.tensor_tensor(pr[:], bank[4][0:P, 0:T * X].rearrange("p (t e) -> p t e", t=T),
                                             gbias[:].unsqueeze(1).to_broadcast([P, T, X]), ALU.add))
                link(nc.vector.memset(pr[:, :, 0:1], -1e9))
                link(nc.vector.tensor_reduce(m[:], pr[:], AX.X, ALU.max))
                nc.vector.tensor_tensor(pr[:], pr[:], m[:].unsqueeze(2).to_broadcast([P, T, X]),
                                        ALU.subtract).then_inc(exp_in, 1)
                dve.wait_ge(exp_out, 1)
                link(nc.vector.tensor_reduce(m[:], pr[:], AX.X, ALU.add))
                link(nc.vector.reciprocal(m[:], m[:]))
                link(nc.vector.tensor_tensor(pr[:], pr[:], m[:].unsqueeze(2).to_broadcast([P, T, X]), ALU.mult))
                for c in range(TOP):
                    link(nc.vector.tensor_reduce(topv[:, c, :], pr[:], AX.X, ALU.max))
                    link(nc.vector.tensor_tensor(eq[:], pr[:], topv[:, c, :].unsqueeze(2).to_broadcast([P, T, X]),
                                                 ALU.is_lt))
                    link(nc.vector.tensor_scalar(eq[:], eq[:], float(X), None, ALU.mult))
                    link(nc.vector.tensor_tensor(eq[:], eq[:], iota_x[:].unsqueeze(1).to_broadcast([P, T, X]), ALU.add))
                    link(nc.vector.tensor_reduce(m[:], eq[:], AX.X, ALU.min))
                    link(nc.vector.tensor_tensor(chosen[:, c], iota_x[:].unsqueeze(1).to_broadcast([P, T, X]),
                                                 m[:].unsqueeze(2).to_broadcast([P, T, X]), ALU.is_equal))
                    link(nc.vector.scalar_tensor_tensor(out=pr[:], in0=chosen[:, c], scalar=-4.0, in1=pr[:],
                                                        op0=ALU.mult, op1=ALU.add))
                link(nc.vector.tensor_tensor(sel[:], chosen[:, 0], chosen[:, 1], ALU.add))
                nc.vector.tensor_tensor(sel[:], sel[:], chosen[:, 2], ALU.add).then_inc(sel_ok, 1)
                dve.wait_ge(pos_ok, 1)
                link(nc.vector.tensor_copy(total[:], bank[6][0:P, 0:X]))
                link(nc.vector.tensor_scalar(tiles[:], total[:], 0.0, None, ALU.is_gt))
                for c in range(1, SHARED):
                    link(nc.vector.tensor_scalar(more[:], total[:], float(c * S), None, ALU.is_gt))
                    link(nc.vector.tensor_tensor(tiles[:], tiles[:], more[:], ALU.add))
                link(nc.vector.tensor_tensor_scan(ends[:], one_x[:], tiles[:], float(SHARED), ALU.mult, ALU.add))
                link(nc.vector.tensor_tensor(more[:], ends[:], tiles[:], ALU.subtract))
                link(nc.vector.tensor_scalar(more[:], more[:], float(S), None, ALU.mult))
                link(nc.vector.tensor_tensor(pos[:], bank[5][0:P, 0:T * X].rearrange("p (t e) -> p t e", t=T),
                                             more[:].unsqueeze(1).to_broadcast([P, T, X]), ALU.add))
                for c in range(TOP):
                    link(nc.vector.tensor_tensor(eq[:], chosen[:, c], pos[:], ALU.mult))
                    link(nc.vector.tensor_reduce(slot_f[:, c, :], eq[:], AX.X, ALU.add))
                nc.vector.tensor_copy(slot_i[:], slot_f[:].rearrange("p c t -> p (c t)")).then_inc(slots_ok, 1)
                link(nc.vector.tensor_tensor(at_or_past[:], ends[0:1, :].unsqueeze(1).to_broadcast([1, NTAB, X]),
                                             iota_j[:].unsqueeze(2).to_broadcast([1, NTAB, X]), ALU.is_le))
                link(nc.vector.tensor_reduce(expert_f[:], at_or_past[:], AX.X, ALU.add))
                link(nc.vector.tensor_scalar(expert_f[:], expert_f[:], float(X - 1), None, ALU.min))
                link(nc.vector.tensor_copy(tile_expert[:], expert_f[:]))
                link(nc.vector.tensor_scalar(last_tile[:], ends[0:1, X - 1:X], -1.0, None, ALU.add))

    with stage(nc) as (ff, sem):
        def fb(name, shape, dt=F32):
            return sb(name, shape, dt, ff)

        w1 = fb("w1", [128, KF // 2, FF])
        w2 = fb("w2", [128, KF, D])
        xg = fb("xg", [S, D])
        slot_idx = fb("slot_idx", [S, 1], I32)
        xgT = fb("xgT", [128, KD, S])
        h = fb("h", [S, FF])
        hn = fb("hn", [S, FF])
        hT = fb("hT", [128, KF, S])
        y = fb("y", [S, D])
        row1 = fb("row1", [1, 3 * FF])
        row2 = fb("row2", [1, D])
        all1 = fb("all1", [S, 3 * FF])
        all2 = fb("all2", [S, D])
        mv, stats = fb("e_mv", [S, 2]), fb("e_stats", [S, 3, 6])
        std, rstd = fb("e_std", [S, 1]), fb("e_rstd", [S, 1])
        w1_in = [sem(f"w1_in{c}") for c in range(KD)]
        w2_in = [sem(f"w2_in{c}") for c in range(KD)]
        row1_in, row2_in, idx_in, xg_in, y_out, go = (sem(s) for s in ("row1_in", "row2_in", "idx_in", "xg_in", "y_out", "e_go"))
        w1_used, w2_used, x_turned, xgT_ok, h_ok, h_turned, hT_ok, y_ok = (
            sem(s) for s in ("w1_used", "w2_used", "x_turned", "xgT_ok", "h_ok", "h_turned", "hT_ok", "y_ok"))
        go_sp, go_dve, go_act = sem("go_sp"), sem("go_dve"), sem("go_act")
        all1_ok, all2_ok, biased, gelu_ok, stat_ok, aggr_ok, std_ok, rstd_ok, centred, hn_ok, y_sb = (
            sem(s) for s in ("all1_ok", "all2_ok", "biased", "gelu_ok", "stat_ok", "aggr_ok", "e_std_ok", "rstd_ok",
                             "centred", "hn_ok", "y_sb"))
        with nc.Block() as block:
            def final_tile(eng):
                return eng.value_load(last_tile[0:1, 0:1], min_val=MINT - 1, max_val=MAXT - 1)

            @block.sync
            def _(sp):
                def expert(j):
                    return sp.value_load(tile_expert[0:1, bass.ds(j, 1)], min_val=0, max_val=X - 1)

                def load_w1(j, e, again):
                    for c in range(KD):
                        if again:
                            sp.wait_ge(w1_used, (j - 1) * KD + c + 1)
                            sp.sem_inc(go_sp, 1)
                        sp.dma_start(w1[:, c, :], fc1_w[bass.ds(e, 1), c * 128:(c + 1) * 128, :]
                                     .rearrange("o p n -> (o p) n")).then_inc(w1_in[c], 16)
                    if again:
                        sp.wait_ge(all1_ok, j)
                        sp.sem_inc(go_sp, 1)
                    for c, v in enumerate((fc1_b, ln_w, ln_b)):
                        sp.dma_start(row1[:, c * FF:(c + 1) * FF], v[bass.ds(e, 1), :]).then_inc(row1_in, 16)

                def load_w2(j, e, again):
                    for c in range(KD):
                        if again:
                            sp.wait_ge(w2_used, (j - 1) * KD + c + 1)
                            sp.sem_inc(go_sp, 1)
                        sp.dma_start(w2[:, 2 * c:2 * c + 2, :], fc2_w[bass.ds(e, 1), c * 256:(c + 1) * 256, :]
                                     .rearrange("o (k p) n -> (o p) k n", p=128)).then_inc(w2_in[c], 16)
                    if again:
                        sp.wait_ge(all2_ok, j)
                        sp.sem_inc(go_sp, 1)
                    sp.dma_start(row2[:], fc2_b[bass.ds(e, 1), :]).then_inc(row2_in, 16)

                end = final_tile(sp)
                load_w1(0, expert(0), False)
                load_w2(0, expert(0), False)
                load_w1(1, expert(1), True)
                with sp.Fori(1, end + 1) as j:
                    load_w1(j + 1, expert(j + 1), True)
                    load_w2(j, expert(j), True)
                for c in range(KD):
                    sp.wait_ge(w1_in[c], (end + 2) * 16)
                sp.sem_inc(go_sp, 1)
                sp.wait_ge(row1_in, (end + 2) * 48)
                sp.sem_inc(go_sp, 1)

            @block.gpsimd
            def _(pool):
                def gather(j, again):
                    if again:
                        pool.wait_ge(x_turned, j)
                    nc.gpsimd.sem_inc(go, 1)
                    nc.gpsimd.dma_start(slot_idx[:], slot_token[bass.ds(j * S, S), :]).then_inc(idx_in, 16)
                    pool.wait_ge(idx_in, 16 * (j + 1))
                    nc.gpsimd.sem_inc(go, 1)
                    nc.gpsimd.indirect_dma_start(xg[:], None, token_rows,
                                                 bass.IndirectOffsetOnAxis(ap=slot_idx[:, 0:1], axis=0)).then_inc(xg_in, 16)

                def spread1(j, again):
                    if again:
                        pool.wait_ge(hn_ok, j)
                    pool.wait_ge(row1_in, 48 * (j + 1))
                    nc.gpsimd.sem_inc(go, 1)
                    nc.gpsimd.partition_broadcast(all1[:], row1[:]).then_inc(all1_ok, 1)

                def spread2(j, again):
                    if again:
                        pool.wait_ge(y_sb, 2 * j)
                    pool.wait_ge(row2_in, 16 * (j + 1))
                    nc.gpsimd.sem_inc(go, 1)
                    nc.gpsimd.partition_broadcast(all2[:], row2[:]).then_inc(all2_ok, 1)

                end = final_tile(pool)
                gather(0, False)
                spread1(0, False)
                spread2(0, False)
                gather(1, True)
                with pool.Fori(1, end + 1) as j:
                    spread1(j, True)
                    gather(j + 1, True)
                    spread2(j, True)
                pool.wait_ge(hn_ok, end + 1)
                pool.wait_ge(row1_in, 48 * (end + 2))
                nc.gpsimd.sem_inc(go, 1)
                nc.gpsimd.partition_broadcast(all1[:], row1[:]).then_inc(all1_ok, 1)
                pool.wait_ge(xg_in, 16 * (end + 2))

            @block.tensor
            def _(pe):
                def turn_tokens(j, again):
                    pe.wait_ge(xg_in, 16 * (j + 1))
                    for c in range(KD):
                        last = nc.tensor.transpose(bank[5 + c // 4][:, (c % 4) * S:(c % 4 + 1) * S],
                                                   xg[:, c * 128:(c + 1) * 128], ident[:])
                    last.then_inc(x_turned, 1)

                def first_product(j, slices, again):
                    for c in slices:
                        pe.wait_ge(w1_in[c], 16 * (j + 1))
                        if c == 0:
                            pe.wait_ge(xgT_ok, 2 * (j + 1))
                            if again:
                                pe.wait_ge(biased, 3 * j)
                        for b in range(3):
                            last = nc.tensor.matmul(bank[b][:], xgT[:, c, :], w1[:, c, b * 512:(b + 1) * 512],
                                                    start=(c == 0), stop=(c == KD - 1))
                        last.then_inc(w1_used, 1)

                def turn_hidden(j):
                    pe.wait_ge(hn_ok, j + 1)
                    pe.wait_ge(xgT_ok, 2 * (j + 2))
                    for b in range(3):
                        for u in range(4):
                            c = 4 * b + u
                            last = nc.tensor.transpose(bank[5 + b][:, u * S:(u + 1) * S],
                                                       hn[:, c * 128:(c + 1) * 128], ident[:])
                        last.then_inc(h_turned, 1)

                def second_product(j, slices, again):
                    for c in slices:
                        if c % 2 == 0:
                            pe.wait_ge(w2_in[c // 2], 16 * (j + 1))
                        if c % 4 == 0:
                            pe.wait_ge(hT_ok, 3 * j + c // 4 + 1)
                        if c == 0 and again:
                            pe.wait_ge(y_sb, 2 * j)
                        for b in range(2):
                            last = nc.tensor.matmul(bank[3 + b][:, 0:HALF], hT[:, c, :],
                                                    w2[:, c, b * HALF:(b + 1) * HALF],
                                                    start=(c == 0), stop=(c == KF - 1))
                        if c % 2:
                            last.then_inc(w2_used, 1)

                end = final_tile(pe)
                turn_tokens(0, False)
                first_product(0, range(KD), False)
                turn_tokens(1, True)

                def step(j, again):
                    first_product(j, range(0, 4), True)
                    turn_hidden(j - 1)
                    first_product(j, range(4, KD), True)
                    second_product(j - 1, range(0, 8), again)
                    pe.wait_ge(hT_ok, 3 * j)
                    turn_tokens(j + 1, True)
                    second_product(j - 1, range(8, KF), again)

                step(1, False)
                with pe.Fori(2, end + 1) as j:
                    step(j, True)
                turn_hidden(end)
                second_product(end, range(KF), True)

            @block.scalar
            def _(act):
                def copy_tokens(j):
                    act.wait_ge(x_turned, j + 1)
                    act.wait_ge(w1_used, j * KD)
                    nc.scalar.copy(xgT[:, 0:4, :].rearrange("p k s -> p (k s)"), bank[5][:]).then_inc(xgT_ok, 1)
                    nc.scalar.copy(xgT[:, 4:6, :].rearrange("p k s -> p (k s)"), bank[6][:, 0:2 * S]).then_inc(xgT_ok, 1)

                def hidden(j):
                    for b in range(3):
                        act.wait_ge(biased, 3 * j + b + 1)
                        nc.scalar.activation(h[:, b * 512:(b + 1) * 512], h[:, b * 512:(b + 1) * 512],
                                             ACT.Gelu).then_inc(gelu_ok, 1)
                    act.wait_ge(aggr_ok, j + 1)
                    nc.scalar.activation(std[:], mv[:, 1:2], ACT.Sqrt, bias=eps[:]).then_inc(std_ok, 1)

                def copy_hidden(j, again):
                    for b in range(3):
                        act.wait_ge(h_turned, 3 * j + b + 1)
                        if again:
                            act.wait_ge(w2_used, j * KD)
                        nc.scalar.copy(hT[:, 4 * b:4 * b + 4, :].rearrange("p k s -> p (k s)"),
                                       bank[5 + b][:]).then_inc(hT_ok, 1)

                def store(j):
                    act.wait_ge(y_sb, 2 * (j + 1))
                    act.dma_start(slot_out[bass.ds(j * S, S), :], y[:]).then_inc(y_out, 16)

                end = final_tile(act)
                copy_tokens(0)
                hidden(0)
                copy_tokens(1)

                def step(j, again):
                    copy_hidden(j - 1, again)
                    hidden(j)
                    copy_tokens(j + 1)
                    store(j - 1)

                step(1, False)
                with act.Fori(2, end + 1) as j:
                    step(j, True)
                copy_hidden(end, True)
                store(end)
                act.wait_ge(y_out, 16 * (end + 1))
                act.sem_inc(go_act, 1)

            @block.vector
            def _(dve):
                def hidden(j, again):
                    dve.wait_ge(all1_ok, j + 1)
                    dve.wait_ge(w1_used, KD * (j + 1))
                    if again:
                        dve.wait_ge(hn_ok, j)
                    for b in range(3):
                        nc.vector.tensor_tensor(h[:, b * 512:(b + 1) * 512], bank[b][:],
                                                all1[:, b * 512:(b + 1) * 512], ALU.add).then_inc(biased, 1)
                    for b in range(3):
                        dve.wait_ge(gelu_ok, 3 * j + b + 1)
                        nc.vector.bn_stats(stats[:, b, :], h[:, b * 512:(b + 1) * 512]).then_inc(stat_ok, 1)
                    if again:
                        dve.wait_ge(std_ok, j)
                    dve.wait_ge(stat_ok, 3 * (j + 1))
                    nc.vector.sem_inc(go_dve, 1)
                    nc.vector.bn_aggr(mv[:], stats[:].rearrange("p c s -> p (c s)")).then_inc(aggr_ok, 1)
                    dve.wait_ge(aggr_ok, j + 1)
                    nc.vector.scalar_tensor_tensor(out=h[:], in0=h[:], scalar=mv[:, 0:1], in1=all1[:, FF:2 * FF],
                                                   op0=ALU.subtract, op1=ALU.mult).then_inc(centred, 1)
                    dve.wait_ge(std_ok, j + 1)
                    nc.vector.reciprocal(rstd[:], std[:]).then_inc(rstd_ok, 1)
                    dve.wait_ge(rstd_ok, j + 1)
                    dve.wait_ge(centred, j + 1)
                    if again:
                        dve.wait_ge(h_turned, 3 * j)
                    nc.vector.scalar_tensor_tensor(out=hn[:], in0=h[:], scalar=rstd[:, 0:1], in1=all1[:, 2 * FF:3 * FF],
                                                   op0=ALU.mult, op1=ALU.add).then_inc(hn_ok, 1)

                def output(j, again):
                    dve.wait_ge(all2_ok, j + 1)
                    dve.wait_ge(w2_used, KD * (j + 1))
                    if again:
                        dve.wait_ge(y_out, 16 * j)
                    for b in range(2):
                        nc.vector.tensor_tensor(y[:, b * HALF:(b + 1) * HALF], bank[3 + b][:, 0:HALF],
                                                all2[:, b * HALF:(b + 1) * HALF], ALU.add).then_inc(y_sb, 1)

                end = final_tile(dve)
                hidden(0, False)
                hidden(1, True)
                output(0, False)
                with dve.Fori(2, end + 1) as j:
                    hidden(j, True)
                    output(j - 1, True)
                output(end, True)

    with stage(nc) as (last_stage, sem):
        gathered = sb("gathered", [P, TOP * T, D], F32, last_stage)
        shared = sb("shared", [P, T, D], F32, last_stage)
        slots_in = [sem(f"slots_in{t}") for t in range(T)]
        shared_in, f_chain, row_done, written = sem("shared_in"), sem("f_chain"), sem("row_done"), sem("written")
        with nc.Block() as block:
            @block.sync
            def _(sp):
                sp.dma_start(shared[:], slot_out[0:N, :].rearrange("(t p) d -> p t d", p=P)).then_inc(shared_in, 16)
                for t in range(T):
                    sp.wait_ge(row_done, t + 1)
                    sp.dma_start(out[t * P:(t + 1) * P, :], x_rows[:, t, :]).then_inc(written, 16)
                sp.wait_ge(written, 16 * T)

            @block.gpsimd
            def _(pool):
                for t in range(T):
                    for c in range(TOP):
                        n = c * T + t
                        nc.gpsimd.indirect_dma_start(gathered[:, n, :], None, slot_out,
                                                     bass.IndirectOffsetOnAxis(ap=slot_i[:, n:n + 1], axis=0)
                                                     ).then_inc(slots_in[t], 16)

            @block.vector
            def _(dve):
                link = Chain(dve, f_chain)
                dve.wait_ge(shared_in, 16)
                for t in range(T):
                    link(nc.vector.tensor_tensor(x_rows[:, t, :], x_rows[:, t, :], shared[:, t, :], ALU.add))
                    dve.wait_ge(slots_in[t], 16 * TOP)
                    for c in range(TOP):
                        last = nc.vector.scalar_tensor_tensor(out=x_rows[:, t, :], in0=gathered[:, c * T + t, :],
                                                              scalar=topv[:, c, t:t + 1], in1=x_rows[:, t, :],
                                                              op0=ALU.mult, op1=ALU.add)
                        if c < TOP - 1:
                            link(last)
                    last.then_inc(row_done, 1)


def kernel(**inputs):
    import numpy as _np
    import concourse.bacc as _bacc
    from concourse import mybir as _mybir
    from concourse.bass_utils import run_bass_kernel_spmd as _run

    nc = _bacc.Bacc("TRN2", target_bir_lowering=False, num_devices=1)
    arrays, args = {}, {}
    for name in inputs:
        v = _np.ascontiguousarray(inputs[name])
        arrays[f"in_{name}"] = v
        args[name] = nc.dram_tensor(f"in_{name}", v.shape, _mybir.dt.from_np(v.dtype), kind="ExternalInput").ap()
    out = nc.dram_tensor("out_0", (N, D), F32, kind="ExternalOutput").ap()
    gnn_moe(nc, args, out)
    r = _run(nc, [arrays], core_ids=[0])
    return r.results[0]["out_0"]
```

```python
import concourse.bass as bass
from concourse import mybir
from contextlib import ExitStack, contextmanager

F32 = mybir.dt.float32
F16 = mybir.dt.float16
F32R = mybir.dt.float32r
I32 = mybir.dt.int32
ALU = mybir.AluOpType
ACT = mybir.ActivationFunctionType
AX = mybir.AxisListType

N, D, E_GNN = 625, 768, 20000
P, T = 125, 5
ET = E_GNN // P
HALF_ET = ET // 2
NI = -(-ET * T // 128) * 128
ITEM_TRASH = NI
KD = D // 128
HALF = D // 2
SLOPE, EPS = 0.2, 1e-5
ABSENT = -1e30
TRASH = N * N
G = 8
LAG = 5
REST = N - 512

X, FF = 16, 1536
TOP = 3
KF = FF // 128
S = 128
SHARED = (N + S - 1) // S
MAXT = SHARED + (N * TOP + X * (S - 1)) // S
MINT = SHARED + (N * TOP + S - 1) // S
NTAB = MAXT + 1


@contextmanager
def stage(nc):
    used = []

    def sem(name):
        used.append(nc.alloc_semaphore(name))
        return used[-1]

    with ExitStack() as memory:
        yield memory, sem
        nc.clear_and_free_semaphores(used)
        nc.all_engine_barrier()


class Chain:

    def __init__(self, engine, sem):
        self.engine, self.sem, self.n = engine, sem, 0

    def __call__(self, ins):
        self.n += 1
        ins.then_inc(self.sem, 1)
        self.engine.wait_ge(self.sem, self.n)


def gnn_moe(nc, a, out):
    top = ExitStack()
    with top:
        def sb(name, shape, dt=F32, ctx=top):
            return ctx.enter_context(nc.sbuf_tensor(name, shape, dt))

        def dram(name, shape, dt=F32):
            return nc.dram_tensor(name, shape, dt, kind="Internal").ap()

        psum = top.enter_context(nc.psum_tensor("psum", [128, 8 * 512], F32))
        bank = [psum[:, i * 512:(i + 1) * 512] for i in range(8)]
        x_rows = sb("x_rows", [P, T, D])
        ident = sb("ident", [128, 128])
        eps = sb("eps", [128, 1])
        before = sb("before", [P, P])
        ones = sb("ones", [P, P])
        slot_out = dram("slot_out", (NTAB * S, D))
        gnn = ExitStack()
        with gnn:
            graph_layers(nc, a, gnn, sb, dram, psum, bank, x_rows, ident, eps, before, ones, slot_out)
        moe = ExitStack()
        with moe:
            mixture(nc, a, out, moe, sb, dram, bank, x_rows, ident, eps, before, ones, slot_out)


def row_stats(nc, chain, src, width, stats, mv):
    parts = width // (384 if width == D else 512)
    step = width // parts
    for c in range(parts):
        last = nc.vector.bn_stats(stats[:, c, :], src[:, c * step:(c + 1) * step])
        if c < parts - 1:
            last.then_inc(chain.sem, 1)
            chain.n += 1
    chain(last)
    chain(nc.vector.bn_aggr(mv, stats[:, 0:parts, :].rearrange("p c s -> p (c s)")))


def graph_layers(nc, a, gnn, sb, dram, psum, bank, x_rows, ident, eps, before, ones, slot_out):
    def gb(name, shape, dt=F32):
        return sb(name, shape, dt, gnn)

    fs = gb("fs", [P, T, D])
    counts = gb("counts", [P, T, N])
    item_idx = gb("item_idx", [P, NI, 2], I32)
    item_key = gb("item_key", [P, NI])
    item_dst = gb("item_dst", [P, NI])
    tile_words = gb("tile_words", [1, NI // G], I32)
    octets = gb("octets", [1, 1], I32)
    part_iota = gb("part_iota", [P, 1])
    vecs = gb("vecs", [P, 5, D])
    attn_s = gb("attn_s", [P, 2, D])
    mv = gb("mv", [P, T, 2])
    stats = gb("stats", [P, 2, 6])
    std = gb("std", [P, T])
    rstd = gb("rstd", [P, T])
    key_col = gb("key_col", [P, G])

    def inputs(k):
        p = ("W1s", "W1d", "b1s", "b1d", "attn1", "ln1_w", "ln1_b") if k == 0 else \
            ("Wos", "Wod", "bos", "bod", "attno", "lno_w", "lno_b")
        return [a["L0_gnn_" + n] for n in p]

    heads = (8, 1)
    width = [D + max(h, 2) for h in heads]
    fd_hi = gb("fd_hi", [P, T, width[0]], F32R)
    fd_lo = gb("fd_lo", [P, T, width[0]], F32R)
    logit_tabs = [[dram(f"logit_tab{k}{u}", (N * N + P, heads[k])) for u in range(2)] for k in range(2)]
    fs_tab = [dram(f"fs_tab{k}", (N, width[k])) for k in range(2)]
    item_tab = dram("item_tab", (NI + HALF_ET, 3), I32)

    def node_tiles(pe, g):
        word = pe.value_load(tile_words[0:1, bass.ds(g, 1)], min_val=0, max_val=(T - 1) * (8 ** G - 1) // 7)
        return [((word >> (3 * u)) & 7).with_bounds(min_val=0, max_val=T - 1) for u in range(G)]

    with stage(nc) as (prep, sem):
        x_in_rows = sb("x_in_rows", [P, T, D], F32, prep)
        absent = sb("absent", [128, 6 * D], F32, prep)
        dst_i = sb("dst_i", [HALF_ET, 2, P], I32, prep)
        dst_f = sb("dst_f", [HALF_ET, 2, P], F32, prep)
        dst_tile = sb("dst_tile", [HALF_ET, 2, P], F32, prep)
        same = sb("same", [HALF_ET, 2, P], F32, prep)
        has = sb("has", [HALF_ET, T, 2], F32, prep)
        total = sb("i_total", [HALF_ET, 2 * T], F32, prep)
        until = sb("until", [HALF_ET, 2 * T], F32, prep)
        one_row = sb("one_row", [HALF_ET, 2 * T], F32, prep)
        row_trash = sb("row_trash", [HALF_ET, 1], F32, prep)
        at_f = sb("at_f", [HALF_ET, 2 * T], F32, prep)
        at_i = sb("at_i", [HALF_ET, 2 * T], I32, prep)
        triples = sb("triples", [HALF_ET, 2 * T, 3], I32, prep)
        no_item = sb("no_item", [128, NI // 128, 3], I32, prep)
        blocks_i = sb("blocks_i", [1, 2], I32, prep)
        items_f = sb("items_f", [1, 2], F32, prep)
        item_tile = sb("item_tile", [1, NI], F32, prep)
        words_f = sb("words_f", [1, NI // G], F32, prep)
        triple = sb("triple", [128, 3], I32, prep)
        triple_f = sb("triple_f", [128, 3], F32, prep)
        edge_trash = sb("edge_trash", [128, P], F32, prep)
        rows_i = sb("rows_i", [128, 2, P], I32, prep)
        rows_f = sb("rows_f", [128, 2, P], F32, prep)
        key = sb("key", [128, P], F32, prep)
        local = sb("local", [128, P], F32, prep)
        inside = sb("inside", [128, P], F32, prep)
        BLOCK_STEPS = 9
        go_dve = sem("p_go_dve")
        (x_in, dst_in, const_ok, absent_ok, tab_set, prep_chain, prep_act, var_ok, pool_chain, has_ok, ranked,
         at_ok, no_item_in, listed, count_ok, go, triple_in, rows_in, cols_ok, turned, taken) = (
            sem(s) for s in ("x_in", "dst_in", "const_ok", "absent_ok", "tab_set", "prep_chain", "prep_act",
                             "var_ok", "pool_chain", "has_ok", "ranked", "at_ok", "no_item_in", "listed",
                             "count_ok", "p_go", "triple_in", "rows_in", "i_cols_ok", "i_turned", "taken"))
        with nc.Block() as block:
            @block.sync
            def _(sp):
                for h in range(2):
                    sp.dma_start(dst_i[:, h, :], a["dst"][h * HALF_ET * P:(h + 1) * HALF_ET * P]
                                 .rearrange("(q p) -> q p", p=P)).then_inc(dst_in, 16)
                sp.dma_start(x_in_rows[:], a["x"].rearrange("(t p) d -> p t d", p=P)).then_inc(x_in, 16)
                sp.wait_ge(absent_ok, 1)
                row = MINT * S
                blocks = 0
                while row < NTAB * S:
                    per = min(6, (NTAB * S - row) // 128)
                    sp.dma_start(slot_out[row:row + 128 * per, :].rearrange("(p r) d -> p (r d)", p=128),
                                 absent[:, 0:per * D]).then_inc(tab_set, 16)
                    row += 128 * per
                    blocks += 1
                sp.wait_ge(tab_set, 16 * blocks)

            @block.gpsimd
            def _(pool):
                link = Chain(pool, pool_chain)
                link(nc.gpsimd.memset(ones[:], 1.0))
                link(nc.gpsimd.affine_select(out=before[:], in_=ones[:], compare_op=ALU.is_gt, fill=0.0,
                                             base=0, pattern=[[1, P]], channel_multiplier=-1))
                link(nc.gpsimd.memset(no_item[:], 0))
                link(nc.gpsimd.memset(no_item[:, :, 2:3], T))
                link(nc.gpsimd.iota(triples[:, :, 0], pattern=[[0, T], [HALF_ET, 2]], base=0, channel_multiplier=1))
                link(nc.gpsimd.iota(triples[:, :, 1], pattern=[[1, T], [0, 2]], base=0, channel_multiplier=0))
                link(nc.gpsimd.iota(triples[:, :, 2], pattern=[[1, T], [0, 2]], base=0, channel_multiplier=0))
                link(nc.gpsimd.iota(row_trash[:], pattern=[[0, 1]], base=ITEM_TRASH, channel_multiplier=1,
                                    allow_small_or_imprecise_dtypes=True))
                link(nc.gpsimd.iota(edge_trash[:], pattern=[[1, P]], base=TRASH, channel_multiplier=0,
                                    allow_small_or_imprecise_dtypes=True))
                link(nc.gpsimd.iota(part_iota[:], pattern=[[0, 1]], base=0, channel_multiplier=1,
                                    allow_small_or_imprecise_dtypes=True))
                link(nc.gpsimd.memset(one_row[:], 1.0))
                link(nc.gpsimd.memset(item_idx[:], 0))
                link(nc.gpsimd.memset(item_key[:], 0.0))
                link(nc.gpsimd.memset(item_tile[:], 0.0))
                link(nc.gpsimd.memset(eps[:], EPS))
                link(nc.gpsimd.memset(ident[:], 0.0))
                nc.gpsimd.affine_select(out=ident[:], in_=ident[:], compare_op=ALU.not_equal, fill=1.0,
                                        base=0, pattern=[[-1, 128]], channel_multiplier=1).then_inc(const_ok, 1)
                nc.gpsimd.memset(absent[:], ABSENT).then_inc(absent_ok, 1)
                pool.wait_ge(no_item_in, 16)
                pool.wait_ge(at_ok, 1)
                for n in range(2 * T):
                    if n:
                        pool.wait_ge(listed, 16 * n)
                    nc.gpsimd.indirect_dma_start(
                        item_tab, bass.IndirectOffsetOnAxis(ap=at_i[:, n:n + 1], axis=0),
                        triples[:, n, :], None).then_inc(listed, 16)
                pool.wait_ge(listed, 16 * 2 * T)
                blocks = pool.value_load(blocks_i[0:1, 0:1], min_val=ET // 128, max_val=NI // 128)
                with pool.Fori(0, blocks) as m:
                    pool.wait_ge(taken, 3 * m)
                    pool.sem_inc(go, 1)
                    nc.gpsimd.dma_start(triple[:], item_tab[bass.ds(m * 128, 128), :]).then_inc(triple_in, 16)
                    pool.wait_ge(triple_in, 16 * (m + 1))
                    pool.sem_inc(go, 1)
                    for c, name in enumerate(("src", "dst")):
                        nc.gpsimd.indirect_dma_start(
                            rows_i[:, c, :], None, a[name].rearrange("(n p) -> n p", p=P),
                            bass.IndirectOffsetOnAxis(ap=triple[:, 0:1], axis=0)).then_inc(rows_in, 16)

            @block.scalar
            def _(act):
                act.wait_ge(const_ok, 1)
                act.dma_start(item_tab[0:NI, :].rearrange("(g p) c -> p g c", p=128), no_item[:]).then_inc(no_item_in, 16)
                act.wait_ge(var_ok, 1)
                nc.scalar.activation(std[:], mv[:, :, 1], ACT.Sqrt, bias=eps[0:P, :]).then_inc(prep_act, 1)

            @block.tensor
            def _(pe):
                pe.wait_ge(const_ok, 1)
                pe.wait_ge(has_ok, 1)
                cols = has[:].rearrange("q t h -> q (t h)")
                nc.tensor.matmul(bank[0][0:HALF_ET, 0:2 * T], before[0:HALF_ET, 0:HALF_ET], cols, start=True, stop=True)
                nc.tensor.matmul(bank[1][0:HALF_ET, 0:2 * T], ones[0:HALF_ET, 0:HALF_ET], cols,
                                 start=True, stop=True).then_inc(ranked, 1)
                pe.wait_ge(count_ok, 1)
                blocks = pe.value_load(blocks_i[0:1, 0:1], min_val=ET // 128, max_val=NI // 128)
                with pe.Fori(0, blocks) as m:
                    pe.wait_ge(cols_ok, m + 1)
                    for c, rows in enumerate((rows_f[:, 0, :], key[:], local[:])):
                        nc.tensor.transpose(bank[2 + c][0:P, 0:128], rows, ident[:])
                    nc.tensor.transpose(bank[5][0:1, 0:128], triple_f[:, 1:2], ident[:]).then_inc(turned, 1)

            @block.vector
            def _(dve):
                link = Chain(dve, prep_chain)
                dve.wait_ge(dst_in, 32)
                link(nc.vector.tensor_copy(dst_f[:], dst_i[:]))
                link(nc.vector.tensor_scalar(dst_tile[:], dst_f[:], float(P), None, ALU.is_ge))
                for t in range(2, T):
                    link(nc.vector.scalar_tensor_tensor(out=dst_tile[:], in0=dst_f[:], scalar=float(t * P),
                                                        in1=dst_tile[:], op0=ALU.is_ge, op1=ALU.add))
                for t in range(T):
                    link(nc.vector.tensor_scalar(same[:], dst_tile[:], float(t), None, ALU.is_equal))
                    link(nc.vector.tensor_reduce(has[:, t, :], same[:], AX.X, ALU.max))
                nc.vector.tensor_copy(total[:], has[:].rearrange("q t h -> q (t h)")).then_inc(has_ok, 1)
                dve.wait_ge(has_ok, 1)
                dve.wait_ge(const_ok, 1)
                dve.wait_ge(ranked, 1)
                link(nc.vector.tensor_copy(total[:], bank[1][0:HALF_ET, 0:2 * T]))
                link(nc.vector.tensor_tensor_scan(until[:], one_row[:], total[:], 0.0, ALU.mult, ALU.add))
                link(nc.vector.tensor_scalar(items_f[:, 0:1], until[0:1, 2 * T - 1:2 * T], 127.0, None, ALU.add))
                link(nc.vector.tensor_scalar(items_f[:, 1:2], until[0:1, 2 * T - 1:2 * T], 7.0 - 2 * G, None, ALU.add))
                link(nc.vector.tensor_copy(blocks_i[:], items_f[:]))
                link(nc.vector.tensor_scalar(octets[:], blocks_i[:, 1:2], 3, None, ALU.arith_shift_right))
                link(nc.vector.tensor_scalar(blocks_i[:, 0:1], blocks_i[:, 0:1], 7, None, ALU.arith_shift_right))
                link(nc.vector.tensor_tensor(at_f[:], until[:], total[:], ALU.subtract))
                link(nc.vector.tensor_tensor(at_f[:], at_f[:], bank[0][0:HALF_ET, 0:2 * T], ALU.add))
                link(nc.vector.tensor_scalar(at_f[:], at_f[:], row_trash[:, 0:1], None, ALU.subtract))
                link(nc.vector.tensor_tensor(at_f[:], at_f[:], has[:].rearrange("q t h -> q (t h)"), ALU.mult))
                link(nc.vector.tensor_scalar(at_f[:], at_f[:], row_trash[:, 0:1], None, ALU.add))
                nc.vector.tensor_copy(at_i[:], at_f[:]).then_inc(at_ok, 1)
                nc.vector.memset(item_dst[:], -1.0).then_inc(count_ok, 1)
                dve.wait_ge(x_in, 16)
                for t in range(T):
                    row_stats(nc, link, x_in_rows[:, t, :], D, stats, mv[:, t, :])
                nc.vector.tensor_copy(stats[:, 0, :], stats[:, 1, :]).then_inc(var_ok, 1)
                dve.wait_ge(var_ok, 1)
                dve.wait_ge(prep_act, 1)
                link(nc.vector.reciprocal(rstd[:], std[:]))
                for t in range(T):
                    link(nc.vector.tensor_scalar(x_rows[:, t, :], x_in_rows[:, t, :], mv[:, t, 0:1],
                                                 rstd[:, t:t + 1], ALU.subtract, ALU.mult))
                blocks = dve.value_load(blocks_i[0:1, 0:1], min_val=ET // 128, max_val=NI // 128)
                with dve.Fori(0, blocks) as m:
                    step = iter(range(100))

                    def then(ins):
                        n = next(step)
                        ins.then_inc(go_dve, 1)
                        dve.wait_ge(go_dve, m * BLOCK_STEPS + n + 1)

                    dve.wait_ge(rows_in, 32 * (m + 1))
                    then(nc.vector.tensor_copy(rows_f[:], rows_i[:]))
                    then(nc.vector.tensor_copy(triple_f[:], triple[:]))
                    then(nc.vector.scalar_tensor_tensor(out=key[:], in0=rows_f[:, 1, :], scalar=float(N),
                                                        in1=rows_f[:, 0, :], op0=ALU.mult, op1=ALU.add))
                    then(nc.vector.tensor_scalar(triple_f[:, 2:3], triple_f[:, 2:3], float(P), None, ALU.mult))
                    then(nc.vector.tensor_scalar(local[:], rows_f[:, 1, :], triple_f[:, 2:3], None, ALU.subtract))
                    then(nc.vector.tensor_scalar(inside[:], local[:], float(P), None, ALU.is_lt))
                    then(nc.vector.scalar_tensor_tensor(out=inside[:], in0=local[:], scalar=0.0, in1=inside[:],
                                                        op0=ALU.is_ge, op1=ALU.mult))
                    then(nc.vector.tensor_tensor(key[:], key[:], edge_trash[:], ALU.subtract))
                    then(nc.vector.tensor_tensor(key[:], key[:], inside[:], ALU.mult))
                    nc.vector.tensor_tensor(key[:], key[:], edge_trash[:], ALU.add).then_inc(cols_ok, 1)
                    dve.wait_ge(turned, m + 1)
                    nc.vector.tensor_copy(item_idx[:, bass.ds(m * 128, 128), 0], bank[2][0:P, 0:128]).then_inc(taken, 1)
                    nc.vector.tensor_copy(item_key[:, bass.ds(m * 128, 128)], bank[3][0:P, 0:128])
                    nc.vector.tensor_copy(item_dst[:, bass.ds(m * 128, 128)], bank[4][0:P, 0:128]).then_inc(taken, 1)
                    nc.vector.tensor_copy(item_tile[:, bass.ds(m * 128, 128)], bank[5][0:1, 0:128]).then_inc(taken, 1)
                dve.wait_ge(taken, 3 * blocks)
                tiles_of = item_tile[:].rearrange("o (g u) -> o g u", u=G)
                link(nc.vector.tensor_copy(words_f[:], tiles_of[:, :, 0]))
                for u in range(1, G):
                    link(nc.vector.scalar_tensor_tensor(out=words_f[:], in0=tiles_of[:, :, u], scalar=float(8 ** u),
                                                        in1=words_f[:], op0=ALU.mult, op1=ALU.add))
                link(nc.vector.tensor_copy(tile_words[:], words_f[:]))

    with stage(nc) as (tally, sem):
        junk = sb("junk", [P, G, P], F32, tally)
        later = sb("later", [P, P], F32, tally)
        src_iota = sb("src_iota", [P, N], F16, tally)
        item_src = sb("item_src", [P, NI], F32, tally)
        repeats = sb("repeats", [P, NI], F32, tally)
        trash = sb("trash", [P, 1], F32, tally)
        hot = sb("hot", [P, G, N + P], F16, tally)
        zeros = sb("zeros", [P, 512], F16, tally)
        absent = sb("all_absent", [P, N * 8], F32, tally)
        absent_ok, tab_set = sem("t_absent_ok"), sem("t_tab_set")
        (t_const, t_pool, t_chain, cols_ok, keys_turned, keys_read, hot_ok, counted, cleared) = (
            sem(s) for s in ("t_const", "t_pool", "t_chain", "cols_ok", "keys_turned", "keys_read", "hot_ok",
                             "counted", "cleared"))
        with nc.Block() as block:
            @block.sync
            def _(sp):
                sp.wait_ge(absent_ok, 1)
                for u in range(2):
                    tab0 = logit_tabs[0][u][0:N * N, :].rearrange("(t p s) h -> t p (s h)", t=T, p=P)
                    for t in range(T):
                        sp.dma_start(tab0[t], absent[0:P, :]).then_inc(tab_set, 16)
                    sp.dma_start(logit_tabs[1][u][0:N * N, :].rearrange("(p s) h -> p (s h)", p=P),
                                 absent[0:P, 0:N * T]).then_inc(tab_set, 16)
                sp.wait_ge(tab_set, 16 * 2 * (T + 1))

            @block.gpsimd
            def _(pool):
                link = Chain(pool, t_pool)
                link(nc.gpsimd.affine_select(out=later[:], in_=ones[:], compare_op=ALU.is_gt, fill=0.0,
                                             base=0, pattern=[[-1, P]], channel_multiplier=1))
                link(nc.gpsimd.iota(trash[:], pattern=[[0, 1]], base=TRASH, channel_multiplier=1,
                                    allow_small_or_imprecise_dtypes=True))
                link(nc.gpsimd.memset(zeros[:], 0.0))
                nc.gpsimd.iota(src_iota[:], pattern=[[1, N]], base=0, channel_multiplier=0,
                               allow_small_or_imprecise_dtypes=True).then_inc(t_const, 1)
                nc.gpsimd.memset(absent[:], ABSENT).then_inc(absent_ok, 1)

            @block.tensor
            def _(pe):
                pe.wait_ge(t_const, 1)
                for b in range(7):
                    last = nc.tensor.matmul(psum[0:P, b * 512:(b + 1) * 512], zeros[:, 0:P], zeros[:],
                                            start=True, stop=False, skip_group_check=True)
                n8 = pe.value_load(octets[0:1, 0:1], min_val=ET // G - 2, max_val=NI // G - 2) + 2
                with pe.Fori(0, n8) as g:
                    tiles = node_tiles(pe, g)
                    for h in range(2):
                        if h == 0:
                            pe.wait_ge(cols_ok, g + 1)
                        pe.wait_ge(keys_read, g * G + 4 * h)
                        for u in range(4):
                            last = nc.tensor.transpose(bank[7][0:P, u * P:(u + 1) * P],
                                                       key_col[:, 4 * h + u:4 * h + u + 1].to_broadcast([P, P]),
                                                       ident[0:P, 0:P])
                        last.then_inc(keys_turned, 1)
                        for u in range(4):
                            n = g * G + 4 * h + u
                            t = tiles[4 * h + u]
                            pe.wait_ge(hot_ok, 2 * (n + 1))
                            nc.tensor.matmul(psum[0:P, bass.ds(t * 512, 512)], hot[:, 4 * h + u, N:N + P],
                                             hot[:, 4 * h + u, 0:512], start=False, stop=False, skip_group_check=True)
                            nc.tensor.matmul(psum[0:P, bass.ds(t * 128 + 5 * 512, REST)], hot[:, 4 * h + u, N:N + P],
                                             hot[:, 4 * h + u, 512:N], start=False, stop=False,
                                             skip_group_check=True).then_inc(counted, 1)

            @block.vector
            def _(dve):
                link = Chain(dve, t_chain)
                dve.wait_ge(t_const, 1)
                link(nc.vector.tensor_copy(item_src[:], item_idx[:, :, 0]))
                link(nc.vector.memset(repeats[:], 0.0))
                n8 = dve.value_load(octets[0:1, 0:1], min_val=ET // G - 2, max_val=NI // G - 2) + 2

                def column(g):
                    nc.vector.tensor_copy(key_col[:], item_key[:, bass.ds(g * G, G)]).then_inc(cols_ok, 1)

                def one_hots(g, h, again):
                    if again:
                        dve.wait_ge(counted, (g - 1) * G + 4 * h + 4)
                    for u in range(4):
                        n = g * G + 4 * h + u
                        nc.vector.tensor_scalar(hot[:, 4 * h + u, 0:N], src_iota[:], item_src[:, bass.ds(n, 1)],
                                                None, ALU.is_equal).then_inc(hot_ok, 1)
                        nc.vector.tensor_scalar(hot[:, 4 * h + u, N:N + P], src_iota[:, 0:P],
                                                item_dst[:, bass.ds(n, 1)], None, ALU.is_equal).then_inc(hot_ok, 1)

                def find_repeats(g, h):
                    for u in range(4):
                        n = g * G + 4 * h + u
                        nc.vector.scalar_tensor_tensor(
                            out=junk[:, 4 * h + u, :], in0=bank[7][0:P, u * P:(u + 1) * P],
                            scalar=item_key[:, bass.ds(n, 1)], in1=later[:], op0=ALU.is_equal,
                            op1=ALU.mult, accum_out=repeats[:, bass.ds(n, 1)]).then_inc(keys_read, 1)

                def octet(g, again, final):
                    one_hots(g, 1, again)
                    dve.wait_ge(keys_turned, 2 * g + 1)
                    if again:
                        dve.wait_ge(keys_read, g * G)
                    find_repeats(g, 0)
                    if not final:
                        one_hots(g + 1, 0, True)
                    dve.wait_ge(keys_turned, 2 * g + 2)
                    if not final:
                        column(g + 1)
                    find_repeats(g, 1)

                column(0)
                one_hots(0, 0, False)
                octet(0, False, False)
                with dve.Fori(1, n8 - 1) as g:
                    octet(g, True, False)
                octet(n8 - 1, True, True)
                dve.wait_ge(keys_read, n8 * G)
                link(nc.vector.tensor_scalar(repeats[:], repeats[:], 1.0, None, ALU.min))
                link(nc.vector.tensor_scalar(item_src[:], item_key[:], -1.0, trash[:, 0:1], ALU.mult, ALU.add))
                link(nc.vector.tensor_tensor(item_src[:], item_src[:], repeats[:], ALU.mult))
                link(nc.vector.tensor_tensor(item_src[:], item_src[:], item_key[:], ALU.add))
                link(nc.vector.tensor_copy(item_idx[:, :, 1], item_src[:]))
                dve.wait_ge(counted, n8 * G)
                for t in range(T):
                    link(nc.vector.tensor_copy(counts[:, t, 0:512], psum[0:P, t * 512:(t + 1) * 512]))
                    link(nc.vector.tensor_copy(counts[:, t, 512:N],
                                               psum[0:P, 5 * 512 + t * 128:5 * 512 + t * 128 + REST]))

    for k in range(2):
        H = heads[k]
        HD = D // H
        W = width[k]
        Ws, Wd, bs, bd, attn, ln_w, ln_b = inputs(k)

        with stage(nc) as (project, sem):
            weights = sb(f"weights{k}", [128, 2, KD, D], F32, project)
            xT = sb(f"xT{k}", [128, KD, N], F32, project)
            table_rows = sb(f"table_rows{k}", [P, 2, 2, W], F32, project)
            prod = sb(f"prod{k}", [P, D], F32, project)
            w_in = [sem(f"w_in{k}{c}") for c in range(2)]
            vec_in, turned, xT_ok = sem(f"vec_in{k}"), sem(f"turned{k}"), sem(f"xT_ok{k}")
            proj_ok, proj_read = sem(f"proj_ok{k}"), sem(f"proj_read{k}")
            tab_row_ok, tab_out, pchain = sem(f"tab_row_ok{k}"), [sem(f"tab_out{k}{u}") for u in range(2)], sem(f"pchain{k}")
            with nc.Block() as block:
                @block.sync
                def _(sp):
                    for c, w in enumerate((Ws, Wd)):
                        sp.dma_start(weights[:, c], w.rearrange("(k p) n -> p k n", p=128)).then_inc(w_in[c], 16)
                    for t in range(T):
                        sp.wait_ge(tab_row_ok, 2 * t + 1)
                        sp.dma_start(fs_tab[k][t * P:(t + 1) * P, :], table_rows[:, t % 2, 0, :]).then_inc(tab_out[t % 2], 16)
                    for u in range(2):
                        sp.wait_ge(tab_out[u], 16 * len(range(u, T, 2)))

                @block.scalar
                def _(act):
                    for c, v in enumerate((bs, bd, attn, ln_w, ln_b)):
                        flat = v if len(v.shape) == 1 else v.rearrange("h d -> (h d)")
                        act.dma_start(vecs[:, c, :], flat.partition_broadcast(P)).then_inc(vec_in, 16)
                    for n in range(2 * T):
                        act.wait_ge(turned, n + 1)
                        t, h = divmod(n, 2)
                        nc.scalar.copy(xT[:, 3 * h:3 * h + 3, t * P:(t + 1) * P],
                                       bank[4 + n % 4][:, 0:3 * P].rearrange("p (k n) -> p k n", k=3)).then_inc(xT_ok, 1)

                @block.tensor
                def _(pe):
                    for n in range(2 * T):
                        t, h = divmod(n, 2)
                        if n >= 4:
                            pe.wait_ge(xT_ok, n - 3)
                        for u in range(3):
                            c = 3 * h + u
                            last = nc.tensor.transpose(bank[4 + n % 4][:, u * P:(u + 1) * P],
                                                       x_rows[:, t, c * 128:(c + 1) * 128], ident[0:P, 0:P])
                        last.then_inc(turned, 1)
                    for n in range(2 * T):
                        t, c = divmod(n, 2)
                        pe.wait_ge(xT_ok, 2 * t + 2)
                        pe.wait_ge(w_in[c], 16)
                        if n >= 2:
                            pe.wait_ge(proj_read, n - 1)
                        for h in range(2):
                            for kk in range(KD):
                                last = nc.tensor.matmul(bank[2 * (n % 2) + h][0:P, 0:HALF],
                                                        xT[:, kk, t * P:(t + 1) * P],
                                                        weights[:, c, kk, h * HALF:(h + 1) * HALF],
                                                        start=(kk == 0), stop=(kk == KD - 1))
                        last.then_inc(proj_ok, 1)

                @block.vector
                def _(dve):
                    link = Chain(dve, pchain)
                    dve.wait_ge(vec_in, 16 * 5)
                    link(nc.vector.tensor_scalar(attn_s[:, 0, :], vecs[:, 2, :], SLOPE, None, ALU.mult))
                    link(nc.vector.tensor_scalar(attn_s[:, 1, :], vecs[:, 2, :], 1.0 - SLOPE, None, ALU.mult))
                    if H == 1:
                        link(nc.vector.memset(table_rows[:, :, :, D:W], 0.0))
                    for n in range(2 * T):
                        t, c = divmod(n, 2)
                        dve.wait_ge(proj_ok, n + 1)
                        if t >= 2 and c == 0:
                            dve.wait_ge(tab_out[t % 2], 16 * (t // 2))
                        for h in range(2):
                            last = nc.vector.tensor_tensor(table_rows[:, t % 2, c, h * HALF:(h + 1) * HALF],
                                                           bank[2 * (n % 2) + h][0:P, 0:HALF],
                                                           vecs[:, c, h * HALF:(h + 1) * HALF], ALU.add)
                            if h == 0:
                                link(last)
                        last.then_inc(proj_read, 1)
                        dve.wait_ge(proj_read, n + 1)
                        row = table_rows[:, t % 2, c, 0:D]
                        if c == 0:
                            link(nc.vector.tensor_copy(fs[:, t, :], row))
                        link(nc.vector.tensor_tensor(prod[:], row, attn_s[:, 0, :], ALU.mult))
                        nc.vector.tensor_reduce(table_rows[:, t % 2, c, D:D + H],
                                                prod[:].rearrange("p (h d) -> p h d", h=H),
                                                AX.X, ALU.add).then_inc(tab_row_ok, 1)
                        dve.wait_ge(tab_row_ok, n + 1)
                        if c == 1:
                            link(nc.vector.tensor_copy(fd_hi[:, t, 0:W], table_rows[:, t % 2, c, :]))
                            link(nc.vector.tensor_tensor(fd_lo[:, t, 0:W], table_rows[:, t % 2, c, :],
                                                         fd_hi[:, t, 0:W].bitcast(F32), ALU.subtract))

        with stage(nc) as (edges, sem):
            z = sb(f"z{k}", [P, G, W], F32, edges)
            logit = sb(f"logit{k}", [P, G, H], F32, edges)
            idx = sb(f"idx{k}", [P, G, 2], I32, edges)
            pick = sb(f"pick{k}", [P, G, P], F32R, edges)
            relu = sb(f"relu{k}", [P, 2, D], F32, edges)
            part = sb(f"part{k}", [P, 4, H], F32, edges)
            (go, logit_ok, relu_ok, part_ok, cols_ok, dst_turned, pick_ok, picked, z_ok) = (
                sem(f"{s}{k}") for s in ("go", "logit_ok", "relu_ok", "part_ok", "cols_ok",
                                         "dst_turned", "pick_ok", "picked", "z_ok"))
            sum_in = [sem(f"sum_in{k}{u}") for u in range(G)]
            scattered = [sem(f"scattered{k}{u}") for u in range(2)]

            def octet_count(eng):
                return eng.value_load(octets[0:1, 0:1], min_val=ET // G - 2, max_val=NI // G - 2) + 2

            with nc.Block() as block:
                @block.gpsimd
                def _(pool):
                    def add_source(u, n):
                        pool.wait_ge(z_ok, 3 * (n + 1))
                        nc.gpsimd.sem_inc(go, 1)
                        nc.gpsimd.indirect_dma_start(
                            z[:, u, :], None, fs_tab[k],
                            bass.IndirectOffsetOnAxis(ap=idx[:, u, 0:1], axis=0),
                            compute_op=ALU.add).then_inc(sum_in[u], 16)

                    def scatter(u, n, before):
                        pool.wait_ge(logit_ok, n + 1)
                        if before is not None:
                            pool.wait_ge(scattered[u % 2], before * 16)
                        nc.gpsimd.sem_inc(go, 1)
                        nc.gpsimd.indirect_dma_start(
                            logit_tabs[k][u % 2], bass.IndirectOffsetOnAxis(ap=idx[:, u, 1:2], axis=0),
                            logit[:, u, :], None).then_inc(scattered[u % 2], 16)

                    n8 = octet_count(pool)
                    for u in range(G):
                        add_source(u, u)
                        if u >= LAG:
                            scatter(u - LAG, u - LAG, (u - LAG) // 2 or None)
                    with pool.Fori(1, n8) as g:
                        for u in range(G):
                            add_source(u, g * G + u)
                            scatter((u - LAG) % G, g * G + u - LAG, g * (G // 2) + (u - LAG) // 2)
                    for u in range(G - LAG, G):
                        scatter(u, n8 * G + (u - G), n8 * (G // 2) + (u - G) // 2)
                    for c in range(2):
                        pool.wait_ge(scattered[c], n8 * (16 * G // 2))
                    pool.sem_inc(go, 1)

                @block.tensor
                def _(pe):
                    def turn(g, h):
                        if h == 0:
                            pe.wait_ge(cols_ok, g + 1)
                        pe.wait_ge(pick_ok, 2 * g)
                        for u in range(4):
                            last = nc.tensor.transpose(bank[6 + h][0:P, u * P:(u + 1) * P],
                                                       key_col[:, 4 * h + u:4 * h + u + 1].to_broadcast([P, P]),
                                                       ident[0:P, 0:P])
                        last.then_inc(dst_turned, 1)

                    def rows(g, u, t, again):
                        n = g * G + u
                        pe.wait_ge(pick_ok, 2 * g + u // 4 + 1)
                        if again or u >= 2:
                            pe.wait_ge(z_ok, 3 * (n - 1))
                        b = 2 * (u % 2)
                        for lo, hi in ((0, 512), (512, W)):
                            for part_, (start, stop) in ((fd_hi, (True, False)), (fd_lo, (False, True))):
                                last = nc.tensor.matmul(
                                    bank[b + lo // 512][0:P, 0:hi - lo], pick[:, u, :],
                                    part_[:, bass.ds(t, 1), lo:hi].rearrange("p o d -> p (o d)"),
                                    start=start, stop=stop)
                        last.then_inc(picked, 1)

                    n8 = octet_count(pe)
                    turn(0, 0)
                    turn(0, 1)
                    tiles = node_tiles(pe, 0)
                    for u in range(G):
                        rows(0, u, tiles[u], False)
                    with pe.Fori(1, n8) as g:
                        tiles = node_tiles(pe, g)
                        turn(g, 0)
                        turn(g, 1)
                        for u in range(G):
                            rows(g, u, tiles[u], True)

                @block.scalar
                def _(act):
                    def fill(u, n, g, again):
                        if again:
                            act.wait_ge(scattered[u % 2], (g * (G // 2) + u // 2 + 1 - G // 2) * 16)
                        nc.scalar.copy(idx[:, u, :], item_idx[:, bass.ds(n, 1), :]
                                       .rearrange("p o c -> p (o c)")).then_inc(z_ok, 1)
                        act.wait_ge(picked, n + 1)
                        b = 2 * (u % 2)
                        nc.scalar.copy(z[:, u, 0:512], bank[b][0:P, :]).then_inc(z_ok, 1)
                        nc.scalar.copy(z[:, u, 512:W], bank[b + 1][0:P, 0:W - 512]).then_inc(z_ok, 1)

                    n8 = octet_count(act)
                    for u in range(G):
                        fill(u, u, 0, False)
                    with act.Fori(1, n8) as g:
                        for u in range(G):
                            fill(u, g * G + u, g, True)

                @block.vector
                def _(dve):
                    def columns(g):
                        dve.wait_ge(dst_turned, 2 * g)
                        nc.vector.tensor_copy(key_col[:], item_dst[:, bass.ds(g * G, G)]).then_inc(cols_ok, 1)

                    def one_hot(g, h, again):
                        dve.wait_ge(dst_turned, 2 * g + h + 1)
                        if again:
                            dve.wait_ge(picked, (g - 1) * G + 4 * h + 4)
                        nc.vector.tensor_scalar(pick[:, 4 * h:4 * h + 4, :].rearrange("q u e -> q (u e)"),
                                                bank[6 + h][0:P, 0:4 * P], part_iota[:, 0:1], None,
                                                ALU.is_equal).then_inc(pick_ok, 1)

                    def products(u, n, g):
                        dve.wait_ge(sum_in[u], g * 16 + 16)
                        b = u % 2
                        if H == 1:
                            nc.vector.scalar_tensor_tensor(out=relu[:, b, :], in0=z[:, u, 0:D], scalar=0.0,
                                                           in1=attn_s[:, 1, :], op0=ALU.max, op1=ALU.mult,
                                                           accum_out=part[:, u % 4, :]).then_inc(part_ok, 1)
                        else:
                            nc.vector.scalar_tensor_tensor(out=relu[:, b, :], in0=z[:, u, 0:D], scalar=0.0,
                                                           in1=attn_s[:, 1, :], op0=ALU.max,
                                                           op1=ALU.mult).then_inc(relu_ok, 1)

                    def head_sums(u, n):
                        dve.wait_ge(relu_ok, n + 1)
                        nc.vector.tensor_reduce(part[:, u % 4, :], relu[:, u % 2, :].rearrange("p (h d) -> p h d", h=H),
                                                AX.X, ALU.add).then_inc(part_ok, 1)

                    def logits(u, n, g, again):
                        dve.wait_ge(part_ok, n + 1)
                        if again:
                            dve.wait_ge(scattered[u % 2], (g * (G // 2) + u // 2 + 1 - G // 2) * 16)
                        nc.vector.tensor_tensor(logit[:, u, :], part[:, u % 4, :], z[:, u, D:D + H],
                                                ALU.add).then_inc(logit_ok, 1)

                    def octet(g, first, second, final):
                        if not final:
                            columns(g + 1)
                        for u in range(G):
                            n = g * G + u
                            if u >= 2 or not first:
                                dve.wait_ge(part_ok, n - 1)
                            if H == 1 and (u >= 4 or not first):
                                dve.wait_ge(logit_ok, n - 3)
                            products(u, n, g)
                            if H > 1 and (u or not first):
                                if u >= 5 or not first:
                                    dve.wait_ge(logit_ok, n - 4)
                                head_sums((u - 1) % G, n - 1)
                            if u >= 2:
                                logits(u - 2, n - 2, g, not first)
                            elif not first:
                                logits(u - 2 + G, n - 2, g - 1, not second)
                            if u in (3, 5) and not final:
                                one_hot(g + 1, u // 4, True)

                    n8 = octet_count(dve)
                    columns(0)
                    one_hot(0, 0, False)
                    one_hot(0, 1, False)
                    octet(0, True, False, False)
                    octet(1, False, True, False)
                    with dve.Fori(2, n8 - 1) as g:
                        octet(g, False, False, False)
                    octet(n8 - 1, False, False, True)
                    last = n8 * G - 1
                    dve.wait_ge(logit_ok, last - 1)
                    if H > 1:
                        head_sums(G - 1, last)
                    logits(G - 2, last - 1, n8 - 1, True)
                    logits(G - 1, last, n8 - 1, True)

        with stage(nc) as (attend, sem):
            LEAD, RING = min(2, H), 4
            HEADS = T * H
            pair = sb(f"pair{k}", [P, 2, N, H], F32, attend)
            odd = sb(f"odd{k}", [P, N, H], F32, attend)
            prob = sb(f"prob{k}", [P, RING, N], F32, attend)
            probT = sb(f"probT{k}", [P, 2, T, P], F32, attend)
            negmax = sb(f"negmax{k}", [P, 2, H], F32, attend)
            den = sb(f"den{k}", [P, 2, H], F32, attend)
            rden = sb(f"rden{k}", [P, H], F32, attend)
            o = sb(f"o{k}", [P, D], F32, attend)
            o_neg = sb(f"o_neg{k}", [P, D], F32, attend)
            pair_in = [sem(f"pair_in{k}{u}") for u in range(2)]
            pair_ok = sem(f"pair_ok{k}")
            max_ok, exp_ok, prob_ok, turned, probT_ok, summed, achain, neg_ok, elu_ok, std_ok, mul_ok, var_ok = (
                sem(f"{s}{k}") for s in ("max_ok", "exp_ok", "prob_ok", "p_turned", "probT_ok", "summed", "achain",
                                         "neg_ok", "elu_ok", "std_ok", "mul_ok", "a_var_ok"))
            with nc.Block() as block:
                @block.sync
                def _(sp):
                    tabs = [tab[0:N * N, :].rearrange("(t p s) h -> t p (s h)", t=T, p=P) for tab in logit_tabs[k]]
                    for t in range(T):
                        if t >= 2:
                            sp.wait_ge(exp_ok, (t - 1) * H)
                        sp.dma_start(pair[:, t % 2].rearrange("p s h -> p (s h)"), tabs[0][t]).then_inc(pair_in[t % 2], 16)
                        if t:
                            sp.wait_ge(pair_ok, t)
                        sp.dma_start(odd[:].rearrange("p s h -> p (s h)"), tabs[1][t]).then_inc(pair_in[t % 2], 16)

                @block.tensor
                def _(pe):
                    def turn(n):
                        b = 4 + 2 * (n % 2)
                        pe.wait_ge(prob_ok, n + 1)
                        if n >= 2:
                            pe.wait_ge(probT_ok, 2 * (n - 1))
                        for c in range(T):
                            to = bank[b][0:P, c * P:(c + 1) * P] if c < 4 else bank[b + 1][0:P, 0:P]
                            last = nc.tensor.transpose(to, prob[:, n % RING, c * P:(c + 1) * P], ident[0:P, 0:P])
                        last.then_inc(turned, 1)

                    def weighted_sum(n):
                        t, h = divmod(n, H)
                        pe.wait_ge(probT_ok, 2 * (n + 1))
                        if t >= 2 and h == 0:
                            pe.wait_ge(mul_ok, 2 * (t - 1))
                        for lo, w in ([(h * HD, HD)] if H > 1 else [(0, HALF), (HALF, HALF)]):
                            for c in range(T):
                                last = nc.tensor.matmul(
                                    bank[2 * (t % 2) + lo // HALF][0:P, lo % HALF:lo % HALF + w],
                                    probT[:, n % 2, c, :], fs[:, c, lo:lo + w], start=(c == 0), stop=(c == T - 1))
                        last.then_inc(summed, 1)

                    turn(0)
                    for n in range(HEADS):
                        if n + 1 < HEADS:
                            turn(n + 1)
                        weighted_sum(n)

                @block.scalar
                def _(act):
                    def exps(n):
                        t, h = divmod(n, H)
                        act.wait_ge(max_ok, t + 1)
                        if n >= RING:
                            act.wait_ge(turned, n - RING + 1)
                        nc.scalar.activation(prob[:, n % RING, :], pair[:, t % 2, :, h], ACT.Exp,
                                             bias=negmax[:, t % 2, h:h + 1]).then_inc(exp_ok, 1)

                    def copy_turned(n):
                        act.wait_ge(turned, n + 1)
                        if n >= 2:
                            act.wait_ge(summed, n - 1)
                        b = 4 + 2 * (n % 2)
                        nc.scalar.copy(probT[:, n % 2, 0:4, :].rearrange("p c q -> p (c q)"),
                                       bank[b][0:P, 0:4 * P]).then_inc(probT_ok, 1)
                        nc.scalar.copy(probT[:, n % 2, 4, :], bank[b + 1][0:P, 0:P]).then_inc(probT_ok, 1)

                    def elu(t):
                        act.wait_ge(neg_ok, t + 1)
                        nc.scalar.activation(o_neg[:], o_neg[:], ACT.Exp).then_inc(elu_ok, 1)

                    for n in range(LEAD):
                        exps(n)
                    for n in range(HEADS):
                        if n + LEAD < HEADS:
                            exps(n + LEAD)
                        copy_turned(n)
                        if n >= H and n % H == min(1, H - 1):
                            elu(n // H - 1)
                    elu(T - 1)
                    act.wait_ge(var_ok, 1)
                    nc.scalar.activation(std[:], mv[:, :, 1], ACT.Sqrt, bias=eps[0:P, :]).then_inc(std_ok, 1)

                @block.vector
                def _(dve):
                    link = Chain(dve, achain)

                    def maxima(t):
                        dve.wait_ge(pair_in[t % 2], 32 * (t // 2 + 1))
                        nc.vector.tensor_tensor(pair[:, t % 2], pair[:, t % 2], odd[:], ALU.max).then_inc(pair_ok, 1)
                        dve.wait_ge(pair_ok, t + 1)
                        if t >= 2:
                            dve.wait_ge(exp_ok, (t - 1) * H)
                        nc.vector.tensor_reduce(negmax[:, t % 2, :], pair[:, t % 2].rearrange("p s h -> p h s"),
                                                AX.X, ALU.max, negate=True).then_inc(max_ok, 1)

                    def weigh(n):
                        t, h = divmod(n, H)
                        dve.wait_ge(exp_ok, n + 1)
                        nc.vector.tensor_tensor_reduce(prob[:, n % RING, :], prob[:, n % RING, :], counts[:, t, :],
                                                       1.0, 0.0, ALU.mult, ALU.add,
                                                       den[:, t % 2, h:h + 1]).then_inc(prob_ok, 1)

                    def finish(t):
                        dve.wait_ge(prob_ok, (t + 1) * H)
                        link(nc.vector.tensor_scalar(rden[:], den[:, t % 2, :], 1e-30, None, ALU.max))
                        link(nc.vector.reciprocal(rden[:], rden[:]))
                        dve.wait_ge(summed, (t + 1) * H)
                        for c in range(2):
                            hh = max(H // 2, 1)
                            scale = rden[:, (c * hh) % H:(c * hh) % H + hh]
                            nc.vector.tensor_tensor(
                                o[:, c * HALF:(c + 1) * HALF].rearrange("p (h d) -> p h d", h=hh),
                                bank[2 * (t % 2) + c][0:P, 0:HALF].rearrange("p (h d) -> p h d", h=hh),
                                scale.unsqueeze(2).to_broadcast([P, hh, HALF // hh]), ALU.mult).then_inc(mul_ok, 1)
                        dve.wait_ge(mul_ok, 2 * t + 2)
                        nc.vector.tensor_scalar(o_neg[:], o[:], 0.0, None, ALU.min).then_inc(neg_ok, 1)
                        dve.wait_ge(elu_ok, t + 1)
                        link(nc.vector.scalar_tensor_tensor(out=o[:], in0=o[:], scalar=0.0, in1=o_neg[:],
                                                            op0=ALU.max, op1=ALU.add))
                        if k == 0:
                            link(nc.vector.scalar_tensor_tensor(out=x_rows[:, t, :], in0=o[:], scalar=-1.0,
                                                                in1=x_rows[:, t, :], op0=ALU.add, op1=ALU.add))
                        else:
                            link(nc.vector.tensor_scalar(x_rows[:, t, :], o[:], -1.0, None, ALU.add))
                        row_stats(nc, link, x_rows[:, t, :], D, stats, mv[:, t, :])

                    maxima(0)
                    for n in range(HEADS):
                        t, h = divmod(n, H)
                        if h == H // 2 and t + 1 < T:
                            maxima(t + 1)
                        weigh(n)
                        if n >= H and h == min(1, H - 1):
                            finish(t - 1)
                    finish(T - 1)
                    nc.vector.tensor_copy(stats[:, 0, :], stats[:, 1, :]).then_inc(var_ok, 1)
                    dve.wait_ge(var_ok, 1)
                    dve.wait_ge(std_ok, 1)
                    link(nc.vector.reciprocal(rstd[:], std[:]))
                    for t in range(T):
                        link(nc.vector.scalar_tensor_tensor(out=x_rows[:, t, :], in0=x_rows[:, t, :], scalar=mv[:, t, 0:1],
                                                            in1=vecs[:, 3, :], op0=ALU.subtract, op1=ALU.mult))
                        link(nc.vector.scalar_tensor_tensor(out=x_rows[:, t, :], in0=x_rows[:, t, :],
                                                            scalar=rstd[:, t:t + 1], in1=vecs[:, 4, :],
                                                            op0=ALU.mult, op1=ALU.add))


def mixture(nc, a, out, moe, sb, dram, bank, x_rows, ident, eps, before, ones, slot_out):
    def mb(name, shape, dt=F32):
        return sb(name, shape, dt, moe)

    gate_w, gate_b, fc1_w, fc1_b, ln_w, ln_b, fc2_w, fc2_b = (
        a["L0_ffn_" + n] for n in ("gate_w", "gate_b", "fc1_w", "fc1_b", "ln_w", "ln_b", "fc2_w", "fc2_b"))
    token_rows = dram("token_rows", (N, D))
    slot_token = dram("slot_token", (NTAB * S, 1), I32)

    topv = mb("topv", [P, TOP, T])
    slot_i = mb("slot_i", [P, TOP * T], I32)
    tile_expert = mb("tile_expert", [1, NTAB], I32)
    tile_group = mb("tile_group", [1, NTAB], I32)
    group_expert = mb("group_expert", [1, X + 1], I32)
    group_before = mb("group_before", [1, X + 1], I32)
    last_tile = mb("last_tile", [1, 1], I32)
    last_group = mb("last_group", [1, 1], I32)

    with stage(nc) as (route, sem):
        def rb(name, shape, dt=F32):
            return sb(name, shape, dt, route)

        xf = rb("xf", [P, T, D])
        x_again = rb("x_again", [P, T, D])
        x_back = sem("x_back")
        xfT = rb("xfT", [128, KD, N])
        gw = rb("gw", [128, KD, X])
        gbias = rb("gbias", [P, X])
        mv, stats = rb("r_mv", [P, T, 2]), rb("r_stats", [P, 2, 6])
        std, rstd = rb("r_std", [P, T]), rb("r_rstd", [P, T])
        pr = rb("pr", [P, T, X])
        m = rb("m", [P, T])
        eq = rb("eq", [P, T, X])
        chosen = rb("chosen", [P, TOP, T, X])
        sel = rb("sel", [P, T, X])
        pos = rb("pos", [P, T, X])
        total = rb("total", [P, X])
        tiles = rb("tiles", [P, X])
        more = rb("more", [P, X])
        ends = rb("tile_ends", [P, X])
        one_x = rb("one_x", [P, X])
        iota_x = rb("iota_x", [P, X])
        iota_j = rb("iota_j", [1, NTAB])
        at_or_past = rb("at_or_past", [1, NTAB, X])
        expert_f = rb("expert_f", [1, NTAB])
        some = rb("some", [P, X])
        ordinal = rb("ordinal", [P, X])
        in_group = rb("in_group", [1, X + 1, X])
        weighted = rb("weighted", [1, X + 1, X])
        group_f = rb("group_f", [1, X + 1])
        slot_f = rb("slot_f", [P, TOP, T])
        token_id = rb("token_id", [P, T], I32)
        first_f = rb("first_f", [NTAB, S])
        row_is_shared = rb("row_is_shared", [NTAB, S])
        first_i = rb("first_i", [NTAB, S], I32)
        g_in, r_chain, r_var, r_std, xf_ok, x_out = (sem(s) for s in ("g_in", "r_chain", "r_var", "r_std_ok", "xf_ok", "x_out"))
        r_turned, xfT_ok, score_ok, sel_ok, pos_ok, exp_in, exp_out, r_const, r_pool = (
            sem(s) for s in ("r_turned", "xfT_ok", "score_ok", "sel_ok", "pos_ok", "exp_in", "exp_out", "r_const", "r_pool"))
        first_ok, first_out, slots_ok, slot_out_ok = (sem(s) for s in ("first_ok", "first_out", "slots_ok", "slot_out_ok"))
        with nc.Block() as block:
            @block.sync
            def _(sp):
                sp.dma_start(x_again[:], a["x"].rearrange("(t p) d -> p t d", p=P)).then_inc(x_back, 16)
                sp.dma_start(gw[:], gate_w.rearrange("(k p) e -> p k e", p=128)).then_inc(g_in, 16)
                sp.dma_start(gbias[:], gate_b.partition_broadcast(P)).then_inc(g_in, 16)
                sp.wait_ge(first_ok, 1)
                sp.dma_start(slot_token.rearrange("(j s) o -> j (s o)", s=S), first_i[:]).then_inc(first_out, 16)
                sp.wait_ge(xf_ok, T)
                sp.dma_start(token_rows.rearrange("(t p) d -> p t d", p=P), xf[:]).then_inc(x_out, 16)
                sp.wait_ge(x_out, 16)

            @block.gpsimd
            def _(pool):
                link = Chain(pool, r_pool)
                link(nc.gpsimd.iota(iota_x[:], pattern=[[1, X]], base=0, channel_multiplier=0,
                                    allow_small_or_imprecise_dtypes=True))
                link(nc.gpsimd.iota(iota_j[:], pattern=[[1, NTAB]], base=0, channel_multiplier=0,
                                    allow_small_or_imprecise_dtypes=True))
                link(nc.gpsimd.iota(token_id[:], pattern=[[P, T]], base=0, channel_multiplier=1))
                link(nc.gpsimd.iota(first_f[:], pattern=[[1, S]], base=0, channel_multiplier=S,
                                    allow_small_or_imprecise_dtypes=True))
                link(nc.gpsimd.memset(one_x[:], 1.0))
                nc.gpsimd.memset(row_is_shared[:], 1.0).then_inc(r_const, 1)
                pool.wait_ge(first_out, 16)
                pool.wait_ge(slots_ok, 1)
                for n in range(TOP * T):
                    if n:
                        pool.wait_ge(slot_out_ok, 16 * n)
                    nc.gpsimd.indirect_dma_start(
                        slot_token, bass.IndirectOffsetOnAxis(ap=slot_i[:, n:n + 1], axis=0),
                        token_id[:, n % T:n % T + 1], None).then_inc(slot_out_ok, 16)
                pool.wait_ge(slot_out_ok, 16 * TOP * T)

            @block.scalar
            def _(act):
                act.wait_ge(r_var, 1)
                nc.scalar.activation(std[:], mv[:, :, 1], ACT.Sqrt, bias=eps[0:P, :]).then_inc(r_std, 1)
                for n in range(2 * T):
                    t, h = divmod(n, 2)
                    act.wait_ge(r_turned, n + 1)
                    nc.scalar.copy(xfT[:, 3 * h:3 * h + 3, t * P:(t + 1) * P],
                                   bank[n % 4][:, 0:3 * P].rearrange("p (k n) -> p k n", k=3)).then_inc(xfT_ok, 1)
                act.wait_ge(exp_in, 1)
                nc.scalar.activation(pr[:], pr[:], ACT.Exp).then_inc(exp_out, 1)

            @block.tensor
            def _(pe):
                for n in range(2 * T):
                    t, h = divmod(n, 2)
                    pe.wait_ge(xf_ok, t + 1)
                    if n >= 4:
                        pe.wait_ge(xfT_ok, n - 3)
                    for u in range(3):
                        c = 3 * h + u
                        last = nc.tensor.transpose(bank[n % 4][:, u * P:(u + 1) * P],
                                                   xf[:, t, c * 128:(c + 1) * 128], ident[0:P, 0:P])
                    last.then_inc(r_turned, 1)
                pe.wait_ge(g_in, 32)
                for t in range(T):
                    pe.wait_ge(xfT_ok, 2 * t + 2)
                    for c in range(KD):
                        last = nc.tensor.matmul(bank[4][0:P, t * X:(t + 1) * X], xfT[:, c, t * P:(t + 1) * P],
                                                gw[:, c, :], start=(c == 0), stop=(c == KD - 1))
                last.then_inc(score_ok, 1)
                pe.wait_ge(sel_ok, 1)
                for t in range(T):
                    for c in range(t + 1):
                        last = nc.tensor.matmul(bank[5][0:P, t * X:(t + 1) * X], before[:] if c == t else ones[:],
                                                sel[:, c, :], start=(c == 0), stop=(c == t))
                for c in range(T):
                    last = nc.tensor.matmul(bank[6][0:P, 0:X], ones[:], sel[:, c, :], start=(c == 0), stop=(c == T - 1))
                last.then_inc(pos_ok, 1)

            @block.vector
            def _(dve):
                link = Chain(dve, r_chain)
                dve.wait_ge(x_back, 16)
                for t in range(T):
                    link(nc.vector.tensor_tensor(x_rows[:, t, :], x_rows[:, t, :], x_again[:, t, :], ALU.add))
                    row_stats(nc, link, x_rows[:, t, :], D, stats, mv[:, t, :])
                nc.vector.tensor_copy(stats[:, 0, :], stats[:, 1, :]).then_inc(r_var, 1)
                dve.wait_ge(r_var, 1)
                dve.wait_ge(r_std, 1)
                link(nc.vector.reciprocal(rstd[:], std[:]))
                for t in range(T):
                    nc.vector.tensor_scalar(xf[:, t, :], x_rows[:, t, :], mv[:, t, 0:1], rstd[:, t:t + 1],
                                            ALU.subtract, ALU.mult).then_inc(xf_ok, 1)
                dve.wait_ge(r_const, 1)
                link(nc.vector.tensor_scalar(row_is_shared[:], first_f[:], float(SHARED * S), None, ALU.is_lt))
                link(nc.vector.tensor_scalar(first_f[:], first_f[:], float(N - 1), None, ALU.min))
                link(nc.vector.tensor_tensor(first_f[:], first_f[:], row_is_shared[:], ALU.mult))
                nc.vector.tensor_copy(first_i[:], first_f[:]).then_inc(first_ok, 1)
                dve.wait_ge(g_in, 32)
                dve.wait_ge(score_ok, 1)
                link(nc.vector.tensor_tensor(pr[:], bank[4][0:P, 0:T * X].rearrange("p (t e) -> p t e", t=T),
                                             gbias[:].unsqueeze(1).to_broadcast([P, T, X]), ALU.add))
                link(nc.vector.memset(pr[:, :, 0:1], -1e9))
                link(nc.vector.tensor_reduce(m[:], pr[:], AX.X, ALU.max))
                nc.vector.tensor_tensor(pr[:], pr[:], m[:].unsqueeze(2).to_broadcast([P, T, X]),
                                        ALU.subtract).then_inc(exp_in, 1)
                dve.wait_ge(exp_out, 1)
                link(nc.vector.tensor_reduce(m[:], pr[:], AX.X, ALU.add))
                link(nc.vector.reciprocal(m[:], m[:]))
                link(nc.vector.tensor_tensor(pr[:], pr[:], m[:].unsqueeze(2).to_broadcast([P, T, X]), ALU.mult))
                for c in range(TOP):
                    link(nc.vector.tensor_reduce(topv[:, c, :], pr[:], AX.X, ALU.max))
                    link(nc.vector.tensor_tensor(eq[:], pr[:], topv[:, c, :].unsqueeze(2).to_broadcast([P, T, X]),
                                                 ALU.is_lt))
                    link(nc.vector.tensor_scalar(eq[:], eq[:], float(X), None, ALU.mult))
                    link(nc.vector.tensor_tensor(eq[:], eq[:], iota_x[:].unsqueeze(1).to_broadcast([P, T, X]), ALU.add))
                    link(nc.vector.tensor_reduce(m[:], eq[:], AX.X, ALU.min))
                    link(nc.vector.tensor_tensor(chosen[:, c], iota_x[:].unsqueeze(1).to_broadcast([P, T, X]),
                                                 m[:].unsqueeze(2).to_broadcast([P, T, X]), ALU.is_equal))
                    link(nc.vector.scalar_tensor_tensor(out=pr[:], in0=chosen[:, c], scalar=-4.0, in1=pr[:],
                                                        op0=ALU.mult, op1=ALU.add))
                link(nc.vector.tensor_tensor(sel[:], chosen[:, 0], chosen[:, 1], ALU.add))
                nc.vector.tensor_tensor(sel[:], sel[:], chosen[:, 2], ALU.add).then_inc(sel_ok, 1)
                dve.wait_ge(pos_ok, 1)
                link(nc.vector.tensor_copy(total[:], bank[6][0:P, 0:X]))
                link(nc.vector.tensor_scalar(tiles[:], total[:], 0.0, None, ALU.is_gt))
                for c in range(1, SHARED):
                    link(nc.vector.tensor_scalar(more[:], total[:], float(c * S), None, ALU.is_gt))
                    link(nc.vector.tensor_tensor(tiles[:], tiles[:], more[:], ALU.add))
                link(nc.vector.tensor_tensor_scan(ends[:], one_x[:], tiles[:], float(SHARED), ALU.mult, ALU.add))
                link(nc.vector.tensor_tensor(more[:], ends[:], tiles[:], ALU.subtract))
                link(nc.vector.tensor_scalar(more[:], more[:], float(S), None, ALU.mult))
                link(nc.vector.tensor_tensor(pos[:], bank[5][0:P, 0:T * X].rearrange("p (t e) -> p t e", t=T),
                                             more[:].unsqueeze(1).to_broadcast([P, T, X]), ALU.add))
                for c in range(TOP):
                    link(nc.vector.tensor_tensor(eq[:], chosen[:, c], pos[:], ALU.mult))
                    link(nc.vector.tensor_reduce(slot_f[:, c, :], eq[:], AX.X, ALU.add))
                nc.vector.tensor_copy(slot_i[:], slot_f[:].rearrange("p c t -> p (c t)")).then_inc(slots_ok, 1)
                link(nc.vector.tensor_tensor(at_or_past[:], ends[0:1, :].unsqueeze(1).to_broadcast([1, NTAB, X]),
                                             iota_j[:].unsqueeze(2).to_broadcast([1, NTAB, X]), ALU.is_le))
                link(nc.vector.tensor_reduce(expert_f[:], at_or_past[:], AX.X, ALU.add))
                link(nc.vector.tensor_scalar(expert_f[:], expert_f[:], float(X - 1), None, ALU.min))
                link(nc.vector.tensor_copy(tile_expert[:], expert_f[:]))
                link(nc.vector.tensor_scalar(last_tile[:], ends[0:1, X - 1:X], -1.0, None, ALU.add))
                link(nc.vector.tensor_scalar(some[:], tiles[:], 1.0, None, ALU.min))
                link(nc.vector.tensor_tensor_scan(ordinal[:], one_x[:], some[:], 0.0, ALU.mult, ALU.add))
                link(nc.vector.tensor_copy(last_group[:], ordinal[0:1, X - 1:X]))
                link(nc.vector.tensor_tensor(more[:], ends[:], tiles[:], ALU.subtract))
                link(nc.vector.tensor_tensor(at_or_past[:], more[0:1, :].unsqueeze(1).to_broadcast([1, NTAB, X]),
                                             iota_j[:].unsqueeze(2).to_broadcast([1, NTAB, X]), ALU.is_le))
                link(nc.vector.tensor_tensor(at_or_past[:], at_or_past[:],
                                             some[0:1, :].unsqueeze(1).to_broadcast([1, NTAB, X]), ALU.mult))
                link(nc.vector.tensor_reduce(expert_f[:], at_or_past[:], AX.X, ALU.add))
                link(nc.vector.tensor_copy(tile_group[:], expert_f[:]))
                link(nc.vector.tensor_tensor(in_group[:], ordinal[0:1, :].unsqueeze(1).to_broadcast([1, X + 1, X]),
                                             iota_j[:, 0:X + 1].unsqueeze(2).to_broadcast([1, X + 1, X]), ALU.is_equal))
                link(nc.vector.tensor_tensor(in_group[:], in_group[:],
                                             some[0:1, :].unsqueeze(1).to_broadcast([1, X + 1, X]), ALU.mult))
                for table, value in ((group_expert, iota_x), (group_before, more)):
                    link(nc.vector.tensor_tensor(weighted[:], in_group[:],
                                                 value[0:1, :].unsqueeze(1).to_broadcast([1, X + 1, X]), ALU.mult))
                    link(nc.vector.tensor_reduce(group_f[:], weighted[:], AX.X, ALU.add))
                    if table is group_before:
                        link(nc.vector.tensor_scalar(group_f[:], group_f[:], -1.0, 0.0, ALU.add, ALU.max))
                    link(nc.vector.tensor_copy(table[:], group_f[:]))

    with stage(nc) as (ff, sem):
        def fb(name, shape, dt=F32):
            return sb(name, shape, dt, ff)

        w1 = fb("w1", [128, KF // 2, FF])
        w2 = fb("w2", [128, KF, D])
        xg = fb("xg", [S, D])
        slot_idx = fb("slot_idx", [S, 1], I32)
        xgT = fb("xgT", [128, KD, S])
        h = fb("h", [S, FF])
        hn = fb("hn", [S, FF])
        hT = fb("hT", [128, KF, S])
        y = fb("y", [S, D])
        row1 = fb("row1", [1, 3 * FF])
        row2 = fb("row2", [1, D])
        all1 = fb("all1", [S, 3 * FF])
        all2 = fb("all2", [S, D])
        mv, stats = fb("e_mv", [S, 2]), fb("e_stats", [S, 3, 6])
        std, rstd = fb("e_std", [S, 1]), fb("e_rstd", [S, 1])
        w1_in = [sem(f"w1_in{c}") for c in range(KD)]
        w2_in = [sem(f"w2_in{c}") for c in range(KD)]
        row1_in, row2_in, idx_in, xg_in, y_out, go = (sem(s) for s in ("row1_in", "row2_in", "idx_in", "xg_in", "y_out", "e_go"))
        w1_used, w2_used, x_turned, xgT_ok, h_ok, h_turned, hT_ok, y_ok = (
            sem(s) for s in ("w1_used", "w2_used", "x_turned", "xgT_ok", "h_ok", "h_turned", "hT_ok", "y_ok"))
        go_sp, go_dve, go_act = sem("go_sp"), sem("go_dve"), sem("go_act")
        all1_ok, all2_ok, biased, gelu_ok, stat_ok, aggr_ok, std_ok, rstd_ok, centred, hn_ok, y_sb = (
            sem(s) for s in ("all1_ok", "all2_ok", "biased", "gelu_ok", "stat_ok", "aggr_ok", "e_std_ok", "rstd_ok",
                             "centred", "hn_ok", "y_sb"))
        with nc.Block() as block:
            def final_tile(eng):
                return eng.value_load(last_tile[0:1, 0:1], min_val=MINT - 1, max_val=MAXT - 1)

            @block.sync
            def _(sp):
                def load_w1(e, before):
                    for c in range(KD):
                        if before is not None:
                            sp.wait_ge(w1_used, before * KD + c + 1)
                            sp.sem_inc(go_sp, 1)
                        sp.dma_start(w1[:, c, :], fc1_w[bass.ds(e, 1), c * 128:(c + 1) * 128, :]
                                     .rearrange("o p n -> (o p) n")).then_inc(w1_in[c], 16)

                def load_w2(e, before):
                    for c in range(KD):
                        if before is not None:
                            sp.wait_ge(w2_used, before * KD + c + 1)
                            sp.sem_inc(go_sp, 1)
                        sp.dma_start(w2[:, 2 * c:2 * c + 2, :], fc2_w[bass.ds(e, 1), c * 256:(c + 1) * 256, :]
                                     .rearrange("o (k p) n -> (o p) k n", p=128)).then_inc(w2_in[c], 16)

                def row_of(table, g, top):
                    return sp.value_load(table[0:1, bass.ds(g, 1)], min_val=0, max_val=top)

                groups = sp.value_load(last_group[0:1, 0:1], min_val=TOP, max_val=X)
                load_w1(0, None)
                load_w2(0, None)
                load_w1(row_of(group_expert, 1, X - 1), row_of(group_before, 1, MAXT - 1))
                with sp.Fori(1, groups) as g:
                    e, before = row_of(group_expert, g, X - 1), row_of(group_before, g, MAXT - 1)
                    e_next, before_next = row_of(group_expert, g + 1, X - 1), row_of(group_before, g + 1, MAXT - 1)
                    with sp.If(before_next - before == 1):
                        load_w1(e_next, before_next)
                        load_w2(e, before)
                    with sp.Else():
                        load_w2(e, before)
                        load_w1(e_next, before_next)
                load_w2(row_of(group_expert, groups, X - 1), row_of(group_before, groups, MAXT - 1))

            @block.gpsimd
            def _(pool):
                def load_rows(j, again1, again2):
                    e = pool.value_load(tile_expert[0:1, bass.ds(j, 1)], min_val=0, max_val=X - 1)
                    if again1:
                        pool.wait_ge(all1_ok, j)
                    if again2:
                        pool.wait_ge(all2_ok, j)
                    pool.sem_inc(go, 1)
                    for c, v in enumerate((fc1_b, ln_w, ln_b)):
                        nc.gpsimd.dma_start(row1[:, c * FF:(c + 1) * FF], v[bass.ds(e, 1), :]).then_inc(row1_in, 16)
                    nc.gpsimd.dma_start(row2[:], fc2_b[bass.ds(e, 1), :]).then_inc(row2_in, 16)

                def gather(j, again):
                    if again:
                        pool.wait_ge(x_turned, j)
                    nc.gpsimd.sem_inc(go, 1)
                    nc.gpsimd.dma_start(slot_idx[:], slot_token[bass.ds(j * S, S), :]).then_inc(idx_in, 16)
                    pool.wait_ge(idx_in, 16 * (j + 1))
                    nc.gpsimd.sem_inc(go, 1)
                    nc.gpsimd.indirect_dma_start(xg[:], None, token_rows,
                                                 bass.IndirectOffsetOnAxis(ap=slot_idx[:, 0:1], axis=0)).then_inc(xg_in, 16)

                def spread1(j, again):
                    if again:
                        pool.wait_ge(hn_ok, j)
                    pool.wait_ge(row1_in, 48 * (j + 1))
                    nc.gpsimd.sem_inc(go, 1)
                    nc.gpsimd.partition_broadcast(all1[:], row1[:]).then_inc(all1_ok, 1)

                def spread2(j, again):
                    if again:
                        pool.wait_ge(y_sb, 2 * j)
                    pool.wait_ge(row2_in, 16 * (j + 1))
                    nc.gpsimd.sem_inc(go, 1)
                    nc.gpsimd.partition_broadcast(all2[:], row2[:]).then_inc(all2_ok, 1)

                end = final_tile(pool)
                load_rows(0, False, False)
                gather(0, False)
                spread1(0, False)
                spread2(0, False)
                load_rows(1, True, True)
                gather(1, True)
                with pool.Fori(1, end + 1) as j:
                    spread1(j, True)
                    gather(j + 1, True)
                    spread2(j, True)
                    load_rows(j + 1, True, True)
                pool.wait_ge(row1_in, 48 * (end + 2))
                pool.wait_ge(row2_in, 16 * (end + 2))
                pool.wait_ge(xg_in, 16 * (end + 2))
                pool.sem_inc(go, 1)

            @block.tensor
            def _(pe):
                def turn_tokens(j, again):
                    pe.wait_ge(xg_in, 16 * (j + 1))
                    for c in range(KD):
                        last = nc.tensor.transpose(bank[5 + c // 4][:, (c % 4) * S:(c % 4 + 1) * S],
                                                   xg[:, c * 128:(c + 1) * 128], ident[:])
                    last.then_inc(x_turned, 1)

                def group(j):
                    return pe.value_load(tile_group[0:1, bass.ds(j, 1)], min_val=0, max_val=X)

                def first_product(j, g, slices, again):
                    for c in slices:
                        pe.wait_ge(w1_in[c], 16 * (g + 1))
                        if c == 0:
                            pe.wait_ge(xgT_ok, 2 * (j + 1))
                            if again:
                                pe.wait_ge(biased, 3 * j)
                        for b in range(3):
                            last = nc.tensor.matmul(bank[b][:], xgT[:, c, :], w1[:, c, b * 512:(b + 1) * 512],
                                                    start=(c == 0), stop=(c == KD - 1))
                        last.then_inc(w1_used, 1)

                def turn_hidden(j):
                    pe.wait_ge(hn_ok, j + 1)
                    pe.wait_ge(xgT_ok, 2 * (j + 2))
                    for b in range(3):
                        for u in range(4):
                            c = 4 * b + u
                            last = nc.tensor.transpose(bank[5 + b][:, u * S:(u + 1) * S],
                                                       hn[:, c * 128:(c + 1) * 128], ident[:])
                        last.then_inc(h_turned, 1)

                def second_product(j, g, slices, again):
                    for c in slices:
                        if c % 2 == 0:
                            pe.wait_ge(w2_in[c // 2], 16 * (g + 1))
                        if c % 4 == 0:
                            pe.wait_ge(hT_ok, 3 * j + c // 4 + 1)
                        if c == 0 and again:
                            pe.wait_ge(y_sb, 2 * j)
                        for b in range(2):
                            last = nc.tensor.matmul(bank[3 + b][:, 0:HALF], hT[:, c, :],
                                                    w2[:, c, b * HALF:(b + 1) * HALF],
                                                    start=(c == 0), stop=(c == KF - 1))
                        if c % 2:
                            last.then_inc(w2_used, 1)

                end = final_tile(pe)
                turn_tokens(0, False)
                first_product(0, 0, range(KD), False)
                turn_tokens(1, True)

                def step(j, again):
                    g, g_before = group(j), group(j - 1)
                    first_product(j, g, range(0, 4), True)
                    turn_hidden(j - 1)
                    first_product(j, g, range(4, KD), True)
                    second_product(j - 1, g_before, range(0, 8), again)
                    pe.wait_ge(hT_ok, 3 * j)
                    turn_tokens(j + 1, True)
                    second_product(j - 1, g_before, range(8, KF), again)

                step(1, False)
                with pe.Fori(2, end + 1) as j:
                    step(j, True)
                turn_hidden(end)
                second_product(end, group(end), range(KF), True)

            @block.scalar
            def _(act):
                def copy_tokens(j):
                    act.wait_ge(x_turned, j + 1)
                    act.wait_ge(w1_used, j * KD)
                    nc.scalar.copy(xgT[:, 0:4, :].rearrange("p k s -> p (k s)"), bank[5][:]).then_inc(xgT_ok, 1)
                    nc.scalar.copy(xgT[:, 4:6, :].rearrange("p k s -> p (k s)"), bank[6][:, 0:2 * S]).then_inc(xgT_ok, 1)

                def hidden(j):
                    for b in range(3):
                        act.wait_ge(biased, 3 * j + b + 1)
                        nc.scalar.activation(h[:, b * 512:(b + 1) * 512], h[:, b * 512:(b + 1) * 512],
                                             ACT.Gelu).then_inc(gelu_ok, 1)
                    act.wait_ge(aggr_ok, j + 1)
                    nc.scalar.activation(std[:], mv[:, 1:2], ACT.Sqrt, bias=eps[:]).then_inc(std_ok, 1)

                def copy_hidden(j, again):
                    for b in range(3):
                        act.wait_ge(h_turned, 3 * j + b + 1)
                        if again:
                            act.wait_ge(w2_used, j * KD)
                        nc.scalar.copy(hT[:, 4 * b:4 * b + 4, :].rearrange("p k s -> p (k s)"),
                                       bank[5 + b][:]).then_inc(hT_ok, 1)

                def store(j):
                    act.wait_ge(y_sb, 2 * (j + 1))
                    act.dma_start(slot_out[bass.ds(j * S, S), :], y[:]).then_inc(y_out, 16)

                end = final_tile(act)
                copy_tokens(0)
                hidden(0)
                copy_tokens(1)

                def step(j, again):
                    copy_hidden(j - 1, again)
                    hidden(j)
                    copy_tokens(j + 1)
                    store(j - 1)

                step(1, False)
                with act.Fori(2, end + 1) as j:
                    step(j, True)
                copy_hidden(end, True)
                store(end)
                act.wait_ge(y_out, 16 * (end + 1))
                act.sem_inc(go_act, 1)

            @block.vector
            def _(dve):
                def hidden(j, again):
                    dve.wait_ge(all1_ok, j + 1)
                    dve.wait_ge(w1_used, KD * (j + 1))
                    if again:
                        dve.wait_ge(hn_ok, j)
                    for b in range(3):
                        nc.vector.tensor_tensor(h[:, b * 512:(b + 1) * 512], bank[b][:],
                                                all1[:, b * 512:(b + 1) * 512], ALU.add).then_inc(biased, 1)
                    for b in range(3):
                        dve.wait_ge(gelu_ok, 3 * j + b + 1)
                        nc.vector.bn_stats(stats[:, b, :], h[:, b * 512:(b + 1) * 512]).then_inc(stat_ok, 1)
                    if again:
                        dve.wait_ge(std_ok, j)
                    dve.wait_ge(stat_ok, 3 * (j + 1))
                    nc.vector.sem_inc(go_dve, 1)
                    nc.vector.bn_aggr(mv[:], stats[:].rearrange("p c s -> p (c s)")).then_inc(aggr_ok, 1)
                    dve.wait_ge(aggr_ok, j + 1)
                    nc.vector.scalar_tensor_tensor(out=h[:], in0=h[:], scalar=mv[:, 0:1], in1=all1[:, FF:2 * FF],
                                                   op0=ALU.subtract, op1=ALU.mult).then_inc(centred, 1)
                    dve.wait_ge(std_ok, j + 1)
                    nc.vector.reciprocal(rstd[:], std[:]).then_inc(rstd_ok, 1)
                    dve.wait_ge(rstd_ok, j + 1)
                    dve.wait_ge(centred, j + 1)
                    if again:
                        dve.wait_ge(h_turned, 3 * j)
                    nc.vector.scalar_tensor_tensor(out=hn[:], in0=h[:], scalar=rstd[:, 0:1], in1=all1[:, 2 * FF:3 * FF],
                                                   op0=ALU.mult, op1=ALU.add).then_inc(hn_ok, 1)

                def output(j, again):
                    dve.wait_ge(all2_ok, j + 1)
                    dve.wait_ge(w2_used, KD * (j + 1))
                    if again:
                        dve.wait_ge(y_out, 16 * j)
                    for b in range(2):
                        nc.vector.tensor_tensor(y[:, b * HALF:(b + 1) * HALF], bank[3 + b][:, 0:HALF],
                                                all2[:, b * HALF:(b + 1) * HALF], ALU.add).then_inc(y_sb, 1)

                end = final_tile(dve)
                hidden(0, False)
                hidden(1, True)
                output(0, False)
                with dve.Fori(2, end + 1) as j:
                    hidden(j, True)
                    output(j - 1, True)
                output(end, True)

    with stage(nc) as (last_stage, sem):
        gathered = sb("gathered", [P, TOP * T, D], F32, last_stage)
        shared = sb("shared", [P, T, D], F32, last_stage)
        slots_in = [sem(f"slots_in{t}") for t in range(T)]
        shared_in, f_chain, row_done, written = sem("shared_in"), sem("f_chain"), sem("row_done"), sem("written")
        with nc.Block() as block:
            @block.sync
            def _(sp):
                sp.dma_start(shared[:], slot_out[0:N, :].rearrange("(t p) d -> p t d", p=P)).then_inc(shared_in, 16)
                for t in range(T):
                    sp.wait_ge(row_done, t + 1)
                    sp.dma_start(out[t * P:(t + 1) * P, :], x_rows[:, t, :]).then_inc(written, 16)
                sp.wait_ge(written, 16 * T)

            @block.gpsimd
            def _(pool):
                for t in range(T):
                    for c in range(TOP):
                        n = c * T + t
                        nc.gpsimd.indirect_dma_start(gathered[:, n, :], None, slot_out,
                                                     bass.IndirectOffsetOnAxis(ap=slot_i[:, n:n + 1], axis=0)
                                                     ).then_inc(slots_in[t], 16)

            @block.vector
            def _(dve):
                link = Chain(dve, f_chain)
                dve.wait_ge(shared_in, 16)
                for t in range(T):
                    link(nc.vector.tensor_tensor(x_rows[:, t, :], x_rows[:, t, :], shared[:, t, :], ALU.add))
                    dve.wait_ge(slots_in[t], 16 * TOP)
                    for c in range(TOP):
                        last = nc.vector.scalar_tensor_tensor(out=x_rows[:, t, :], in0=gathered[:, c * T + t, :],
                                                              scalar=topv[:, c, t:t + 1], in1=x_rows[:, t, :],
                                                              op0=ALU.mult, op1=ALU.add)
                        if c < TOP - 1:
                            link(last)
                    last.then_inc(row_done, 1)


def kernel(**inputs):
    import numpy as _np
    import concourse.bacc as _bacc
    from concourse import mybir as _mybir
    from concourse.bass_utils import run_bass_kernel_spmd as _run

    nc = _bacc.Bacc("TRN2", target_bir_lowering=False, num_devices=1)
    arrays, args = {}, {}
    for name in inputs:
        v = _np.ascontiguousarray(inputs[name])
        arrays[f"in_{name}"] = v
        args[name] = nc.dram_tensor(f"in_{name}", v.shape, _mybir.dt.from_np(v.dtype), kind="ExternalInput").ap()
    out = nc.dram_tensor("out_0", (N, D), F32, kind="ExternalOutput").ap()
    gnn_moe(nc, args, out)
    r = _run(nc, [arrays], core_ids=[0])
    return r.results[0]["out_0"]
```

```python
import concourse.bass as bass
from concourse import mybir
from contextlib import ExitStack, contextmanager

F32 = mybir.dt.float32
F16 = mybir.dt.float16
F32R = mybir.dt.float32r
I32 = mybir.dt.int32
ALU = mybir.AluOpType
ACT = mybir.ActivationFunctionType
AX = mybir.AxisListType

N, D, E_GNN = 625, 768, 20000
P, T = 125, 5
ET = E_GNN // P
HALF_ET = ET // 2
NI = -(-ET * T // 128) * 128
ITEM_TRASH = NI
KD = D // 128
HALF = D // 2
SLOPE, EPS = 0.2, 1e-5
ABSENT = -1e30
TRASH = N * N
G = 8
LAG = 5
REST = N - 512

X, FF = 16, 1536
TOP = 3
KF = FF // 128
S = 128
SHARED = (N + S - 1) // S
MAXT = SHARED + (N * TOP + X * (S - 1)) // S
MINT = SHARED + (N * TOP + S - 1) // S
NTAB = MAXT + 1


@contextmanager
def stage(nc):
    used = []

    def sem(name):
        used.append(nc.alloc_semaphore(name))
        return used[-1]

    with ExitStack() as memory:
        yield memory, sem
        nc.clear_and_free_semaphores(used)
        nc.all_engine_barrier()


class Chain:

    def __init__(self, engine, sem):
        self.engine, self.sem, self.n = engine, sem, 0

    def __call__(self, ins):
        self.n += 1
        ins.then_inc(self.sem, 1)
        self.engine.wait_ge(self.sem, self.n)


def gnn_moe(nc, a, out):
    top = ExitStack()
    with top:
        def sb(name, shape, dt=F32, ctx=top):
            return ctx.enter_context(nc.sbuf_tensor(name, shape, dt))

        def dram(name, shape, dt=F32):
            return nc.dram_tensor(name, shape, dt, kind="Internal").ap()

        psum = top.enter_context(nc.psum_tensor("psum", [128, 8 * 512], F32))
        bank = [psum[:, i * 512:(i + 1) * 512] for i in range(8)]
        x_rows = sb("x_rows", [P, T, D])
        ident = sb("ident", [128, 128])
        eps = sb("eps", [128, 1])
        before = sb("before", [P, P])
        ones = sb("ones", [P, P])
        slot_out = dram("slot_out", (NTAB * S, D))
        gnn = ExitStack()
        with gnn:
            graph_layers(nc, a, gnn, sb, dram, psum, bank, x_rows, ident, eps, before, ones, slot_out)
        moe = ExitStack()
        with moe:
            mixture(nc, a, out, moe, sb, dram, bank, x_rows, ident, eps, before, ones, slot_out)


def row_stats(nc, chain, src, width, stats, mv):
    parts = width // (384 if width == D else 512)
    step = width // parts
    for c in range(parts):
        last = nc.vector.bn_stats(stats[:, c, :], src[:, c * step:(c + 1) * step])
        if c < parts - 1:
            last.then_inc(chain.sem, 1)
            chain.n += 1
    chain(last)
    chain(nc.vector.bn_aggr(mv, stats[:, 0:parts, :].rearrange("p c s -> p (c s)")))


def graph_layers(nc, a, gnn, sb, dram, psum, bank, x_rows, ident, eps, before, ones, slot_out):
    def gb(name, shape, dt=F32):
        return sb(name, shape, dt, gnn)

    fs = gb("fs", [P, T, D])
    counts = gb("counts", [P, T, N])
    item_idx = gb("item_idx", [P, NI, 2], I32)
    item_key = gb("item_key", [P, NI])
    item_dst = gb("item_dst", [P, NI])
    tile_words = gb("tile_words", [1, NI // G], I32)
    octets = gb("octets", [1, 1], I32)
    part_iota = gb("part_iota", [P, 1])
    vecs = gb("vecs", [P, 5, D])
    attn_s = gb("attn_s", [P, 2, D])
    mv = gb("mv", [P, T, 2])
    stats = gb("stats", [P, 2, 6])
    std = gb("std", [P, T])
    rstd = gb("rstd", [P, T])
    key_col = gb("key_col", [P, G])

    def inputs(k):
        p = ("W1s", "W1d", "b1s", "b1d", "attn1", "ln1_w", "ln1_b") if k == 0 else \
            ("Wos", "Wod", "bos", "bod", "attno", "lno_w", "lno_b")
        return [a["L0_gnn_" + n] for n in p]

    heads = (8, 1)
    width = [D + max(h, 2) for h in heads]
    fd_hi = gb("fd_hi", [P, T, width[0]], F32R)
    fd_lo = gb("fd_lo", [P, T, width[0]], F32R)
    logit_tabs = [[dram(f"logit_tab{k}{u}", (N * N + P, heads[k])) for u in range(2)] for k in range(2)]
    fs_tab = [dram(f"fs_tab{k}", (N, width[k])) for k in range(2)]
    item_tab = dram("item_tab", (NI + HALF_ET, 3), I32)

    def node_tiles(pe, g):
        word = pe.value_load(tile_words[0:1, bass.ds(g, 1)], min_val=0, max_val=(T - 1) * (8 ** G - 1) // 7)
        return [((word >> (3 * u)) & 7).with_bounds(min_val=0, max_val=T - 1) for u in range(G)]

    with stage(nc) as (prep, sem):
        x_in_rows = sb("x_in_rows", [P, T, D], F32, prep)
        dst_i = sb("dst_i", [HALF_ET, 2, P], I32, prep)
        dst_f = sb("dst_f", [HALF_ET, 2, P], F32, prep)
        dst_tile = sb("dst_tile", [HALF_ET, 2, P], F32, prep)
        same = sb("same", [HALF_ET, 2, P], F32, prep)
        has = sb("has", [HALF_ET, T, 2], F32, prep)
        total = sb("i_total", [HALF_ET, 2 * T], F32, prep)
        until = sb("until", [HALF_ET, 2 * T], F32, prep)
        one_row = sb("one_row", [HALF_ET, 2 * T], F32, prep)
        row_trash = sb("row_trash", [HALF_ET, 1], F32, prep)
        at_f = sb("at_f", [HALF_ET, 2 * T], F32, prep)
        at_i = sb("at_i", [HALF_ET, 2 * T], I32, prep)
        triples = sb("triples", [HALF_ET, 2 * T, 3], I32, prep)
        no_item = sb("no_item", [128, NI // 128, 3], I32, prep)
        blocks_i = sb("blocks_i", [1, 2], I32, prep)
        items_f = sb("items_f", [1, 2], F32, prep)
        item_tile = sb("item_tile", [1, NI], F32, prep)
        words_f = sb("words_f", [1, NI // G], F32, prep)
        triple = sb("triple", [128, 3], I32, prep)
        triple_f = sb("triple_f", [128, 3], F32, prep)
        edge_trash = sb("edge_trash", [128, P], F32, prep)
        rows_i = sb("rows_i", [128, 2, P], I32, prep)
        rows_f = sb("rows_f", [128, 2, P], F32, prep)
        key = sb("key", [128, P], F32, prep)
        local = sb("local", [128, P], F32, prep)
        inside = sb("inside", [128, P], F32, prep)
        BLOCK_STEPS = 9
        go_dve = sem("p_go_dve")
        (x_in, dst_in, const_ok, prep_chain, prep_act, var_ok, pool_chain, has_ok, ranked,
         at_ok, no_item_in, listed, count_ok, go, triple_in, rows_in, cols_ok, turned, taken) = (
            sem(s) for s in ("x_in", "dst_in", "const_ok", "prep_chain", "prep_act",
                             "var_ok", "pool_chain", "has_ok", "ranked", "at_ok", "no_item_in", "listed",
                             "count_ok", "p_go", "triple_in", "rows_in", "i_cols_ok", "i_turned", "taken"))
        with nc.Block() as block:
            @block.sync
            def _(sp):
                for h in range(2):
                    sp.dma_start(dst_i[:, h, :], a["dst"][h * HALF_ET * P:(h + 1) * HALF_ET * P]
                                 .rearrange("(q p) -> q p", p=P)).then_inc(dst_in, 16)
                sp.dma_start(x_in_rows[:], a["x"].rearrange("(t p) d -> p t d", p=P)).then_inc(x_in, 16)

            @block.gpsimd
            def _(pool):
                link = Chain(pool, pool_chain)
                link(nc.gpsimd.memset(ones[:], 1.0))
                link(nc.gpsimd.affine_select(out=before[:], in_=ones[:], compare_op=ALU.is_gt, fill=0.0,
                                             base=0, pattern=[[1, P]], channel_multiplier=-1))
                link(nc.gpsimd.memset(no_item[:], 0))
                link(nc.gpsimd.memset(no_item[:, :, 2:3], T))
                link(nc.gpsimd.iota(triples[:, :, 0], pattern=[[0, T], [HALF_ET, 2]], base=0, channel_multiplier=1))
                link(nc.gpsimd.iota(triples[:, :, 1], pattern=[[1, T], [0, 2]], base=0, channel_multiplier=0))
                link(nc.gpsimd.iota(triples[:, :, 2], pattern=[[1, T], [0, 2]], base=0, channel_multiplier=0))
                link(nc.gpsimd.iota(row_trash[:], pattern=[[0, 1]], base=ITEM_TRASH, channel_multiplier=1,
                                    allow_small_or_imprecise_dtypes=True))
                link(nc.gpsimd.iota(edge_trash[:], pattern=[[1, P]], base=TRASH, channel_multiplier=0,
                                    allow_small_or_imprecise_dtypes=True))
                link(nc.gpsimd.iota(part_iota[:], pattern=[[0, 1]], base=0, channel_multiplier=1,
                                    allow_small_or_imprecise_dtypes=True))
                link(nc.gpsimd.memset(one_row[:], 1.0))
                link(nc.gpsimd.memset(item_idx[:], 0))
                link(nc.gpsimd.memset(item_key[:], 0.0))
                link(nc.gpsimd.memset(item_tile[:], 0.0))
                link(nc.gpsimd.memset(eps[:], EPS))
                link(nc.gpsimd.memset(ident[:], 0.0))
                nc.gpsimd.affine_select(out=ident[:], in_=ident[:], compare_op=ALU.not_equal, fill=1.0,
                                        base=0, pattern=[[-1, 128]], channel_multiplier=1).then_inc(const_ok, 1)
                pool.wait_ge(no_item_in, 16)
                pool.wait_ge(at_ok, 1)
                for n in range(2 * T):
                    if n:
                        pool.wait_ge(listed, 16 * n)
                    nc.gpsimd.indirect_dma_start(
                        item_tab, bass.IndirectOffsetOnAxis(ap=at_i[:, n:n + 1], axis=0),
                        triples[:, n, :], None).then_inc(listed, 16)
                pool.wait_ge(listed, 16 * 2 * T)
                blocks = pool.value_load(blocks_i[0:1, 0:1], min_val=ET // 128, max_val=NI // 128)
                with pool.Fori(0, blocks) as m:
                    pool.wait_ge(taken, 3 * m)
                    pool.sem_inc(go, 1)
                    nc.gpsimd.dma_start(triple[:], item_tab[bass.ds(m * 128, 128), :]).then_inc(triple_in, 16)
                    pool.wait_ge(triple_in, 16 * (m + 1))
                    pool.sem_inc(go, 1)
                    for c, name in enumerate(("src", "dst")):
                        nc.gpsimd.indirect_dma_start(
                            rows_i[:, c, :], None, a[name].rearrange("(n p) -> n p", p=P),
                            bass.IndirectOffsetOnAxis(ap=triple[:, 0:1], axis=0)).then_inc(rows_in, 16)

            @block.scalar
            def _(act):
                act.wait_ge(const_ok, 1)
                act.dma_start(item_tab[0:NI, :].rearrange("(g p) c -> p g c", p=128), no_item[:]).then_inc(no_item_in, 16)
                act.wait_ge(var_ok, 1)
                nc.scalar.activation(std[:], mv[:, :, 1], ACT.Sqrt, bias=eps[0:P, :]).then_inc(prep_act, 1)

            @block.tensor
            def _(pe):
                pe.wait_ge(const_ok, 1)
                pe.wait_ge(has_ok, 1)
                cols = has[:].rearrange("q t h -> q (t h)")
                nc.tensor.matmul(bank[0][0:HALF_ET, 0:2 * T], before[0:HALF_ET, 0:HALF_ET], cols, start=True, stop=True)
                nc.tensor.matmul(bank[1][0:HALF_ET, 0:2 * T], ones[0:HALF_ET, 0:HALF_ET], cols,
                                 start=True, stop=True).then_inc(ranked, 1)
                pe.wait_ge(count_ok, 1)
                blocks = pe.value_load(blocks_i[0:1, 0:1], min_val=ET // 128, max_val=NI // 128)
                with pe.Fori(0, blocks) as m:
                    pe.wait_ge(cols_ok, m + 1)
                    for c, rows in enumerate((rows_f[:, 0, :], key[:], local[:])):
                        nc.tensor.transpose(bank[2 + c][0:P, 0:128], rows, ident[:])
                    nc.tensor.transpose(bank[5][0:1, 0:128], triple_f[:, 1:2], ident[:]).then_inc(turned, 1)

            @block.vector
            def _(dve):
                link = Chain(dve, prep_chain)
                dve.wait_ge(dst_in, 32)
                link(nc.vector.tensor_copy(dst_f[:], dst_i[:]))
                link(nc.vector.tensor_scalar(dst_tile[:], dst_f[:], float(P), None, ALU.is_ge))
                for t in range(2, T):
                    link(nc.vector.scalar_tensor_tensor(out=dst_tile[:], in0=dst_f[:], scalar=float(t * P),
                                                        in1=dst_tile[:], op0=ALU.is_ge, op1=ALU.add))
                for t in range(T):
                    link(nc.vector.tensor_scalar(same[:], dst_tile[:], float(t), None, ALU.is_equal))
                    link(nc.vector.tensor_reduce(has[:, t, :], same[:], AX.X, ALU.max))
                nc.vector.tensor_copy(total[:], has[:].rearrange("q t h -> q (t h)")).then_inc(has_ok, 1)
                dve.wait_ge(has_ok, 1)
                dve.wait_ge(const_ok, 1)
                dve.wait_ge(ranked, 1)
                link(nc.vector.tensor_copy(total[:], bank[1][0:HALF_ET, 0:2 * T]))
                link(nc.vector.tensor_tensor_scan(until[:], one_row[:], total[:], 0.0, ALU.mult, ALU.add))
                link(nc.vector.tensor_scalar(items_f[:, 0:1], until[0:1, 2 * T - 1:2 * T], 127.0, None, ALU.add))
                link(nc.vector.tensor_scalar(items_f[:, 1:2], until[0:1, 2 * T - 1:2 * T], 7.0 - 2 * G, None, ALU.add))
                link(nc.vector.tensor_copy(blocks_i[:], items_f[:]))
                link(nc.vector.tensor_scalar(octets[:], blocks_i[:, 1:2], 3, None, ALU.arith_shift_right))
                link(nc.vector.tensor_scalar(blocks_i[:, 0:1], blocks_i[:, 0:1], 7, None, ALU.arith_shift_right))
                link(nc.vector.tensor_tensor(at_f[:], until[:], total[:], ALU.subtract))
                link(nc.vector.tensor_tensor(at_f[:], at_f[:], bank[0][0:HALF_ET, 0:2 * T], ALU.add))
                link(nc.vector.tensor_scalar(at_f[:], at_f[:], row_trash[:, 0:1], None, ALU.subtract))
                link(nc.vector.tensor_tensor(at_f[:], at_f[:], has[:].rearrange("q t h -> q (t h)"), ALU.mult))
                link(nc.vector.tensor_scalar(at_f[:], at_f[:], row_trash[:, 0:1], None, ALU.add))
                nc.vector.tensor_copy(at_i[:], at_f[:]).then_inc(at_ok, 1)
                nc.vector.memset(item_dst[:], -1.0).then_inc(count_ok, 1)
                dve.wait_ge(x_in, 16)
                for t in range(T):
                    row_stats(nc, link, x_in_rows[:, t, :], D, stats, mv[:, t, :])
                nc.vector.tensor_copy(stats[:, 0, :], stats[:, 1, :]).then_inc(var_ok, 1)
                dve.wait_ge(var_ok, 1)
                dve.wait_ge(prep_act, 1)
                link(nc.vector.reciprocal(rstd[:], std[:]))
                for t in range(T):
                    link(nc.vector.tensor_scalar(x_rows[:, t, :], x_in_rows[:, t, :], mv[:, t, 0:1],
                                                 rstd[:, t:t + 1], ALU.subtract, ALU.mult))
                blocks = dve.value_load(blocks_i[0:1, 0:1], min_val=ET // 128, max_val=NI // 128)
                with dve.Fori(0, blocks) as m:
                    step = iter(range(100))

                    def then(ins):
                        n = next(step)
                        ins.then_inc(go_dve, 1)
                        dve.wait_ge(go_dve, m * BLOCK_STEPS + n + 1)

                    dve.wait_ge(rows_in, 32 * (m + 1))
                    then(nc.vector.tensor_copy(rows_f[:], rows_i[:]))
                    then(nc.vector.tensor_copy(triple_f[:], triple[:]))
                    then(nc.vector.scalar_tensor_tensor(out=key[:], in0=rows_f[:, 1, :], scalar=float(N),
                                                        in1=rows_f[:, 0, :], op0=ALU.mult, op1=ALU.add))
                    then(nc.vector.tensor_scalar(triple_f[:, 2:3], triple_f[:, 2:3], float(P), None, ALU.mult))
                    then(nc.vector.tensor_scalar(local[:], rows_f[:, 1, :], triple_f[:, 2:3], None, ALU.subtract))
                    then(nc.vector.tensor_scalar(inside[:], local[:], float(P), None, ALU.is_lt))
                    then(nc.vector.scalar_tensor_tensor(out=inside[:], in0=local[:], scalar=0.0, in1=inside[:],
                                                        op0=ALU.is_ge, op1=ALU.mult))
                    then(nc.vector.tensor_tensor(key[:], key[:], edge_trash[:], ALU.subtract))
                    then(nc.vector.tensor_tensor(key[:], key[:], inside[:], ALU.mult))
                    nc.vector.tensor_tensor(key[:], key[:], edge_trash[:], ALU.add).then_inc(cols_ok, 1)
                    dve.wait_ge(turned, m + 1)
                    nc.vector.tensor_copy(item_idx[:, bass.ds(m * 128, 128), 0], bank[2][0:P, 0:128]).then_inc(taken, 1)
                    nc.vector.tensor_copy(item_key[:, bass.ds(m * 128, 128)], bank[3][0:P, 0:128])
                    nc.vector.tensor_copy(item_dst[:, bass.ds(m * 128, 128)], bank[4][0:P, 0:128]).then_inc(taken, 1)
                    nc.vector.tensor_copy(item_tile[:, bass.ds(m * 128, 128)], bank[5][0:1, 0:128]).then_inc(taken, 1)
                dve.wait_ge(taken, 3 * blocks)
                tiles_of = item_tile[:].rearrange("o (g u) -> o g u", u=G)
                link(nc.vector.tensor_copy(words_f[:], tiles_of[:, :, 0]))
                for u in range(1, G):
                    link(nc.vector.scalar_tensor_tensor(out=words_f[:], in0=tiles_of[:, :, u], scalar=float(8 ** u),
                                                        in1=words_f[:], op0=ALU.mult, op1=ALU.add))
                link(nc.vector.tensor_copy(tile_words[:], words_f[:]))

    with stage(nc) as (tally, sem):
        junk = sb("junk", [P, G, P], F32, tally)
        later = sb("later", [P, P], F32, tally)
        src_iota = sb("src_iota", [P, N], F16, tally)
        item_src = sb("item_src", [P, NI], F32, tally)
        repeats = sb("repeats", [P, NI], F32, tally)
        trash = sb("trash", [P, 1], F32, tally)
        hot = sb("hot", [P, G, N + P], F16, tally)
        zeros = sb("zeros", [P, 512], F16, tally)
        absent = sb("absent", [128, N * 8], F32, tally)
        absent_ok, tab_set = sem("t_absent_ok"), sem("t_tab_set")
        copied, copied_act = sem("copied"), sem("copied_act")
        (t_const, t_pool, t_chain, cols_ok, keys_turned, keys_read, hot_ok, counted, cleared) = (
            sem(s) for s in ("t_const", "t_pool", "t_chain", "cols_ok", "keys_turned", "keys_read", "hot_ok",
                             "counted", "cleared"))
        with nc.Block() as block:
            @block.sync
            def _(sp):
                sp.wait_ge(absent_ok, 1)
                for u in range(2):
                    tab0 = logit_tabs[0][u][0:N * N, :].rearrange("(t p s) h -> t p (s h)", t=T, p=P)
                    for t in range(T):
                        sp.dma_start(tab0[t], absent[0:P, :]).then_inc(tab_set, 16)
                    sp.dma_start(logit_tabs[1][u][0:N * N, :].rearrange("(p s) h -> p (s h)", p=P),
                                 absent[0:P, 0:N * T]).then_inc(tab_set, 16)
                row = MINT * S
                blocks = 0
                while row < NTAB * S:
                    per = min(6, (NTAB * S - row) // 128)
                    sp.dma_start(slot_out[row:row + 128 * per, :].rearrange("(p r) d -> p (r d)", p=128),
                                 absent[:, 0:per * D]).then_inc(tab_set, 16)
                    row += 128 * per
                    blocks += 1
                sp.wait_ge(tab_set, 16 * (2 * (T + 1) + blocks))

            @block.gpsimd
            def _(pool):
                link = Chain(pool, t_pool)
                link(nc.gpsimd.affine_select(out=later[:], in_=ones[:], compare_op=ALU.is_gt, fill=0.0,
                                             base=0, pattern=[[-1, P]], channel_multiplier=1))
                link(nc.gpsimd.iota(trash[:], pattern=[[0, 1]], base=TRASH, channel_multiplier=1,
                                    allow_small_or_imprecise_dtypes=True))
                link(nc.gpsimd.memset(zeros[:], 0.0))
                nc.gpsimd.iota(src_iota[:], pattern=[[1, N]], base=0, channel_multiplier=0,
                               allow_small_or_imprecise_dtypes=True).then_inc(t_const, 1)
                nc.gpsimd.memset(absent[:], ABSENT).then_inc(absent_ok, 1)

            @block.tensor
            def _(pe):
                pe.wait_ge(t_const, 1)
                for b in range(7):
                    last = nc.tensor.matmul(psum[0:P, b * 512:(b + 1) * 512], zeros[:, 0:P], zeros[:],
                                            start=True, stop=False, skip_group_check=True)
                n8 = pe.value_load(octets[0:1, 0:1], min_val=ET // G - 2, max_val=NI // G - 2) + 2
                with pe.Fori(0, n8) as g:
                    tiles = node_tiles(pe, g)
                    for h in range(2):
                        if h == 0:
                            pe.wait_ge(cols_ok, g + 1)
                        pe.wait_ge(keys_read, g * G + 4 * h)
                        for u in range(4):
                            last = nc.tensor.transpose(bank[7][0:P, u * P:(u + 1) * P],
                                                       key_col[:, 4 * h + u:4 * h + u + 1].to_broadcast([P, P]),
                                                       ident[0:P, 0:P])
                        last.then_inc(keys_turned, 1)
                        for u in range(4):
                            n = g * G + 4 * h + u
                            t = tiles[4 * h + u]
                            pe.wait_ge(hot_ok, 2 * (n + 1))
                            nc.tensor.matmul(psum[0:P, bass.ds(t * 512, 512)], hot[:, 4 * h + u, N:N + P],
                                             hot[:, 4 * h + u, 0:512], start=False, stop=False, skip_group_check=True)
                            nc.tensor.matmul(psum[0:P, bass.ds(t * 128 + 5 * 512, REST)], hot[:, 4 * h + u, N:N + P],
                                             hot[:, 4 * h + u, 512:N], start=False, stop=False,
                                             skip_group_check=True).then_inc(counted, 1)

            @block.scalar
            def _(act):
                n8 = act.value_load(octets[0:1, 0:1], min_val=ET // G - 2, max_val=NI // G - 2) + 2
                act.wait_ge(counted, n8 * G)
                for t in range(T):
                    nc.scalar.copy(counts[:, t, 0:512], psum[0:P, t * 512:(t + 1) * 512]).then_inc(copied_act, 1)
                act.wait_ge(copied_act, T)

            @block.vector
            def _(dve):
                link = Chain(dve, t_chain)
                dve.wait_ge(t_const, 1)
                link(nc.vector.tensor_copy(item_src[:], item_idx[:, :, 0]))
                link(nc.vector.memset(repeats[:], 0.0))
                n8 = dve.value_load(octets[0:1, 0:1], min_val=ET // G - 2, max_val=NI // G - 2) + 2

                def column(g):
                    nc.vector.tensor_copy(key_col[:], item_key[:, bass.ds(g * G, G)]).then_inc(cols_ok, 1)

                def one_hots(g, h, again):
                    if again:
                        dve.wait_ge(counted, (g - 1) * G + 4 * h + 4)
                    for u in range(4):
                        n = g * G + 4 * h + u
                        nc.vector.tensor_scalar(hot[:, 4 * h + u, 0:N], src_iota[:], item_src[:, bass.ds(n, 1)],
                                                None, ALU.is_equal).then_inc(hot_ok, 1)
                        nc.vector.tensor_scalar(hot[:, 4 * h + u, N:N + P], src_iota[:, 0:P],
                                                item_dst[:, bass.ds(n, 1)], None, ALU.is_equal).then_inc(hot_ok, 1)

                def find_repeats(g, h):
                    for u in range(4):
                        n = g * G + 4 * h + u
                        nc.vector.scalar_tensor_tensor(
                            out=junk[:, 4 * h + u, :], in0=bank[7][0:P, u * P:(u + 1) * P],
                            scalar=item_key[:, bass.ds(n, 1)], in1=later[:], op0=ALU.is_equal,
                            op1=ALU.mult, accum_out=repeats[:, bass.ds(n, 1)]).then_inc(keys_read, 1)

                def octet(g, again, final):
                    one_hots(g, 1, again)
                    dve.wait_ge(keys_turned, 2 * g + 1)
                    if again:
                        dve.wait_ge(keys_read, g * G)
                    find_repeats(g, 0)
                    if not final:
                        one_hots(g + 1, 0, True)
                    dve.wait_ge(keys_turned, 2 * g + 2)
                    if not final:
                        column(g + 1)
                    find_repeats(g, 1)

                column(0)
                one_hots(0, 0, False)
                octet(0, False, False)
                with dve.Fori(1, n8 - 1) as g:
                    octet(g, True, False)
                octet(n8 - 1, True, True)
                dve.wait_ge(keys_read, n8 * G)
                link(nc.vector.tensor_scalar(repeats[:], repeats[:], 1.0, None, ALU.min))
                link(nc.vector.tensor_scalar(item_src[:], item_key[:], -1.0, trash[:, 0:1], ALU.mult, ALU.add))
                link(nc.vector.tensor_tensor(item_src[:], item_src[:], repeats[:], ALU.mult))
                link(nc.vector.tensor_tensor(item_src[:], item_src[:], item_key[:], ALU.add))
                link(nc.vector.tensor_copy(item_idx[:, :, 1], item_src[:]))
                dve.wait_ge(counted, n8 * G)
                for t in range(T):
                    nc.vector.tensor_copy(counts[:, t, 512:N],
                                          psum[0:P, 5 * 512 + t * 128:5 * 512 + t * 128 + REST]).then_inc(copied, 1)
                dve.wait_ge(copied, T)

    for k in range(2):
        H = heads[k]
        HD = D // H
        W = width[k]
        Ws, Wd, bs, bd, attn, ln_w, ln_b = inputs(k)

        with stage(nc) as (project, sem):
            weights = sb(f"weights{k}", [128, 2, KD, D], F32, project)
            xT = sb(f"xT{k}", [128, KD, N], F32, project)
            table_rows = sb(f"table_rows{k}", [P, 2, 2, W], F32, project)
            prod = sb(f"prod{k}", [P, D], F32, project)
            w_in = [sem(f"w_in{k}{c}") for c in range(2)]
            vec_in, turned, xT_ok = sem(f"vec_in{k}"), sem(f"turned{k}"), sem(f"xT_ok{k}")
            proj_ok, proj_read = sem(f"proj_ok{k}"), sem(f"proj_read{k}")
            tab_row_ok, tab_out, pchain = sem(f"tab_row_ok{k}"), [sem(f"tab_out{k}{u}") for u in range(2)], sem(f"pchain{k}")
            with nc.Block() as block:
                @block.sync
                def _(sp):
                    for c, w in enumerate((Ws, Wd)):
                        sp.dma_start(weights[:, c], w.rearrange("(k p) n -> p k n", p=128)).then_inc(w_in[c], 16)
                    for t in range(T):
                        sp.wait_ge(tab_row_ok, 2 * t + 1)
                        sp.dma_start(fs_tab[k][t * P:(t + 1) * P, :], table_rows[:, t % 2, 0, :]).then_inc(tab_out[t % 2], 16)
                    for u in range(2):
                        sp.wait_ge(tab_out[u], 16 * len(range(u, T, 2)))

                @block.scalar
                def _(act):
                    for c, v in enumerate((bs, bd, attn, ln_w, ln_b)):
                        flat = v if len(v.shape) == 1 else v.rearrange("h d -> (h d)")
                        act.dma_start(vecs[:, c, :], flat.partition_broadcast(P)).then_inc(vec_in, 16)
                    for n in range(2 * T):
                        act.wait_ge(turned, n + 1)
                        t, h = divmod(n, 2)
                        nc.scalar.copy(xT[:, 3 * h:3 * h + 3, t * P:(t + 1) * P],
                                       bank[4 + n % 4][:, 0:3 * P].rearrange("p (k n) -> p k n", k=3)).then_inc(xT_ok, 1)

                @block.tensor
                def _(pe):
                    for n in range(2 * T):
                        t, h = divmod(n, 2)
                        if n >= 4:
                            pe.wait_ge(xT_ok, n - 3)
                        for u in range(3):
                            c = 3 * h + u
                            last = nc.tensor.transpose(bank[4 + n % 4][:, u * P:(u + 1) * P],
                                                       x_rows[:, t, c * 128:(c + 1) * 128], ident[0:P, 0:P])
                        last.then_inc(turned, 1)
                    for n in range(2 * T):
                        t, c = divmod(n, 2)
                        pe.wait_ge(xT_ok, 2 * t + 2)
                        pe.wait_ge(w_in[c], 16)
                        if n >= 2:
                            pe.wait_ge(proj_read, n - 1)
                        for h in range(2):
                            for kk in range(KD):
                                last = nc.tensor.matmul(bank[2 * (n % 2) + h][0:P, 0:HALF],
                                                        xT[:, kk, t * P:(t + 1) * P],
                                                        weights[:, c, kk, h * HALF:(h + 1) * HALF],
                                                        start=(kk == 0), stop=(kk == KD - 1))
                        last.then_inc(proj_ok, 1)

                @block.vector
                def _(dve):
                    link = Chain(dve, pchain)
                    dve.wait_ge(vec_in, 16 * 5)
                    link(nc.vector.tensor_scalar(attn_s[:, 0, :], vecs[:, 2, :], SLOPE, None, ALU.mult))
                    link(nc.vector.tensor_scalar(attn_s[:, 1, :], vecs[:, 2, :], 1.0 - SLOPE, None, ALU.mult))
                    if H == 1:
                        link(nc.vector.memset(table_rows[:, :, :, D:W], 0.0))
                    for n in range(2 * T):
                        t, c = divmod(n, 2)
                        dve.wait_ge(proj_ok, n + 1)
                        if t >= 2 and c == 0:
                            dve.wait_ge(tab_out[t % 2], 16 * (t // 2))
                        for h in range(2):
                            last = nc.vector.tensor_tensor(table_rows[:, t % 2, c, h * HALF:(h + 1) * HALF],
                                                           bank[2 * (n % 2) + h][0:P, 0:HALF],
                                                           vecs[:, c, h * HALF:(h + 1) * HALF], ALU.add)
                            if h == 0:
                                link(last)
                        last.then_inc(proj_read, 1)
                        dve.wait_ge(proj_read, n + 1)
                        row = table_rows[:, t % 2, c, 0:D]
                        if c == 0:
                            link(nc.vector.tensor_copy(fs[:, t, :], row))
                        link(nc.vector.tensor_tensor(prod[:], row, attn_s[:, 0, :], ALU.mult))
                        nc.vector.tensor_reduce(table_rows[:, t % 2, c, D:D + H],
                                                prod[:].rearrange("p (h d) -> p h d", h=H),
                                                AX.X, ALU.add).then_inc(tab_row_ok, 1)
                        dve.wait_ge(tab_row_ok, n + 1)
                        if c == 1:
                            link(nc.vector.tensor_copy(fd_hi[:, t, 0:W], table_rows[:, t % 2, c, :]))
                            link(nc.vector.tensor_tensor(fd_lo[:, t, 0:W], table_rows[:, t % 2, c, :],
                                                         fd_hi[:, t, 0:W].bitcast(F32), ALU.subtract))

        with stage(nc) as (edges, sem):
            z = sb(f"z{k}", [P, G, W], F32, edges)
            logit = sb(f"logit{k}", [P, G, H], F32, edges)
            idx = sb(f"idx{k}", [P, G, 2], I32, edges)
            pick = sb(f"pick{k}", [P, G, P], F32R, edges)
            relu = sb(f"relu{k}", [P, 2, D], F32, edges)
            part = sb(f"part{k}", [P, 4, H], F32, edges)
            (go, logit_ok, relu_ok, part_ok, cols_ok, dst_turned, pick_ok, picked, z_ok) = (
                sem(f"{s}{k}") for s in ("go", "logit_ok", "relu_ok", "part_ok", "cols_ok",
                                         "dst_turned", "pick_ok", "picked", "z_ok"))
            sum_in = [sem(f"sum_in{k}{u}") for u in range(G)]
            scattered = [sem(f"scattered{k}{u}") for u in range(2)]

            def octet_count(eng):
                return eng.value_load(octets[0:1, 0:1], min_val=ET // G - 2, max_val=NI // G - 2) + 2

            with nc.Block() as block:
                @block.gpsimd
                def _(pool):
                    def add_source(u, n):
                        pool.wait_ge(z_ok, 3 * (n + 1))
                        nc.gpsimd.sem_inc(go, 1)
                        nc.gpsimd.indirect_dma_start(
                            z[:, u, :], None, fs_tab[k],
                            bass.IndirectOffsetOnAxis(ap=idx[:, u, 0:1], axis=0),
                            compute_op=ALU.add).then_inc(sum_in[u], 16)

                    def scatter(u, n, before):
                        pool.wait_ge(logit_ok, n + 1)
                        if before is not None:
                            pool.wait_ge(scattered[u % 2], before * 16)
                        nc.gpsimd.sem_inc(go, 1)
                        nc.gpsimd.indirect_dma_start(
                            logit_tabs[k][u % 2], bass.IndirectOffsetOnAxis(ap=idx[:, u, 1:2], axis=0),
                            logit[:, u, :], None).then_inc(scattered[u % 2], 16)

                    n8 = octet_count(pool)
                    for u in range(G):
                        add_source(u, u)
                        if u >= LAG:
                            scatter(u - LAG, u - LAG, (u - LAG) // 2 or None)
                    with pool.Fori(1, n8) as g:
                        for u in range(G):
                            add_source(u, g * G + u)
                            scatter((u - LAG) % G, g * G + u - LAG, g * (G // 2) + (u - LAG) // 2)
                    for u in range(G - LAG, G):
                        scatter(u, n8 * G + (u - G), n8 * (G // 2) + (u - G) // 2)
                    for c in range(2):
                        pool.wait_ge(scattered[c], n8 * (16 * G // 2))
                    pool.sem_inc(go, 1)

                @block.tensor
                def _(pe):
                    def turn(g, h):
                        if h == 0:
                            pe.wait_ge(cols_ok, g + 1)
                        pe.wait_ge(pick_ok, 2 * g)
                        for u in range(4):
                            last = nc.tensor.transpose(bank[6 + h][0:P, u * P:(u + 1) * P],
                                                       key_col[:, 4 * h + u:4 * h + u + 1].to_broadcast([P, P]),
                                                       ident[0:P, 0:P])
                        last.then_inc(dst_turned, 1)

                    def rows(g, u, t, again):
                        n = g * G + u
                        pe.wait_ge(pick_ok, 2 * g + u // 4 + 1)
                        if again or u >= 2:
                            pe.wait_ge(z_ok, 3 * (n - 1))
                        b = 2 * (u % 2)
                        for lo, hi in ((0, 512), (512, W)):
                            for part_, (start, stop) in ((fd_hi, (True, False)), (fd_lo, (False, True))):
                                last = nc.tensor.matmul(
                                    bank[b + lo // 512][0:P, 0:hi - lo], pick[:, u, :],
                                    part_[:, bass.ds(t, 1), lo:hi].rearrange("p o d -> p (o d)"),
                                    start=start, stop=stop)
                        last.then_inc(picked, 1)

                    n8 = octet_count(pe)
                    turn(0, 0)
                    turn(0, 1)
                    tiles = node_tiles(pe, 0)
                    for u in range(G):
                        rows(0, u, tiles[u], False)
                    with pe.Fori(1, n8) as g:
                        tiles = node_tiles(pe, g)
                        turn(g, 0)
                        turn(g, 1)
                        for u in range(G):
                            rows(g, u, tiles[u], True)

                @block.scalar
                def _(act):
                    def fill(u, n, g, again):
                        if again:
                            act.wait_ge(scattered[u % 2], (g * (G // 2) + u // 2 + 1 - G // 2) * 16)
                        nc.scalar.copy(idx[:, u, :], item_idx[:, bass.ds(n, 1), :]
                                       .rearrange("p o c -> p (o c)")).then_inc(z_ok, 1)
                        act.wait_ge(picked, n + 1)
                        b = 2 * (u % 2)
                        nc.scalar.copy(z[:, u, 0:512], bank[b][0:P, :]).then_inc(z_ok, 1)
                        nc.scalar.copy(z[:, u, 512:W], bank[b + 1][0:P, 0:W - 512]).then_inc(z_ok, 1)

                    n8 = octet_count(act)
                    for u in range(G):
                        fill(u, u, 0, False)
                    with act.Fori(1, n8) as g:
                        for u in range(G):
                            fill(u, g * G + u, g, True)

                @block.vector
                def _(dve):
                    def columns(g):
                        dve.wait_ge(dst_turned, 2 * g)
                        nc.vector.tensor_copy(key_col[:], item_dst[:, bass.ds(g * G, G)]).then_inc(cols_ok, 1)

                    def one_hot(g, h, again):
                        dve.wait_ge(dst_turned, 2 * g + h + 1)
                        if again:
                            dve.wait_ge(picked, (g - 1) * G + 4 * h + 4)
                        nc.vector.tensor_scalar(pick[:, 4 * h:4 * h + 4, :].rearrange("q u e -> q (u e)"),
                                                bank[6 + h][0:P, 0:4 * P], part_iota[:, 0:1], None,
                                                ALU.is_equal).then_inc(pick_ok, 1)

                    def products(u, n, g):
                        dve.wait_ge(sum_in[u], g * 16 + 16)
                        b = u % 2
                        if H == 1:
                            nc.vector.scalar_tensor_tensor(out=relu[:, b, :], in0=z[:, u, 0:D], scalar=0.0,
                                                           in1=attn_s[:, 1, :], op0=ALU.max, op1=ALU.mult,
                                                           accum_out=part[:, u % 4, :]).then_inc(part_ok, 1)
                        else:
                            nc.vector.scalar_tensor_tensor(out=relu[:, b, :], in0=z[:, u, 0:D], scalar=0.0,
                                                           in1=attn_s[:, 1, :], op0=ALU.max,
                                                           op1=ALU.mult).then_inc(relu_ok, 1)

                    def head_sums(u, n):
                        dve.wait_ge(relu_ok, n + 1)
                        nc.vector.tensor_reduce(part[:, u % 4, :], relu[:, u % 2, :].rearrange("p (h d) -> p h d", h=H),
                                                AX.X, ALU.add).then_inc(part_ok, 1)

                    def logits(u, n, g, again):
                        dve.wait_ge(part_ok, n + 1)
                        if again:
                            dve.wait_ge(scattered[u % 2], (g * (G // 2) + u // 2 + 1 - G // 2) * 16)
                        nc.vector.tensor_tensor(logit[:, u, :], part[:, u % 4, :], z[:, u, D:D + H],
                                                ALU.add).then_inc(logit_ok, 1)

                    def octet(g, first, second, final):
                        if not final:
                            columns(g + 1)
                        for u in range(G):
                            n = g * G + u
                            if u >= 2 or not first:
                                dve.wait_ge(part_ok, n - 1)
                            if H == 1 and (u >= 4 or not first):
                                dve.wait_ge(logit_ok, n - 3)
                            products(u, n, g)
                            if H > 1 and (u or not first):
                                if u >= 5 or not first:
                                    dve.wait_ge(logit_ok, n - 4)
                                head_sums((u - 1) % G, n - 1)
                            if u >= 2:
                                logits(u - 2, n - 2, g, not first)
                            elif not first:
                                logits(u - 2 + G, n - 2, g - 1, not second)
                            if u in (3, 5) and not final:
                                one_hot(g + 1, u // 4, True)

                    n8 = octet_count(dve)
                    columns(0)
                    one_hot(0, 0, False)
                    one_hot(0, 1, False)
                    octet(0, True, False, False)
                    octet(1, False, True, False)
                    with dve.Fori(2, n8 - 1) as g:
                        octet(g, False, False, False)
                    octet(n8 - 1, False, False, True)
                    last = n8 * G - 1
                    dve.wait_ge(logit_ok, last - 1)
                    if H > 1:
                        head_sums(G - 1, last)
                    logits(G - 2, last - 1, n8 - 1, True)
                    logits(G - 1, last, n8 - 1, True)

        with stage(nc) as (attend, sem):
            LEAD, RING = min(3, H), 6
            HEADS = T * H
            BEHIND = 1 if H > 1 else 2
            FINISH = min(3, H - 1)
            pair = sb(f"pair{k}", [P, 2, N, H], F32, attend)
            odd = sb(f"odd{k}", [P, N, H], F32, attend)
            prob = sb(f"prob{k}", [P, RING, N], F32, attend)
            probT = sb(f"probT{k}", [P, 2, T, P], F32, attend)
            negmax = sb(f"negmax{k}", [P, 2, H], F32, attend)
            den = sb(f"den{k}", [P, 3, H], F32, attend)
            rden = sb(f"rden{k}", [P, H], F32, attend)
            o = sb(f"o{k}", [P, D], F32, attend)
            o_neg = sb(f"o_neg{k}", [P, D], F32, attend)
            pair_in = [sem(f"pair_in{k}{u}") for u in range(2)]
            pair_ok = sem(f"pair_ok{k}")
            normed = sem(f"normed{k}")
            x_in_again, shifted = sem(f"x_in_again{k}"), sem(f"shifted{k}")
            if k == 1:
                x_and_b = sb("x_and_b", [P, T, D], F32, attend)
            max_ok, exp_ok, prob_ok, turned, probT_ok, summed, achain, neg_ok, elu_ok, std_ok, mul_ok, var_ok = (
                sem(f"{s}{k}") for s in ("max_ok", "exp_ok", "prob_ok", "p_turned", "probT_ok", "summed", "achain",
                                         "neg_ok", "elu_ok", "std_ok", "mul_ok", "a_var_ok"))
            with nc.Block() as block:
                @block.sync
                def _(sp):
                    tabs = [tab[0:N * N, :].rearrange("(t p s) h -> t p (s h)", t=T, p=P) for tab in logit_tabs[k]]
                    for t in range(T):
                        if t >= 2:
                            sp.wait_ge(exp_ok, (t - 1) * H)
                        sp.dma_start(pair[:, t % 2].rearrange("p s h -> p (s h)"), tabs[0][t]).then_inc(pair_in[t % 2], 16)
                        if t:
                            sp.wait_ge(pair_ok, t)
                        sp.dma_start(odd[:].rearrange("p s h -> p (s h)"), tabs[1][t]).then_inc(pair_in[t % 2], 16)
                    if k == 1:
                        sp.dma_start(x_and_b[:], a["x"].rearrange("(t p) d -> p t d", p=P)).then_inc(x_in_again, 16)

                @block.tensor
                def _(pe):
                    def turn(n):
                        b = 4 + 2 * (n % 2)
                        pe.wait_ge(prob_ok, n + 1)
                        if n >= 2:
                            pe.wait_ge(probT_ok, 2 * (n - 1))
                        for c in range(T):
                            to = bank[b][0:P, c * P:(c + 1) * P] if c < 4 else bank[b + 1][0:P, 0:P]
                            last = nc.tensor.transpose(to, prob[:, n % RING, c * P:(c + 1) * P], ident[0:P, 0:P])
                        last.then_inc(turned, 1)

                    def weighted_sum(n):
                        t, h = divmod(n, H)
                        pe.wait_ge(probT_ok, 2 * (n + 1))
                        if t >= 2 and h == 0:
                            pe.wait_ge(mul_ok, 2 * (t - 1))
                        for lo, w in ([(h * HD, HD)] if H > 1 else [(0, HALF), (HALF, HALF)]):
                            for c in range(T):
                                last = nc.tensor.matmul(
                                    bank[2 * (t % 2) + lo // HALF][0:P, lo % HALF:lo % HALF + w],
                                    probT[:, n % 2, c, :], fs[:, c, lo:lo + w], start=(c == 0), stop=(c == T - 1))
                        last.then_inc(summed, 1)

                    turn(0)
                    for n in range(HEADS):
                        if n + 1 < HEADS:
                            turn(n + 1)
                        weighted_sum(n)

                @block.scalar
                def _(act):
                    def exps(n):
                        t, h = divmod(n, H)
                        act.wait_ge(max_ok, t + 1)
                        if n >= RING:
                            act.wait_ge(turned, n - RING + 1)
                        nc.scalar.activation(prob[:, n % RING, :], pair[:, t % 2, :, h], ACT.Exp,
                                             bias=negmax[:, t % 2, h:h + 1]).then_inc(exp_ok, 1)

                    def copy_turned(n):
                        act.wait_ge(turned, n + 1)
                        if n >= 2:
                            act.wait_ge(summed, n - 1)
                        b = 4 + 2 * (n % 2)
                        nc.scalar.copy(probT[:, n % 2, 0:4, :].rearrange("p c q -> p (c q)"),
                                       bank[b][0:P, 0:4 * P]).then_inc(probT_ok, 1)
                        nc.scalar.copy(probT[:, n % 2, 4, :], bank[b + 1][0:P, 0:P]).then_inc(probT_ok, 1)

                    def elu(t):
                        act.wait_ge(neg_ok, t + 1)
                        nc.scalar.activation(o_neg[:], o_neg[:], ACT.Exp).then_inc(elu_ok, 1)

                    for n in range(LEAD):
                        exps(n)
                    for n in range(HEADS):
                        if n + LEAD < HEADS:
                            exps(n + LEAD)
                        copy_turned(n)
                        if n >= BEHIND * H and n % H == FINISH:
                            elu(n // H - BEHIND)
                    for t in range(T - BEHIND, T):
                        elu(t)
                    act.wait_ge(var_ok, 1)
                    nc.scalar.activation(std[:], mv[:, :, 1], ACT.Sqrt, bias=eps[0:P, :]).then_inc(std_ok, 1)

                @block.vector
                def _(dve):
                    link = Chain(dve, achain)

                    def merge(t):
                        dve.wait_ge(pair_in[t % 2], 32 * (t // 2 + 1))
                        nc.vector.tensor_tensor(pair[:, t % 2], pair[:, t % 2], odd[:], ALU.max).then_inc(pair_ok, 1)

                    def maxima(t):
                        dve.wait_ge(pair_ok, t + 1)
                        if t >= 2:
                            dve.wait_ge(exp_ok, (t - 1) * H)
                        nc.vector.tensor_reduce(negmax[:, t % 2, :], pair[:, t % 2].rearrange("p s h -> p h s"),
                                                AX.X, ALU.max, negate=True).then_inc(max_ok, 1)

                    def weigh(n):
                        t, h = divmod(n, H)
                        dve.wait_ge(exp_ok, n + 1)
                        nc.vector.tensor_tensor_reduce(prob[:, n % RING, :], prob[:, n % RING, :], counts[:, t, :],
                                                       1.0, 0.0, ALU.mult, ALU.add,
                                                       den[:, t % 3, h:h + 1]).then_inc(prob_ok, 1)

                    def finish(t):
                        dve.wait_ge(prob_ok, (t + 1) * H)
                        link(nc.vector.tensor_scalar(rden[:], den[:, t % 3, :], 1e-30, None, ALU.max))
                        link(nc.vector.reciprocal(rden[:], rden[:]))
                        dve.wait_ge(summed, (t + 1) * H)
                        for c in range(2):
                            hh = max(H // 2, 1)
                            scale = rden[:, (c * hh) % H:(c * hh) % H + hh]
                            nc.vector.tensor_tensor(
                                o[:, c * HALF:(c + 1) * HALF].rearrange("p (h d) -> p h d", h=hh),
                                bank[2 * (t % 2) + c][0:P, 0:HALF].rearrange("p (h d) -> p h d", h=hh),
                                scale.unsqueeze(2).to_broadcast([P, hh, HALF // hh]), ALU.mult).then_inc(mul_ok, 1)
                        dve.wait_ge(mul_ok, 2 * t + 2)
                        nc.vector.tensor_scalar(o_neg[:], o[:], 0.0, None, ALU.min).then_inc(neg_ok, 1)
                        dve.wait_ge(elu_ok, t + 1)
                        link(nc.vector.scalar_tensor_tensor(out=o[:], in0=o[:], scalar=0.0, in1=o_neg[:],
                                                            op0=ALU.max, op1=ALU.add))
                        if k == 0:
                            link(nc.vector.scalar_tensor_tensor(out=x_rows[:, t, :], in0=o[:], scalar=-1.0,
                                                                in1=x_rows[:, t, :], op0=ALU.add, op1=ALU.add))
                        else:
                            link(nc.vector.tensor_scalar(x_rows[:, t, :], o[:], -1.0, None, ALU.add))
                        row_stats(nc, link, x_rows[:, t, :], D, stats, mv[:, t, :])
                        link(nc.vector.scalar_tensor_tensor(out=x_rows[:, t, :], in0=x_rows[:, t, :], scalar=mv[:, t, 0:1],
                                                            in1=vecs[:, 3, :], op0=ALU.subtract, op1=ALU.mult))

                    merge(0)
                    maxima(0)
                    for n in range(HEADS):
                        t, h = divmod(n, H)
                        if h == FINISH and t + 1 < T:
                            merge(t + 1)
                        if h == min(5, H - 1) and t + 1 < T:
                            maxima(t + 1)
                        weigh(n)
                        if t >= BEHIND and h == FINISH:
                            finish(t - BEHIND)
                    if k == 1:
                        dve.wait_ge(x_in_again, 16)
                        for t in range(T):
                            nc.vector.tensor_tensor(x_and_b[:, t, :], x_and_b[:, t, :], vecs[:, 4, :],
                                                    ALU.add).then_inc(shifted, 1)
                    for t in range(T - BEHIND, T):
                        finish(t)
                    nc.vector.tensor_copy(stats[:, 0, :], stats[:, 1, :]).then_inc(var_ok, 1)
                    dve.wait_ge(var_ok, 1)
                    dve.wait_ge(std_ok, 1)
                    link(nc.vector.reciprocal(rstd[:], std[:]))
                    if k == 1:
                        dve.wait_ge(shifted, T)
                    for t in range(T):
                        nc.vector.scalar_tensor_tensor(out=x_rows[:, t, :], in0=x_rows[:, t, :],
                                                       scalar=rstd[:, t:t + 1],
                                                       in1=vecs[:, 4, :] if k == 0 else x_and_b[:, t, :],
                                                       op0=ALU.mult, op1=ALU.add).then_inc(normed, 1)
                    dve.wait_ge(normed, T)


def mixture(nc, a, out, moe, sb, dram, bank, x_rows, ident, eps, before, ones, slot_out):
    def mb(name, shape, dt=F32):
        return sb(name, shape, dt, moe)

    gate_w, gate_b, fc1_w, fc1_b, ln_w, ln_b, fc2_w, fc2_b = (
        a["L0_ffn_" + n] for n in ("gate_w", "gate_b", "fc1_w", "fc1_b", "ln_w", "ln_b", "fc2_w", "fc2_b"))
    token_rows = dram("token_rows", (N, D))
    slot_token = dram("slot_token", (NTAB * S, 1), I32)
    choice_token = [dram(f"choice_token{c}", (NTAB * S, 1), I32) for c in range(TOP)]

    topv = mb("topv", [P, TOP, T])
    slot_i = mb("slot_i", [P, TOP * T], I32)
    tile_expert = mb("tile_expert", [1, NTAB], I32)
    tile_group = mb("tile_group", [1, NTAB], I32)
    group_expert = mb("group_expert", [1, X + 1], I32)
    group_before = mb("group_before", [1, X + 1], I32)
    last_tile = mb("last_tile", [1, 1], I32)
    last_group = mb("last_group", [1, 1], I32)

    RAW = 3
    EARLY, LATE = range(RAW), range(RAW, KD)
    weights = ExitStack()
    w1_in_rows = sb("w1_in_rows", [128, RAW, FF], F32, weights)
    w1_hi = sb("w1_hi", [128, KD, FF], F32R, weights)
    w1_lo = sb("w1_lo", [128, KD, FF], F32R, weights)
    w2 = sb("w2", [128, KF, D], F32, weights)

    def first_part(c):
        return nc.scalar.copy(w1_hi[:, c, :], w1_in_rows[:, c % RAW, :])

    def second_part(c):
        return nc.vector.tensor_tensor(w1_lo[:, c, :], w1_in_rows[:, c % RAW, :], w1_hi[:, c, :].bitcast(F32),
                                       ALU.subtract)

    with stage(nc) as (route, sem):
        def rb(name, shape, dt=F32):
            return sb(name, shape, dt, route)

        xf = rb("xf", [P, T, D])
        xfT = rb("xfT", [128, KD, N])
        gw = rb("gw", [128, KD, X])
        gbias = rb("gbias", [P, X])
        mv, stats = rb("r_mv", [P, T, 2]), rb("r_stats", [P, 2, 6])
        std, rstd = rb("r_std", [P, T]), rb("r_rstd", [P, T])
        pr = rb("pr", [P, T, X])
        m = rb("m", [P, T])
        eq = rb("eq", [P, T, X])
        chosen = rb("chosen", [P, TOP, T, X])
        sel = rb("sel", [P, T, X])
        pos = rb("pos", [P, T, X])
        total = rb("total", [P, X])
        tiles = rb("tiles", [P, X])
        more = rb("more", [P, X])
        ends = rb("tile_ends", [P, X])
        one_x = rb("one_x", [P, X])
        iota_x = rb("iota_x", [P, X])
        iota_j = rb("iota_j", [1, NTAB])
        at_or_past = rb("at_or_past", [1, NTAB, X])
        expert_f = rb("expert_f", [1, NTAB])
        some = rb("some", [P, X])
        ordinal = rb("ordinal", [P, X])
        in_group = rb("in_group", [1, X + 1, X])
        weighted = rb("weighted", [1, X + 1, X])
        group_f = rb("group_f", [1, X + 1])
        slot_f = rb("slot_f", [P, TOP, T])
        token_id = rb("token_id", [P, T], I32)
        first_f = rb("first_f", [NTAB, S])
        row_is_shared = rb("row_is_shared", [NTAB, S])
        first_i = rb("first_i", [NTAB, S], I32)
        zero_i = rb("zero_i", [NTAB, S], I32)
        parts = rb("parts", [NTAB, TOP, S], I32)
        parts_in, merged, merged_out = sem("parts_in"), sem("merged"), sem("merged_out")
        scattered = [sem(f"choice_out{c}") for c in range(TOP)]
        w1_here, w2_here, hi_here, lo_here = [sem("w1_here0"), sem("w1_here1")], sem("w2_here"), sem("hi_here"), sem("lo_here")
        g_in, r_chain, r_var, r_std, xf_ok, x_out = (sem(s) for s in ("g_in", "r_chain", "r_var", "r_std_ok", "xf_ok", "x_out"))
        r_turned, xfT_ok, score_ok, sel_ok, pos_ok, exp_in, exp_out, r_const, r_pool = (
            sem(s) for s in ("r_turned", "xfT_ok", "score_ok", "sel_ok", "pos_ok", "exp_in", "exp_out", "r_const", "r_pool"))
        first_ok, first_out, slots_ok = (sem(s) for s in ("first_ok", "first_out", "slots_ok"))
        with nc.Block() as block:
            @block.sync
            def _(sp):
                sp.dma_start(gw[:], gate_w.rearrange("(k p) e -> p k e", p=128)).then_inc(g_in, 16)
                sp.dma_start(gbias[:], gate_b.partition_broadcast(P)).then_inc(g_in, 16)
                for c in EARLY:
                    sp.dma_start(w1_in_rows[:, c, :], fc1_w[0, c * 128:(c + 1) * 128, :]).then_inc(w1_here[0], 16)
                sp.wait_ge(first_ok, 1)
                for c in range(TOP):
                    sp.dma_start(choice_token[c].rearrange("(j s) o -> j (s o)", s=S),
                                 (zero_i if c else first_i)[:]).then_inc(first_out, 16)
                sp.wait_ge(xf_ok, T)
                sp.dma_start(token_rows.rearrange("(t p) d -> p t d", p=P), xf[:]).then_inc(x_out, 16)
                for c in range(KD):
                    sp.dma_start(w2[:, 2 * c:2 * c + 2, :], fc2_w[0, c * 256:(c + 1) * 256, :]
                                 .rearrange("(k p) n -> p k n", p=128)).then_inc(w2_here, 16)
                for c in LATE:
                    sp.wait_ge(lo_here, c + 1 - RAW)
                    sp.dma_start(w1_in_rows[:, c % RAW, :], fc1_w[0, c * 128:(c + 1) * 128, :]).then_inc(w1_here[1], 16)
                sp.wait_ge(w2_here, 16 * KD)
                for c in range(TOP):
                    sp.wait_ge(scattered[c], 16 * T)
                    sp.dma_start(parts[:, c, :], choice_token[c].rearrange("(j s) o -> j (s o)", s=S)).then_inc(parts_in, 16)
                sp.wait_ge(merged, 1)
                sp.dma_start(slot_token.rearrange("(j s) o -> j (s o)", s=S), first_i[:]).then_inc(merged_out, 16)
                sp.wait_ge(merged_out, 16)
                sp.wait_ge(x_out, 16)

            @block.gpsimd
            def _(pool):
                link = Chain(pool, r_pool)
                link(nc.gpsimd.iota(iota_x[:], pattern=[[1, X]], base=0, channel_multiplier=0,
                                    allow_small_or_imprecise_dtypes=True))
                link(nc.gpsimd.iota(iota_j[:], pattern=[[1, NTAB]], base=0, channel_multiplier=0,
                                    allow_small_or_imprecise_dtypes=True))
                link(nc.gpsimd.iota(token_id[:], pattern=[[P, T]], base=0, channel_multiplier=1))
                link(nc.gpsimd.iota(first_f[:], pattern=[[1, S]], base=0, channel_multiplier=S,
                                    allow_small_or_imprecise_dtypes=True))
                link(nc.gpsimd.memset(one_x[:], 1.0))
                nc.gpsimd.memset(row_is_shared[:], 1.0).then_inc(r_const, 1)
                pool.wait_ge(first_out, 16 * TOP)
                pool.wait_ge(slots_ok, 1)
                for t in range(T):
                    for c in range(TOP):
                        n = c * T + t
                        if t:
                            pool.wait_ge(scattered[c], 16 * t)
                        nc.gpsimd.indirect_dma_start(
                            choice_token[c], bass.IndirectOffsetOnAxis(ap=slot_i[:, n:n + 1], axis=0),
                            token_id[:, t:t + 1], None).then_inc(scattered[c], 16)

            @block.scalar
            def _(act):
                act.wait_ge(w1_here[0], 16 * len(EARLY))
                for c in EARLY:
                    first_part(c).then_inc(hi_here, 1)
                act.wait_ge(r_var, 1)
                nc.scalar.activation(std[:], mv[:, :, 1], ACT.Sqrt, bias=eps[0:P, :]).then_inc(r_std, 1)
                for n in range(2 * T):
                    t, h = divmod(n, 2)
                    act.wait_ge(r_turned, n + 1)
                    nc.scalar.copy(xfT[:, 3 * h:3 * h + 3, t * P:(t + 1) * P],
                                   bank[n % 4][:, 0:3 * P].rearrange("p (k n) -> p k n", k=3)).then_inc(xfT_ok, 1)
                act.wait_ge(exp_in, 1)
                nc.scalar.activation(pr[:], pr[:], ACT.Exp).then_inc(exp_out, 1)
                act.wait_ge(w1_here[1], 16 * len(LATE))
                for c in LATE:
                    first_part(c).then_inc(hi_here, 1)

            @block.tensor
            def _(pe):
                for n in range(2 * T):
                    t, h = divmod(n, 2)
                    pe.wait_ge(xf_ok, t + 1)
                    if n >= 4:
                        pe.wait_ge(xfT_ok, n - 3)
                    for u in range(3):
                        c = 3 * h + u
                        last = nc.tensor.transpose(bank[n % 4][:, u * P:(u + 1) * P],
                                                   xf[:, t, c * 128:(c + 1) * 128], ident[0:P, 0:P])
                    last.then_inc(r_turned, 1)
                pe.wait_ge(g_in, 32)
                for t in range(T):
                    pe.wait_ge(xfT_ok, 2 * t + 2)
                    for c in range(KD):
                        last = nc.tensor.matmul(bank[4][0:P, t * X:(t + 1) * X], xfT[:, c, t * P:(t + 1) * P],
                                                gw[:, c, :], start=(c == 0), stop=(c == KD - 1))
                last.then_inc(score_ok, 1)
                pe.wait_ge(sel_ok, 1)
                for t in range(T):
                    for c in range(t + 1):
                        last = nc.tensor.matmul(bank[5][0:P, t * X:(t + 1) * X], before[:] if c == t else ones[:],
                                                sel[:, c, :], start=(c == 0), stop=(c == t))
                for c in range(T):
                    last = nc.tensor.matmul(bank[6][0:P, 0:X], ones[:], sel[:, c, :], start=(c == 0), stop=(c == T - 1))
                last.then_inc(pos_ok, 1)

            @block.vector
            def _(dve):
                link = Chain(dve, r_chain)
                for t in range(T):
                    row_stats(nc, link, x_rows[:, t, :], D, stats, mv[:, t, :])
                nc.vector.tensor_copy(stats[:, 0, :], stats[:, 1, :]).then_inc(r_var, 1)
                dve.wait_ge(r_var, 1)
                dve.wait_ge(r_std, 1)
                link(nc.vector.reciprocal(rstd[:], std[:]))
                for t in range(T):
                    nc.vector.tensor_scalar(xf[:, t, :], x_rows[:, t, :], mv[:, t, 0:1], rstd[:, t:t + 1],
                                            ALU.subtract, ALU.mult).then_inc(xf_ok, 1)
                dve.wait_ge(r_const, 1)
                link(nc.vector.tensor_scalar(row_is_shared[:], first_f[:], float(SHARED * S), None, ALU.is_lt))
                link(nc.vector.tensor_scalar(first_f[:], first_f[:], float(N - 1), None, ALU.min))
                link(nc.vector.tensor_tensor(first_f[:], first_f[:], row_is_shared[:], ALU.mult))
                link(nc.vector.memset(zero_i[:], 0))
                nc.vector.tensor_copy(first_i[:], first_f[:]).then_inc(first_ok, 1)
                for c in EARLY:
                    dve.wait_ge(hi_here, c + 1)
                    second_part(c).then_inc(lo_here, 1)
                dve.wait_ge(g_in, 32)
                dve.wait_ge(score_ok, 1)
                link(nc.vector.tensor_tensor(pr[:], bank[4][0:P, 0:T * X].rearrange("p (t e) -> p t e", t=T),
                                             gbias[:].unsqueeze(1).to_broadcast([P, T, X]), ALU.add))
                link(nc.vector.memset(pr[:, :, 0:1], -1e9))
                link(nc.vector.tensor_reduce(m[:], pr[:], AX.X, ALU.max))
                nc.vector.tensor_tensor(pr[:], pr[:], m[:].unsqueeze(2).to_broadcast([P, T, X]),
                                        ALU.subtract).then_inc(exp_in, 1)
                dve.wait_ge(exp_out, 1)
                link(nc.vector.tensor_reduce(m[:], pr[:], AX.X, ALU.add))
                link(nc.vector.reciprocal(m[:], m[:]))
                link(nc.vector.tensor_tensor(pr[:], pr[:], m[:].unsqueeze(2).to_broadcast([P, T, X]), ALU.mult))
                for c in range(TOP):
                    link(nc.vector.tensor_reduce(topv[:, c, :], pr[:], AX.X, ALU.max))
                    link(nc.vector.tensor_tensor(eq[:], pr[:], topv[:, c, :].unsqueeze(2).to_broadcast([P, T, X]),
                                                 ALU.is_lt))
                    link(nc.vector.tensor_scalar(eq[:], eq[:], float(X), None, ALU.mult))
                    link(nc.vector.tensor_tensor(eq[:], eq[:], iota_x[:].unsqueeze(1).to_broadcast([P, T, X]), ALU.add))
                    link(nc.vector.tensor_reduce(m[:], eq[:], AX.X, ALU.min))
                    link(nc.vector.tensor_tensor(chosen[:, c], iota_x[:].unsqueeze(1).to_broadcast([P, T, X]),
                                                 m[:].unsqueeze(2).to_broadcast([P, T, X]), ALU.is_equal))
                    link(nc.vector.scalar_tensor_tensor(out=pr[:], in0=chosen[:, c], scalar=-4.0, in1=pr[:],
                                                        op0=ALU.mult, op1=ALU.add))
                link(nc.vector.tensor_tensor(sel[:], chosen[:, 0], chosen[:, 1], ALU.add))
                nc.vector.tensor_tensor(sel[:], sel[:], chosen[:, 2], ALU.add).then_inc(sel_ok, 1)
                dve.wait_ge(pos_ok, 1)
                link(nc.vector.tensor_copy(total[:], bank[6][0:P, 0:X]))
                link(nc.vector.tensor_scalar(tiles[:], total[:], 0.0, None, ALU.is_gt))
                for c in range(1, SHARED):
                    link(nc.vector.tensor_scalar(more[:], total[:], float(c * S), None, ALU.is_gt))
                    link(nc.vector.tensor_tensor(tiles[:], tiles[:], more[:], ALU.add))
                link(nc.vector.tensor_tensor_scan(ends[:], one_x[:], tiles[:], float(SHARED), ALU.mult, ALU.add))
                link(nc.vector.tensor_tensor(more[:], ends[:], tiles[:], ALU.subtract))
                link(nc.vector.tensor_scalar(more[:], more[:], float(S), None, ALU.mult))
                link(nc.vector.tensor_tensor(pos[:], bank[5][0:P, 0:T * X].rearrange("p (t e) -> p t e", t=T),
                                             more[:].unsqueeze(1).to_broadcast([P, T, X]), ALU.add))
                for c in range(TOP):
                    link(nc.vector.tensor_tensor(eq[:], chosen[:, c], pos[:], ALU.mult))
                    link(nc.vector.tensor_reduce(slot_f[:, c, :], eq[:], AX.X, ALU.add))
                nc.vector.tensor_copy(slot_i[:], slot_f[:].rearrange("p c t -> p (c t)")).then_inc(slots_ok, 1)
                link(nc.vector.tensor_tensor(at_or_past[:], ends[0:1, :].unsqueeze(1).to_broadcast([1, NTAB, X]),
                                             iota_j[:].unsqueeze(2).to_broadcast([1, NTAB, X]), ALU.is_le))
                link(nc.vector.tensor_reduce(expert_f[:], at_or_past[:], AX.X, ALU.add))
                link(nc.vector.tensor_scalar(expert_f[:], expert_f[:], float(X - 1), None, ALU.min))
                link(nc.vector.tensor_copy(tile_expert[:], expert_f[:]))
                link(nc.vector.tensor_scalar(last_tile[:], ends[0:1, X - 1:X], -1.0, None, ALU.add))
                link(nc.vector.tensor_scalar(some[:], tiles[:], 1.0, None, ALU.min))
                link(nc.vector.tensor_tensor_scan(ordinal[:], one_x[:], some[:], 0.0, ALU.mult, ALU.add))
                link(nc.vector.tensor_copy(last_group[:], ordinal[0:1, X - 1:X]))
                link(nc.vector.tensor_tensor(more[:], ends[:], tiles[:], ALU.subtract))
                link(nc.vector.tensor_tensor(at_or_past[:], more[0:1, :].unsqueeze(1).to_broadcast([1, NTAB, X]),
                                             iota_j[:].unsqueeze(2).to_broadcast([1, NTAB, X]), ALU.is_le))
                link(nc.vector.tensor_tensor(at_or_past[:], at_or_past[:],
                                             some[0:1, :].unsqueeze(1).to_broadcast([1, NTAB, X]), ALU.mult))
                link(nc.vector.tensor_reduce(expert_f[:], at_or_past[:], AX.X, ALU.add))
                link(nc.vector.tensor_copy(tile_group[:], expert_f[:]))
                link(nc.vector.tensor_tensor(in_group[:], ordinal[0:1, :].unsqueeze(1).to_broadcast([1, X + 1, X]),
                                             iota_j[:, 0:X + 1].unsqueeze(2).to_broadcast([1, X + 1, X]), ALU.is_equal))
                link(nc.vector.tensor_tensor(in_group[:], in_group[:],
                                             some[0:1, :].unsqueeze(1).to_broadcast([1, X + 1, X]), ALU.mult))
                for table, value in ((group_expert, iota_x), (group_before, more)):
                    link(nc.vector.tensor_tensor(weighted[:], in_group[:],
                                                 value[0:1, :].unsqueeze(1).to_broadcast([1, X + 1, X]), ALU.mult))
                    link(nc.vector.tensor_reduce(group_f[:], weighted[:], AX.X, ALU.add))
                    if table is group_before:
                        link(nc.vector.tensor_scalar(group_f[:], group_f[:], -1.0, 0.0, ALU.add, ALU.max))
                    link(nc.vector.tensor_copy(table[:], group_f[:]))
                for c in LATE:
                    dve.wait_ge(hi_here, c + 1)
                    second_part(c).then_inc(lo_here, 1)
                dve.wait_ge(parts_in, 16 * TOP)
                link(nc.vector.tensor_tensor(parts[:, 0, :], parts[:, 0, :], parts[:, 1, :], ALU.add))
                nc.vector.tensor_tensor(first_i[:], parts[:, 0, :], parts[:, 2, :], ALU.add).then_inc(merged, 1)

    with stage(nc) as (ff, sem):
        def fb(name, shape, dt=F32):
            return sb(name, shape, dt, ff)

        xg = fb("xg", [S, D])
        slot_idx = fb("slot_idx", [S, 1], I32)
        xgT_hi = fb("xgT_hi", [128, KD, S], F32R)
        xgT_lo = fb("xgT_lo", [128, KD, S], F32R)
        h = fb("h", [S, FF])
        hT = fb("hT", [128, KF, S])
        y = fb("y", [S, D])
        row = fb("row", [1, 2, FF])
        all_rows = fb("all_rows", [S, 3 * FF + D])
        mv, stats = fb("e_mv", [S, 2]), fb("e_stats", [S, 3, 6])
        std, rstd = fb("e_std", [S, 1]), fb("e_rstd", [S, 1])
        w1_in = [sem(f"w1_in{c}") for c in range(KD)]
        w2_in = [sem(f"w2_in{c}") for c in range(KD)]
        row_in = [sem(f"row_in{u}") for u in range(2)]
        idx_in, xg_in, y_out, go = (sem(s) for s in ("idx_in", "xg_in", "y_out", "e_go"))
        w1_used, w2_used, x_turned, xgT_ok, h_turned, hT_ok = (
            sem(s) for s in ("w1_used", "w2_used", "x_turned", "xgT_ok", "h_turned", "hT_ok"))
        w1_hi_ok, w1_ok, xgT_lo_ok = sem("w1_hi_ok"), sem("w1_ok"), sem("xgT_lo_ok")
        go_sp, go_dve, go_act = sem("go_sp"), sem("go_dve"), sem("go_act")
        spread, biased, gelu_ok, stat_ok, aggr_ok, std_ok, rstd_ok, centred, hn_ok, y_sb = (
            sem(s) for s in ("spread", "biased", "gelu_ok", "stat_ok", "aggr_ok", "e_std_ok", "rstd_ok",
                             "centred", "hn_ok", "y_sb"))
        with nc.Block() as block:
            def final_tile(eng):
                return eng.value_load(last_tile[0:1, 0:1], min_val=MINT - 1, max_val=MAXT - 1)

            def group_of(eng, j):
                return eng.value_load(tile_group[0:1, bass.ds(j, 1)], min_val=0, max_val=X)

            @block.sync
            def _(sp):
                def load_w1(e, g):
                    for c in range(KD):
                        sp.wait_ge(w1_ok, g * KD + c + 1 - RAW)
                        sp.sem_inc(go_sp, 1)
                        sp.dma_start(w1_in_rows[:, c % RAW, :], fc1_w[bass.ds(e, 1), c * 128:(c + 1) * 128, :]
                                     .rearrange("o p n -> (o p) n")).then_inc(w1_in[c], 16)

                def load_w2(e, before):
                    for c in range(KD):
                        sp.wait_ge(w2_used, before * KD + c + 1)
                        sp.sem_inc(go_sp, 1)
                        sp.dma_start(w2[:, 2 * c:2 * c + 2, :], fc2_w[bass.ds(e, 1), c * 256:(c + 1) * 256, :]
                                     .rearrange("o (k p) n -> (o p) k n", p=128)).then_inc(w2_in[c], 16)

                def row_of(table, g, top):
                    return sp.value_load(table[0:1, bass.ds(g, 1)], min_val=0, max_val=top)

                groups = sp.value_load(last_group[0:1, 0:1], min_val=TOP, max_val=X)
                for c in range(KD):
                    sp.sem_inc(w1_in[c], 16)
                    sp.sem_inc(w2_in[c], 16)
                sp.wait_ge(xg_in, 16)
                load_w1(row_of(group_expert, 1, X - 1), 1)
                with sp.Fori(1, groups) as g:
                    e, before = row_of(group_expert, g, X - 1), row_of(group_before, g, MAXT - 1)
                    e_next, before_next = row_of(group_expert, g + 1, X - 1), row_of(group_before, g + 1, MAXT - 1)
                    with sp.If(before_next - before == 1):
                        load_w1(e_next, g + 1)
                        load_w2(e, before)
                    with sp.Else():
                        load_w2(e, before)
                        load_w1(e_next, g + 1)
                load_w2(row_of(group_expert, groups, X - 1), row_of(group_before, groups, MAXT - 1))

            @block.gpsimd
            def _(pool):
                def load_row(j, n, of, again):
                    e = pool.value_load(tile_expert[0:1, bass.ds(of, 1)], min_val=0, max_val=X - 1)
                    if again:
                        pool.wait_ge(spread, 4 * j + n - 1)
                        pool.sem_inc(go, 1)
                    v = (fc1_b, ln_w, ln_b, fc2_b)[n]
                    nc.gpsimd.dma_start(row[:, n % 2, 0:v.shape[1]], v[bass.ds(e, 1), :]).then_inc(row_in[n % 2], 16)

                def spread_row(j, n, again):
                    if again:
                        used, times = ((biased, 3 * j), (centred, j), (hn_ok, j), (y_sb, 2 * (j - 1)))[n]
                        pool.wait_ge(used, times)
                    pool.wait_ge(row_in[n % 2], 16 * (2 * j + n // 2 + 1))
                    nc.gpsimd.sem_inc(go, 1)
                    width = (FF, FF, FF, D)[n]
                    nc.gpsimd.partition_broadcast(all_rows[:, n * FF:n * FF + width], row[:, n % 2, 0:width]).then_inc(spread, 1)

                def gather(j, again):
                    if again:
                        pool.wait_ge(x_turned, j)
                    nc.gpsimd.sem_inc(go, 1)
                    nc.gpsimd.dma_start(slot_idx[:], slot_token[bass.ds(j * S, S), :]).then_inc(idx_in, 16)
                    pool.wait_ge(idx_in, 16 * (j + 1))
                    nc.gpsimd.sem_inc(go, 1)
                    nc.gpsimd.indirect_dma_start(xg[:], None, token_rows,
                                                 bass.IndirectOffsetOnAxis(ap=slot_idx[:, 0:1], axis=0)).then_inc(xg_in, 16)

                def tile(j, before, again):
                    spread_row(j, 0, again)
                    load_row(j, 2, j, True)
                    spread_row(j, 1, again)
                    load_row(j, 3, before, True)
                    spread_row(j, 2, again)
                    load_row(j + 1, 0, j + 1, True)
                    gather(j + 1, True)
                    spread_row(j, 3, again)
                    load_row(j + 1, 1, j + 1, True)

                end = final_tile(pool)
                gather(0, False)
                load_row(0, 0, 0, False)
                load_row(0, 1, 0, False)
                tile(0, 0, False)
                with pool.Fori(1, end + 1) as j:
                    tile(j, j - 1, True)
                pool.wait_ge(spread, 4 * (end + 1))
                pool.wait_ge(row_in[1], 16 * (2 * (end + 1) + 1))
                pool.sem_inc(go, 1)
                load_row(end + 1, 3, end, False)
                pool.wait_ge(y_sb, 2 * end)
                pool.wait_ge(row_in[0], 16 * (2 * (end + 1) + 1))
                pool.wait_ge(row_in[1], 16 * (2 * (end + 1) + 2))
                pool.sem_inc(go, 1)
                nc.gpsimd.partition_broadcast(all_rows[:, 3 * FF:3 * FF + D], row[:, 1, 0:D]).then_inc(spread, 1)
                pool.wait_ge(xg_in, 16 * (end + 2))
                pool.sem_inc(go, 1)

            @block.tensor
            def _(pe):
                def turn_tokens(j, again):
                    pe.wait_ge(xg_in, 16 * (j + 1))
                    for c in range(KD):
                        last = nc.tensor.transpose(bank[5 + c // 4][:, (c % 4) * S:(c % 4 + 1) * S],
                                                   xg[:, c * 128:(c + 1) * 128], ident[:])
                    last.then_inc(x_turned, 1)

                def first_product(j, g, slices, again):
                    for c in slices:
                        pe.wait_ge(w1_ok, g * KD + c + 1)
                        if c == 0:
                            pe.wait_ge(xgT_ok, 2 * (j + 1))
                            pe.wait_ge(xgT_lo_ok, 2 * (j + 1))
                            if again:
                                pe.wait_ge(biased, 3 * j)
                        for n, (part_x, part_w) in enumerate(((xgT_hi, w1_hi), (xgT_hi, w1_lo), (xgT_lo, w1_hi))):
                            for b in range(3):
                                last = nc.tensor.matmul(bank[b][:], part_x[:, c, :], part_w[:, c, b * 512:(b + 1) * 512],
                                                        start=(c == 0 and n == 0), stop=(c == KD - 1 and n == 2))
                        last.then_inc(w1_used, 1)

                def turn_hidden(j):
                    pe.wait_ge(hn_ok, j + 1)
                    pe.wait_ge(xgT_ok, 2 * (j + 2))
                    pe.wait_ge(xgT_lo_ok, 2 * (j + 2))
                    for b in range(3):
                        for u in range(4):
                            c = 4 * b + u
                            last = nc.tensor.transpose(bank[5 + b][:, u * S:(u + 1) * S],
                                                       h[:, c * 128:(c + 1) * 128], ident[:])
                        last.then_inc(h_turned, 1)

                def second_product(j, g, slices, again):
                    for c in slices:
                        if c % 2 == 0:
                            pe.wait_ge(w2_in[c // 2], 16 * (g + 1))
                        if c % 4 == 0:
                            pe.wait_ge(hT_ok, 3 * j + c // 4 + 1)
                        if c == 0 and again:
                            pe.wait_ge(y_sb, 2 * j)
                        for b in range(2):
                            last = nc.tensor.matmul(bank[3 + b][:, 0:HALF], hT[:, c, :],
                                                    w2[:, c, b * HALF:(b + 1) * HALF],
                                                    start=(c == 0), stop=(c == KF - 1))
                        if c % 2:
                            last.then_inc(w2_used, 1)

                end = final_tile(pe)
                turn_tokens(0, False)
                first_product(0, 0, range(KD), False)
                turn_tokens(1, True)

                def step(j, again):
                    g, g_before = group_of(pe, j), group_of(pe, j - 1)
                    first_product(j, g, range(0, 4), True)
                    turn_hidden(j - 1)
                    first_product(j, g, range(4, KD), True)
                    second_product(j - 1, g_before, range(0, 8), again)
                    pe.wait_ge(hT_ok, 3 * j)
                    turn_tokens(j + 1, True)
                    second_product(j - 1, g_before, range(8, KF), again)

                step(1, False)
                with pe.Fori(2, end + 1) as j:
                    step(j, True)
                turn_hidden(end)
                second_product(end, group_of(pe, end), range(KF), True)

            @block.scalar
            def _(act):
                def copy_tokens(j):
                    act.wait_ge(x_turned, j + 1)
                    act.wait_ge(w1_used, j * KD)
                    nc.scalar.copy(xgT_hi[:, 0:4, :].rearrange("p k s -> p (k s)"), bank[5][:]).then_inc(xgT_ok, 1)
                    nc.scalar.copy(xgT_hi[:, 4:6, :].rearrange("p k s -> p (k s)"), bank[6][:, 0:2 * S]).then_inc(xgT_ok, 1)

                def first_parts(g, slices, tiles):
                    for c in slices:
                        act.wait_ge(w1_in[c], 16 * (g + 1))
                        act.wait_ge(w1_used, (tiles - 1) * KD + c + 1)
                        first_part(c).then_inc(w1_hi_ok, 1)

                def hidden(j):
                    for b in range(3):
                        act.wait_ge(biased, 3 * j + b + 1)
                        nc.scalar.activation(h[:, b * 512:(b + 1) * 512], h[:, b * 512:(b + 1) * 512],
                                             ACT.Gelu).then_inc(gelu_ok, 1)
                    act.wait_ge(aggr_ok, j + 1)
                    nc.scalar.activation(std[:], mv[:, 1:2], ACT.Sqrt, bias=eps[:]).then_inc(std_ok, 1)

                def copy_hidden(j, again):
                    for b in range(3):
                        act.wait_ge(h_turned, 3 * j + b + 1)
                        if again:
                            act.wait_ge(w2_used, j * KD)
                        nc.scalar.copy(hT[:, 4 * b:4 * b + 4, :].rearrange("p k s -> p (k s)"),
                                       bank[5 + b][:]).then_inc(hT_ok, 1)

                def store(j):
                    act.wait_ge(y_sb, 2 * (j + 1))
                    act.dma_start(slot_out[bass.ds(j * S, S), :], y[:]).then_inc(y_out, 16)

                end = final_tile(act)
                act.sem_inc(w1_hi_ok, KD)
                copy_tokens(0)
                copy_tokens(1)
                hidden(0)

                def step(j, again):
                    copy_hidden(j - 1, again)
                    g, g_next = group_of(act, j), group_of(act, j + 1)
                    with act.If(g_next - g == 1):
                        first_parts(g_next, EARLY, j + 1)
                    hidden(j)
                    with act.If(g_next - g == 1):
                        first_parts(g_next, LATE, j + 1)
                    copy_tokens(j + 1)
                    store(j - 1)

                step(1, False)
                with act.Fori(2, end + 1) as j:
                    step(j, True)
                copy_hidden(end, True)
                store(end)
                act.wait_ge(y_out, 16 * (end + 1))
                act.sem_inc(go_act, 1)

            @block.vector
            def _(dve):
                def second_parts(g, slices, tiles):
                    for c in slices:
                        dve.wait_ge(w1_hi_ok, g * KD + c + 1)
                        dve.wait_ge(w1_used, (tiles - 1) * KD + c + 1)
                        second_part(c).then_inc(w1_ok, 1)

                def token_parts(j, again):
                    if again:
                        dve.wait_ge(w1_used, j * KD)
                    for n, (lo, hi) in enumerate(((0, 4), (4, KD))):
                        dve.wait_ge(xgT_ok, 2 * j + n + 1)
                        nc.vector.tensor_tensor(xgT_lo[:, lo:hi, :].rearrange("p k s -> p (k s)"),
                                                bank[5 + n][:, 0:(hi - lo) * S],
                                                xgT_hi[:, lo:hi, :].bitcast(F32).rearrange("p k s -> p (k s)"),
                                                ALU.subtract).then_inc(xgT_lo_ok, 1)

                def hidden(j, again):
                    dve.wait_ge(spread, 4 * j + 1)
                    dve.wait_ge(w1_used, KD * (j + 1))
                    if again:
                        dve.wait_ge(h_turned, 3 * j)
                    for b in range(3):
                        nc.vector.tensor_tensor(h[:, b * 512:(b + 1) * 512], bank[b][:],
                                                all_rows[:, b * 512:(b + 1) * 512], ALU.add).then_inc(biased, 1)
                    for b in range(3):
                        dve.wait_ge(gelu_ok, 3 * j + b + 1)
                        nc.vector.bn_stats(stats[:, b, :], h[:, b * 512:(b + 1) * 512]).then_inc(stat_ok, 1)
                    if again:
                        dve.wait_ge(std_ok, j)
                    dve.wait_ge(stat_ok, 3 * (j + 1))
                    nc.vector.sem_inc(go_dve, 1)
                    nc.vector.bn_aggr(mv[:], stats[:].rearrange("p c s -> p (c s)")).then_inc(aggr_ok, 1)
                    dve.wait_ge(aggr_ok, j + 1)
                    dve.wait_ge(spread, 4 * j + 2)
                    nc.vector.scalar_tensor_tensor(out=h[:], in0=h[:], scalar=mv[:, 0:1], in1=all_rows[:, FF:2 * FF],
                                                   op0=ALU.subtract, op1=ALU.mult).then_inc(centred, 1)
                    dve.wait_ge(std_ok, j + 1)
                    nc.vector.reciprocal(rstd[:], std[:]).then_inc(rstd_ok, 1)
                    dve.wait_ge(rstd_ok, j + 1)
                    dve.wait_ge(centred, j + 1)
                    dve.wait_ge(spread, 4 * j + 3)
                    nc.vector.scalar_tensor_tensor(out=h[:], in0=h[:], scalar=rstd[:, 0:1], in1=all_rows[:, 2 * FF:3 * FF],
                                                   op0=ALU.mult, op1=ALU.add).then_inc(hn_ok, 1)

                def output(j, again, last=False):
                    dve.wait_ge(spread, 4 * (j + 1) + (1 if last else 4))
                    dve.wait_ge(w2_used, KD * (j + 1))
                    if again:
                        dve.wait_ge(y_out, 16 * j)
                    for b in range(2):
                        nc.vector.tensor_tensor(y[:, b * HALF:(b + 1) * HALF], bank[3 + b][:, 0:HALF],
                                                all_rows[:, 3 * FF + b * HALF:3 * FF + (b + 1) * HALF], ALU.add).then_inc(y_sb, 1)

                def step(j, again):
                    g, g_next = group_of(dve, j), group_of(dve, j + 1)
                    with dve.If(g_next - g == 1):
                        second_parts(g_next, EARLY, j + 1)
                    hidden(j, True)
                    with dve.If(g_next - g == 1):
                        second_parts(g_next, LATE, j + 1)
                    token_parts(j + 1, True)
                    output(j - 1, again)

                end = final_tile(dve)
                dve.sem_inc(w1_ok, KD)
                token_parts(0, False)
                token_parts(1, True)
                hidden(0, False)
                step(1, False)
                with dve.Fori(2, end + 1) as j:
                    step(j, True)
                output(end, True, last=True)

    weights.close()

    with stage(nc) as (last_stage, sem):
        gathered = sb("gathered", [P, TOP * T, D], F32, last_stage)
        shared = sb("shared", [P, T, D], F32, last_stage)
        slots_in = [sem(f"slots_in{t}") for t in range(T)]
        shared_in, f_chain, row_done, written = sem("shared_in"), sem("f_chain"), sem("row_done"), sem("written")
        with nc.Block() as block:
            @block.sync
            def _(sp):
                sp.dma_start(shared[:], slot_out[0:N, :].rearrange("(t p) d -> p t d", p=P)).then_inc(shared_in, 16)
                for t in range(T):
                    sp.wait_ge(row_done, t + 1)
                    sp.dma_start(out[t * P:(t + 1) * P, :], x_rows[:, t, :]).then_inc(written, 16)
                sp.wait_ge(written, 16 * T)

            @block.gpsimd
            def _(pool):
                for t in range(T):
                    for c in range(TOP):
                        n = c * T + t
                        nc.gpsimd.indirect_dma_start(gathered[:, n, :], None, slot_out,
                                                     bass.IndirectOffsetOnAxis(ap=slot_i[:, n:n + 1], axis=0)
                                                     ).then_inc(slots_in[t], 16)

            @block.vector
            def _(dve):
                link = Chain(dve, f_chain)
                dve.wait_ge(shared_in, 16)
                for t in range(T):
                    link(nc.vector.tensor_tensor(x_rows[:, t, :], x_rows[:, t, :], shared[:, t, :], ALU.add))
                    dve.wait_ge(slots_in[t], 16 * TOP)
                    for c in range(TOP):
                        last = nc.vector.scalar_tensor_tensor(out=x_rows[:, t, :], in0=gathered[:, c * T + t, :],
                                                              scalar=topv[:, c, t:t + 1], in1=x_rows[:, t, :],
                                                              op0=ALU.mult, op1=ALU.add)
                        if c < TOP - 1:
                            link(last)
                    last.then_inc(row_done, 1)


def kernel(**inputs):
    import numpy as _np
    import concourse.bacc as _bacc
    from concourse import mybir as _mybir
    from concourse.bass_utils import run_bass_kernel_spmd as _run

    nc = _bacc.Bacc("TRN2", target_bir_lowering=False, num_devices=1)
    arrays, args = {}, {}
    for name in inputs:
        v = _np.ascontiguousarray(inputs[name])
        arrays[f"in_{name}"] = v
        args[name] = nc.dram_tensor(f"in_{name}", v.shape, _mybir.dt.from_np(v.dtype), kind="ExternalInput").ap()
    out = nc.dram_tensor("out_0", (N, D), F32, kind="ExternalOutput").ap()
    gnn_moe(nc, args, out)
    r = _run(nc, [arrays], core_ids=[0])
    return r.results[0]["out_0"]
```
